# Optimizing a Trainium2 kernel written in Bass

```python
import numpy as np
import jax
import jax.numpy as jnp

def _softmax(x, axis=-1):
    return jax.nn.softmax(x, axis=axis)

def _gelu(x):
    return jax.nn.gelu(x, approximate=True)

def _silu(x):
    return jax.nn.silu(x)

def _sigmoid(x):
    return jax.nn.sigmoid(x)

def _layernorm(x, axis=-1, eps=1e-05):
    m = jnp.mean(x, axis=axis, keepdims=True)
    v = jnp.var(x, axis=axis, keepdims=True)
    return (x - m) / jnp.sqrt(v + eps)

def _scatter_add(tgt, idx, src, axis=0):
    return tgt.at[idx].add(src)

def _segment_sum(src, seg, n):
    return jax.ops.segment_sum(src, seg, n)
kernel_name = 'mk_prb_d2_jaxref_r8_11c064'

def setup_inputs(seed: int=0):
    np.random.seed(seed)
    _w = jnp.asarray

    def _L0_attn_setup():
        import jax, jax.numpy as jnp
        import numpy as np
        H = 16
        D = 128
        M = 16
        ROPE = 64
        THETA = 10000.0
        WIN = 64
        CAP = 50.0
        G = 4
        HID = 256
        QC = 64
        INTER = 256

        def rope_cache(t):
            inv = 1.0 / THETA ** (jnp.arange(0, ROPE, 2, dtype=jnp.float32) / ROPE)
            ang = jnp.arange(t, dtype=jnp.float32)[:, None] * inv[None, :]
            return (jnp.cos(ang), jnp.sin(ang))

        def apply_partial_rope(x, cos, sin):
            x1 = x[..., :ROPE // 2]
            x2 = x[..., ROPE // 2:ROPE]
            rest = x[..., ROPE:]
            return jnp.concatenate([x1 * cos - x2 * sin, x1 * sin + x2 * cos, rest], axis=-1)

        def rmsnorm(x, w, eps=1e-06):
            return x * jax.lax.rsqrt(jnp.mean(x * x, axis=-1, keepdims=True) + eps) * w

        def attend(scores, mask, sink, v, sub):
            b, h, t, _ = scores.shape
            logits = jnp.where(mask, scores, jnp.float32(-1e+30))
            sink_col = jnp.broadcast_to(sink[None, :, None, None], (b, h, t, 1))
            probs = jax.nn.softmax(jnp.concatenate([logits, sink_col], axis=-1), axis=-1)[..., :-1]
            return jnp.einsum(sub, probs, v)
        key = jax.random.key(seed)
        ks = jax.random.split(key, 12)
        s = 0.02
        return {'h': jax.random.normal(ks[0], (2, 256, HID), dtype=jnp.float32), 'Wq_c': jax.random.normal(ks[1], (HID, QC), dtype=jnp.float32) * s, 'Wq_up': jax.random.normal(ks[2], (QC, H * D), dtype=jnp.float32) * s, 'Wk': jax.random.normal(ks[3], (HID, D), dtype=jnp.float32) * s, 'Wv': jax.random.normal(ks[4], (HID, D), dtype=jnp.float32) * s, 'W_comp': jax.random.normal(ks[5], (M * HID, D), dtype=jnp.float32) * s, 'q_norm_w': jnp.ones((D,), dtype=jnp.float32), 'k_norm_w': jnp.ones((D,), dtype=jnp.float32), 'sink': jnp.zeros((H,), dtype=jnp.float32), 'Wg': jax.random.normal(ks[6], (G, H // G * D, INTER), dtype=jnp.float32) * s, 'Wo': jax.random.normal(ks[7], (G * INTER, HID), dtype=jnp.float32) * s}
    _L0_attn_in = _L0_attn_setup()

    def _L0_ffn_setup():
        import jax, jax.numpy as jnp
        import numpy as np
        D_MODEL = 256
        D_HIDDEN = 176
        NUM_SHARED = 2
        NUM_ROUTED = 32
        TOP_K = 6

        def _expert_apply(xf, w1, b1, w2, b2):
            return jnp.maximum(xf @ w1 + b1, 0.0) @ w2 + b2
        key = jax.random.key(seed)
        ks = jax.random.split(key, 11)
        d, h = (D_MODEL, D_HIDDEN)
        s1 = 1.0 / np.sqrt(d)
        s2 = 1.0 / np.sqrt(h)
        x = jax.random.normal(ks[0], (2, 256, d), dtype=jnp.float32)
        sw1 = jax.random.uniform(ks[1], (NUM_SHARED, d, h), jnp.float32, -s1, s1)
        sb1 = jax.random.uniform(ks[2], (NUM_SHARED, h), jnp.float32, -s1, s1)
        sw2 = jax.random.uniform(ks[3], (NUM_SHARED, h, d), jnp.float32, -s2, s2)
        sb2 = jax.random.uniform(ks[4], (NUM_SHARED, d), jnp.float32, -s2, s2)
        rw1 = jax.random.uniform(ks[5], (NUM_ROUTED, d, h), jnp.float32, -s1, s1)
        rb1 = jax.random.uniform(ks[6], (NUM_ROUTED, h), jnp.float32, -s1, s1)
        rw2 = jax.random.uniform(ks[7], (NUM_ROUTED, h, d), jnp.float32, -s2, s2)
        rb2 = jax.random.uniform(ks[8], (NUM_ROUTED, d), jnp.float32, -s2, s2)
        router_w = jax.random.uniform(ks[9], (d, NUM_ROUTED), jnp.float32, -s1, s1)
        router_b = jax.random.uniform(ks[10], (NUM_ROUTED,), jnp.float32, -s1, s1)
        return {'x': x, 'sw1': sw1, 'sb1': sb1, 'sw2': sw2, 'sb2': sb2, 'rw1': rw1, 'rb1': rb1, 'rw2': rw2, 'rb2': rb2, 'router_w': router_w, 'router_b': router_b}
    _L0_ffn_in = _L0_ffn_setup()

    def _L1_attn_setup():
        import math
        import jax, jax.numpy as jnp
        import numpy as np
        HID = 256
        H = 16
        HKV = 8
        D = HID // H
        F = D
        SEQ = 256
        BATCH = 2
        THETA = 10000.0

        def _rotate_half(x):
            x1, x2 = (x[..., :x.shape[-1] // 2], x[..., x.shape[-1] // 2:])
            return jnp.concatenate((-x2, x1), axis=-1)

        def _softmax_kernel(x, R):
            n = jnp.sqrt(jnp.sum(x * x, axis=-1, keepdims=True))
            x = x / jnp.maximum(n, 1e-06)
            p = jnp.einsum('...d,ed->...e', x, R)
            feats = jnp.concatenate([jnp.sin(p), jnp.cos(p)], axis=-1)
            return feats / math.sqrt(F)
        key = jax.random.key(seed)
        ks = jax.random.split(key, 10)
        s = lambda k, shape, scale=0.02: jax.random.normal(k, shape, dtype=jnp.float32) * scale
        return {'hidden_states': jax.random.normal(ks[0], (BATCH, SEQ, HID), dtype=jnp.float32), 'Wq': s(ks[1], (HID, HID)), 'bq': s(ks[2], (HID,)), 'Wk': s(ks[3], (HKV * D, HID)), 'bk': s(ks[4], (HKV * D,)), 'Wv': s(ks[5], (HKV * D, HID)), 'bv': s(ks[6], (HKV * D,)), 'Wo': s(ks[7], (HID, HID)), 'bo': s(ks[8], (HID,)), 'rand_matrix': jax.random.normal(ks[9], (F // 2, D), dtype=jnp.float32)}
    _L1_attn_in = _L1_attn_setup()

    def _L1_ffn_setup():
        import jax, jax.numpy as jnp
        import numpy as np
        TOP_K = 2
        key = jax.random.key(seed)
        ks = jax.random.split(key, 5)
        B, S, D, M, E = (4, 256, 256, 256, 8)
        x = jax.random.normal(ks[0], (B, S, D), dtype=jnp.float32)
        gate_kernel = jax.random.normal(ks[1], (D, E), dtype=jnp.float32) / np.sqrt(D)
        wi_0 = jax.random.normal(ks[2], (E, D, M), dtype=jnp.float32) / np.sqrt(D)
        wi_1 = jax.random.normal(ks[3], (E, D, M), dtype=jnp.float32) / np.sqrt(D)
        wo = jax.random.normal(ks[4], (E, M, D), dtype=jnp.float32) / np.sqrt(M)
        return {'x': x, 'gate_kernel': gate_kernel, 'wi_0': wi_0, 'wi_1': wi_1, 'wo': wo}
    _L1_ffn_in = _L1_ffn_setup()
    _d = {'L0_attn_h': _L0_attn_in['h'], 'L0_attn_Wq_c': _L0_attn_in['Wq_c'], 'L0_attn_Wq_up': _L0_attn_in['Wq_up'], 'L0_attn_Wk': _L0_attn_in['Wk'], 'L0_attn_Wv': _L0_attn_in['Wv'], 'L0_attn_W_comp': _L0_attn_in['W_comp'], 'L0_attn_q_norm_w': _L0_attn_in['q_norm_w'], 'L0_attn_k_norm_w': _L0_attn_in['k_norm_w'], 'L0_attn_sink': _L0_attn_in['sink'], 'L0_attn_Wg': _L0_attn_in['Wg'], 'L0_attn_Wo': _L0_attn_in['Wo'], 'L0_ffn_sw1': _L0_ffn_in['sw1'], 'L0_ffn_sb1': _L0_ffn_in['sb1'], 'L0_ffn_sw2': _L0_ffn_in['sw2'], 'L0_ffn_sb2': _L0_ffn_in['sb2'], 'L0_ffn_rw1': _L0_ffn_in['rw1'], 'L0_ffn_rb1': _L0_ffn_in['rb1'], 'L0_ffn_rw2': _L0_ffn_in['rw2'], 'L0_ffn_rb2': _L0_ffn_in['rb2'], 'L0_ffn_router_w': _L0_ffn_in['router_w'], 'L0_ffn_router_b': _L0_ffn_in['router_b'], 'L1_attn_Wq': _L1_attn_in['Wq'], 'L1_attn_bq': _L1_attn_in['bq'], 'L1_attn_Wk': _L1_attn_in['Wk'], 'L1_attn_bk': _L1_attn_in['bk'], 'L1_attn_Wv': _L1_attn_in['Wv'], 'L1_attn_bv': _L1_attn_in['bv'], 'L1_attn_Wo': _L1_attn_in['Wo'], 'L1_attn_bo': _L1_attn_in['bo'], 'L1_attn_rand_matrix': _L1_attn_in['rand_matrix'], 'L1_ffn_gate_kernel': _L1_ffn_in['gate_kernel'], 'L1_ffn_wi_0': _L1_ffn_in['wi_0'], 'L1_ffn_wi_1': _L1_ffn_in['wi_1'], 'L1_ffn_wo': _L1_ffn_in['wo']}
    _x0 = _d['L0_attn_h']
    _d['L0_attn_h'] = jax.random.normal(jax.random.fold_in(jax.random.key(seed), 1), (4, 256, 256), dtype=_x0.dtype)
    del _x0
    return _d

def reference(L0_attn_h, L0_attn_Wq_c, L0_attn_Wq_up, L0_attn_Wk, L0_attn_Wv, L0_attn_W_comp, L0_attn_q_norm_w, L0_attn_k_norm_w, L0_attn_sink, L0_attn_Wg, L0_attn_Wo, L0_ffn_sw1, L0_ffn_sb1, L0_ffn_sw2, L0_ffn_sb2, L0_ffn_rw1, L0_ffn_rb1, L0_ffn_rw2, L0_ffn_rb2, L0_ffn_router_w, L0_ffn_router_b, L1_attn_Wq, L1_attn_bq, L1_attn_Wk, L1_attn_bk, L1_attn_Wv, L1_attn_bv, L1_attn_Wo, L1_attn_bo, L1_attn_rand_matrix, L1_ffn_gate_kernel, L1_ffn_wi_0, L1_ffn_wi_1, L1_ffn_wo):

    def _L0_attn_ref(h, Wq_c, Wq_up, Wk, Wv, W_comp, q_norm_w, k_norm_w, sink, Wg, Wo):
        import jax, jax.numpy as jnp
        import numpy as np
        H = 16
        D = 128
        M = 16
        ROPE = 64
        THETA = 10000.0
        WIN = 64
        CAP = 50.0
        G = 4
        HID = 256
        QC = 64
        INTER = 256

        def rope_cache(t):
            inv = 1.0 / THETA ** (jnp.arange(0, ROPE, 2, dtype=jnp.float32) / ROPE)
            ang = jnp.arange(t, dtype=jnp.float32)[:, None] * inv[None, :]
            return (jnp.cos(ang), jnp.sin(ang))

        def apply_partial_rope(x, cos, sin):
            x1 = x[..., :ROPE // 2]
            x2 = x[..., ROPE // 2:ROPE]
            rest = x[..., ROPE:]
            return jnp.concatenate([x1 * cos - x2 * sin, x1 * sin + x2 * cos, rest], axis=-1)

        def rmsnorm(x, w, eps=1e-06):
            return x * jax.lax.rsqrt(jnp.mean(x * x, axis=-1, keepdims=True) + eps) * w

        def attend(scores, mask, sink, v, sub):
            b, h, t, _ = scores.shape
            logits = jnp.where(mask, scores, jnp.float32(-1e+30))
            sink_col = jnp.broadcast_to(sink[None, :, None, None], (b, h, t, 1))
            probs = jax.nn.softmax(jnp.concatenate([logits, sink_col], axis=-1), axis=-1)[..., :-1]
            return jnp.einsum(sub, probs, v)
        b, t, _ = h.shape
        cos, sin = rope_cache(t)
        q = (h @ Wq_c @ Wq_up).reshape(b, t, H, D).transpose(0, 2, 1, 3)
        q = rmsnorm(apply_partial_rope(q, cos, sin), q_norm_w)
        k_sw = rmsnorm(apply_partial_rope(h @ Wk, cos, sin), k_norm_w)
        v_sw = h @ Wv
        nb = t // M
        ck = rmsnorm(h.reshape(b, nb, M * HID) @ W_comp, k_norm_w)
        scale = 1.0 / jnp.sqrt(jnp.float32(D))
        pos = jnp.arange(t)
        blk_end = jnp.arange(nb) * M + (M - 1)
        valid = blk_end[None, :] < pos[:, None]
        c_scores = jnp.einsum('bhtd,bnd->bhtn', q, ck) * scale
        c_out = attend(c_scores, valid[None, None], sink, ck, 'bhtn,bnd->bhtd')
        sw_scores = jnp.einsum('bhtd,bsd->bhts', q, k_sw) * scale
        sw_scores = CAP * jnp.tanh(sw_scores / CAP)
        sw_mask = (pos[None, :] <= pos[:, None]) & (pos[:, None] - pos[None, :] < WIN)
        sw_out = attend(sw_scores, sw_mask[None, None], sink, v_sw, 'bhts,bsd->bhtd')
        ao = (c_out + sw_out).transpose(0, 2, 1, 3).reshape(b, t, G, H // G * D)
        inter = jnp.einsum('btgf,gfi->btgi', ao, Wg)
        return inter.reshape(b, t, G * INTER) @ Wo

    def _L0_ffn_ref(x, sw1, sb1, sw2, sb2, rw1, rb1, rw2, rb2, router_w, router_b):
        import jax, jax.numpy as jnp
        import numpy as np
        D_MODEL = 256
        D_HIDDEN = 176
        NUM_SHARED = 2
        NUM_ROUTED = 32
        TOP_K = 6

        def _expert_apply(xf, w1, b1, w2, b2):
            return jnp.maximum(xf @ w1 + b1, 0.0) @ w2 + b2
        B, S, d = x.shape
        flat = x.reshape(-1, d)
        T = flat.shape[0]

        def sh_body(acc, p):
            w1, b1, w2, b2 = p
            return (acc + _expert_apply(flat, w1, b1, w2, b2), None)
        shared_out, _ = jax.lax.scan(sh_body, jnp.zeros_like(flat), (sw1, sb1, sw2, sb2))
        shared_out = shared_out / NUM_SHARED
        logits = flat @ router_w + router_b
        probs = jax.nn.softmax(logits, axis=-1)
        topk_p, topk_i = jax.lax.top_k(probs, TOP_K)
        topk_p = topk_p / jnp.sum(topk_p, axis=-1, keepdims=True)
        gates = jnp.zeros((T, NUM_ROUTED), dtype=flat.dtype)
        gates = gates.at[jnp.arange(T)[:, None], topk_i].add(topk_p)

        def r_body(acc, p):
            w1, b1, w2, b2, g = p
            return (acc + g[:, None] * _expert_apply(flat, w1, b1, w2, b2), None)
        routed_out, _ = jax.lax.scan(r_body, jnp.zeros_like(flat), (rw1, rb1, rw2, rb2, gates.T))
        return (shared_out + routed_out).reshape(B, S, d)

    def _L1_attn_ref(hidden_states, Wq, bq, Wk, bk, Wv, bv, Wo, bo, rand_matrix):
        import math
        import jax, jax.numpy as jnp
        import numpy as np
        HID = 256
        H = 16
        HKV = 8
        D = HID // H
        F = D
        SEQ = 256
        BATCH = 2
        THETA = 10000.0

        def _rotate_half(x):
            x1, x2 = (x[..., :x.shape[-1] // 2], x[..., x.shape[-1] // 2:])
            return jnp.concatenate((-x2, x1), axis=-1)

        def _softmax_kernel(x, R):
            n = jnp.sqrt(jnp.sum(x * x, axis=-1, keepdims=True))
            x = x / jnp.maximum(n, 1e-06)
            p = jnp.einsum('...d,ed->...e', x, R)
            feats = jnp.concatenate([jnp.sin(p), jnp.cos(p)], axis=-1)
            return feats / math.sqrt(F)
        b, s, _ = hidden_states.shape
        q = (hidden_states @ Wq.T + bq).reshape(b, s, H, D).transpose(0, 2, 1, 3)
        k = (hidden_states @ Wk.T + bk).reshape(b, s, HKV, D).transpose(0, 2, 1, 3)
        v = (hidden_states @ Wv.T + bv).reshape(b, s, HKV, D).transpose(0, 2, 1, 3)
        inv_freq = 1.0 / THETA ** (jnp.arange(0, D, 2, dtype=jnp.float32) / D)
        freqs = jnp.arange(s, dtype=jnp.float32)[:, None] * inv_freq[None, :]
        emb = jnp.concatenate((freqs, freqs), axis=-1)
        cos = jnp.cos(emb)[None, None, :, :]
        sin = jnp.sin(emb)[None, None, :, :]
        q = q * cos + _rotate_half(q) * sin
        k = k * cos + _rotate_half(k) * sin
        rep = H // HKV
        k = jnp.repeat(k, rep, axis=1)
        v = jnp.repeat(v, rep, axis=1)
        qp = _softmax_kernel(q, rand_matrix)
        kp = _softmax_kernel(k, rand_matrix)
        kv = jnp.einsum('bhsf,bhsd->bsfd', kp, v)
        out = jnp.einsum('bhsf,bsfd->bhsd', qp, kv)
        out = out.reshape(b, s, HID)
        return out @ Wo.T + bo

    def _L1_ffn_ref(x, gate_kernel, wi_0, wi_1, wo):
        import jax, jax.numpy as jnp
        import numpy as np
        TOP_K = 2
        E = gate_kernel.shape[-1]
        gate_logits = jnp.einsum('bsd,de->bse', x, gate_kernel)
        top_k_weights, top_k_indices = jax.lax.top_k(gate_logits, TOP_K)
        top_k_weights = jax.nn.softmax(top_k_weights.astype(jnp.float32), axis=-1).astype(x.dtype)
        combine_w = jnp.sum(jax.nn.one_hot(top_k_indices, E, dtype=x.dtype) * top_k_weights[..., None], axis=-2)
        h0 = jnp.einsum('bsd,edm->bsem', x, wi_0)
        h1 = jnp.einsum('bsd,edm->bsem', x, wi_1)
        h = jax.nn.silu(h0) * h1 * combine_w[..., None]
        out = jnp.einsum('bsem,emd->bsd', h, wo)
        return out
    x = L0_attn_h
    xn = _layernorm(x, axis=-1)
    x = x + _L0_attn_ref(xn, L0_attn_Wq_c, L0_attn_Wq_up, L0_attn_Wk, L0_attn_Wv, L0_attn_W_comp, L0_attn_q_norm_w, L0_attn_k_norm_w, L0_attn_sink, L0_attn_Wg, L0_attn_Wo) + _L0_ffn_ref(xn, L0_ffn_sw1, L0_ffn_sb1, L0_ffn_sw2, L0_ffn_sb2, L0_ffn_rw1, L0_ffn_rb1, L0_ffn_rw2, L0_ffn_rb2, L0_ffn_router_w, L0_ffn_router_b)
    xn = _layernorm(x, axis=-1)
    x = x + _L1_attn_ref(xn, L1_attn_Wq, L1_attn_bq, L1_attn_Wk, L1_attn_bk, L1_attn_Wv, L1_attn_bv, L1_attn_Wo, L1_attn_bo, L1_attn_rand_matrix) + _L1_ffn_ref(xn, L1_ffn_gate_kernel, L1_ffn_wi_0, L1_ffn_wi_1, L1_ffn_wo)
    return x

_drawn_inputs = setup_inputs


def setup_inputs(seed=0):
    import zlib

    import numpy as np

    out = dict(_drawn_inputs(seed))
    spreads = {'L0_attn_q_norm_w': (1.0, 0.2),
     'L0_attn_k_norm_w': (1.0, 0.2),
     'L0_attn_sink': (0.0, 0.634)}
    factors = {'L0_ffn_rb1': 3.075,
     'L1_attn_bq': 8.0,
     'L1_attn_bk': 8.0,
     'L1_attn_bv': 8.0,
     'L1_attn_bo': 3.317}
    for name, (base, spread) in spreads.items():
        noise = np.random.default_rng([zlib.crc32(name.encode()), seed]).standard_normal(out[name].shape)
        drawn = base * np.exp(spread * noise) if base else spread * noise
        out[name] = jnp.asarray(drawn.astype(out[name].dtype))
    for name, factor in factors.items():
        out[name] = (out[name] * factor).astype(out[name].dtype)
    return out
```

```python
from contextlib import ExitStack

import numpy as np

import concourse.bass as bass
from concourse import mybir

F32 = mybir.dt.float32
BF16 = mybir.dt.bfloat16
I32 = mybir.dt.int32
U32 = mybir.dt.uint32
ALU = mybir.AluOpType
ACT = mybir.ActivationFunctionType
AX = mybir.AxisListType.X

P = 128
B, S, HID = 4, 256, 256
T = B * S
NT = T // P
KC = HID // P
TPB = S // P
LN_EPS, RMS_EPS = 1e-5, 1e-6

H, D, QC, M, ROPE, WIN, CAP = 16, 128, 64, 16, 64, 64, 50.0
HR = ROPE // 2
NB = S // M
SCALE = 1.0 / float(np.sqrt(np.float32(D)))
NKEY = P + WIN + NB
KROW = P + NB + NKEY
NPAIR = H // 2
NG = H // 4

E0, K0, DH, NSH = 32, 6, 176, 2
DHB = DH - P
W1A, W1B, W2A, W2B, EW0 = 0, DH, 2 * DH, 2 * DH + HID, 2 * DH + 2 * HID
NT0 = 2 * ((T * K0 // P + E0 + 1) // 2)

H1, D1, HKV, E1, K1, MI = 16, 16, 8, 8, 2, 256
R1 = 8
EW1 = KC * 2 * MI + KC * HID
NT1 = 2 * ((T * K1 // P + E1 + 1) // 2)
MAGIC = 1.5 * 2.0 ** 23


def constants():
    f = np.float32
    t = np.arange(S, dtype=f)[:, None]
    c = {}
    a0 = t * (f(1) / f(10000.0) ** (np.arange(0, ROPE, 2, dtype=f) / f(ROPE)))[None]
    a1 = t * (f(1) / f(10000.0) ** (np.arange(0, D1, 2, dtype=f) / f(D1)))[None]
    tile = lambda a: a.reshape(TPB, P, -1).transpose(1, 0, 2).reshape(P, -1)
    c["rope0"] = np.concatenate([tile(np.cos(a0)), tile(np.sin(a0))], 1)
    c["rope1"] = np.concatenate([tile(np.cos(a1)), tile(np.sin(a1))], 1)
    p = np.arange(P)
    own = (p[None] <= p[:, None]) & (p[:, None] - p[None] < WIN)
    prev = np.arange(WIN)[None] > p[:, None]
    c["window"] = np.concatenate([own, prev], 1)
    end = np.arange(NB) * M + M - 1
    c["blocks"] = np.concatenate([np.where(end[None] < (p + j * P)[:, None], 0.0, -1e30) for j in range(TPB)], 1)
    c["ident"] = np.eye(P)
    c["before"] = p[:, None] < p[None]
    c["iota"] = np.tile(np.arange(NT0)[None], (P, 1))
    return {"table_" + k: np.ascontiguousarray(v, dtype=f) for k, v in c.items()}


class Steps:

    def __init__(self, eng, sem, base=0):
        self.eng, self.sem, self.base, self.n = eng, sem, base, 0

    def __call__(self, ins):
        ins.then_inc(self.sem, 1)
        self.n += 1

    def wait(self):
        self.eng.wait_ge(self.sem, self.base + self.n)

    def link(self, ins):
        self(ins)
        self.wait()


def bc(ap, shape):
    return ap.to_broadcast(shape)


def build(nc, a, out):
    ctx = ExitStack()
    sb = lambda name, cols, dt=F32, rows=P: ctx.enter_context(nc.sbuf_tensor(name, [rows, cols], dt))
    sem = lambda name: ctx.enter_context(nc.semaphore(name))
    v3 = lambda ap, n: ap.rearrange("p (a b) -> p a b", a=n)

    with ctx:
        xs0 = nc.dram_tensor("sorted_x0", [NT0 * P, HID], F32).ap()
        ys0 = nc.dram_tensor("sorted_y0", [NT0 * P, HID], F32).ap()
        xs1 = nc.dram_tensor("sorted_x1", [NT1 * P, HID], F32).ap()
        ys1 = nc.dram_tensor("sorted_y1", [NT1 * P, HID], F32).ap()
        heads1 = nc.dram_tensor("heads1", [T, HID], F32).ap()

        RW = sb("expert_weights", E0 * EW0)
        X = sb("residual", NT * HID)
        XN = sb("normed", 2 * NT * HID)
        WC = sb("out_weights", H * HID)
        WQ = sb("q_up_weights", H * D, rows=QC)
        SW1 = sb("shared_w1", NSH * KC * DH)
        SW2 = sb("shared_w2", NSH * 2 * HID)
        TA = sb("tiles", 3072)
        VA = sb("values", NT * D)
        V2A = sb("values_before", B * D, rows=WIN + NB)
        CK0 = sb("blocks_at_zero", B * D, rows=NB)
        QCT = sb("qc_T", (NT + 1) * P, rows=QC)
        KCAT = sb("keys", B * KROW)
        VOWN = sb("values_tile", TPB * D)
        V2 = sb("values_before_tile", D, rows=WIN + NB)
        CKS = sb("blocks_tile", D, rows=NB)
        QCS = sb("qc_tile", TPB * P, rows=QC)
        IDN = sb("ident", P)
        WINDOW = sb("window", P + WIN)
        BLOCKS = sb("blocks_valid", TPB * NB)
        BEFORE = sb("before", P)
        BEFOREB = sb("before_bf16", P, BF16)
        ONESB = sb("ones_bf16", P, BF16)
        IOTA = sb("iota", NT0)
        ROPE0 = sb("rope0", 2 * TPB * HR)
        ROPE1 = sb("rope1", 2 * TPB * D1 // 2)
        ZERO = sb("zeros", HID)
        MHALF = sb("minus_half", NT * (H1 + HKV))
        RB = sb("router_bias", E0)
        RTW = sb("router_w", KC * E0)
        TOP = sb("top8", NT * 8)
        TOPI = sb("top8_index", NT * 8, U32)
        TOPF = sb("top8_float", NT * 8)
        GATE = sb("gates", NT * K0)
        GSUM = sb("gate_sums", 2 * NT)
        SLOTF = sb("slots_float", NT * K0)
        SLOT = sb("slots", NT * K0, I32)
        IDX = sb("slots_tile", K0, I32)
        MASKB = sb("chosen_bf16", NT * E0, BF16)
        CUMB = sb("chosen_before_bf16", (NT + 1) * E0, BF16)
        START = sb("starts", 4 * E0)
        TEXP = sb("tile_expert_float", NT0)
        TEX = sb("tile_expert", NT0, I32)
        B1A = sb("expert_b1_T", E0 + NSH)
        B1B = sb("expert_b1_T2", E0 + NSH, rows=DHB)
        STAT = sb("ln_stats", NT * 6)
        MV = sb("ln_mean_var", NT * 2)
        RSTD = sb("rstd", NT)
        RR = sb("rms", H)
        SSQ = sb("sum_squares", H)
        KW = sb("norm_columns", 4)
        SINK = sb("sinks", 4 * H)
        LSUM = sb("prob_sums", 4 * H)
        CM = sb("block_max", 4 * H)
        ps = [ctx.enter_context(nc.psum_tensor(f"bank{i}", [P, 512], F32)) for i in range(8)]

        xn, xnT = XN[:, 0:NT * HID], XN[:, NT * HID:]
        x3, xn3 = v3(X[:, :], NT), v3(xn, NT)
        xnT3 = v3(xnT, KC)
        rw3 = v3(RW[:, :], E0)
        wc3 = v3(WC[:, :], H)
        kc3 = v3(KCAT[:, :], B)

        ELATE = 17
        tail = RW[:, ELATE * EW0:]
        o = 0

        def cut(n):
            nonlocal o
            o += n
            return tail[:, o - n:o]
        WCP = cut(M * KC * D)
        WGS = cut(H * HID)
        WOS = cut(H // 2 * HID)
        KRAW = cut(NT * D)
        KTMP = cut(NT * ROPE * 2)
        WKV = cut(KC * 2 * D)
        WQC = cut(KC * QC)
        o2 = 2 * NT * K0 * E0
        B1 = WC[0:E0 + NSH, o2:o2 + DH]
        KWR = WC[0:NB * B, o2 + DH:o2 + DH + D]
        LOGIT = WC[:, o2 + DH + D:o2 + DH + D + NT * E0]
        CUM = WC[:, o2 + DH + D + NT * E0:o2 + DH + D + 2 * NT * E0]
        CKR = TA[0:NB * B, 2560:2560 + 2 * D]
        ONEH, PROD = WC[:, 0:NT * K0 * E0], WC[:, NT * K0 * E0:2 * NT * K0 * E0]

        def route_dve(dve, st, E, K, chosen_ready, gates_sub):
            lg, tp, ti = v3(LOGIT[:, 0:NT * E], NT), v3(TOP[:, :], NT), v3(TOPI[:, :], NT)
            tf, g3 = v3(TOPF[:, :], NT), v3(GATE[:, 0:NT * K], NT)
            oh = ONEH[:, 0:NT * K * E].rearrange("p (t k e) -> p t k e", t=NT, k=K)
            pr = PROD[:, 0:NT * K * E].rearrange("p (t k e) -> p t k e", t=NT, k=K)
            for t in range(NT):
                st(nc.vector.max(tp[:, t, :], lg[:, t, :]))
            st.wait()
            for t in range(NT):
                st(nc.vector.max_index(ti[:, t, :], tp[:, t, :], lg[:, t, :]))
            st.wait()
            st.link(nc.vector.tensor_copy(TOPF[:, :], TOPI[:, :]))
            for t in range(NT):
                st(nc.vector.tensor_tensor(oh[:, t], bc(IOTA[:, 0:E].unsqueeze(1), [P, K, E]),
                                           bc(tf[:, t, 0:K].unsqueeze(2), [P, K, E]), ALU.is_equal))
            st.wait()
            st.link(nc.vector.tensor_reduce(v3(CUM[:, 0:NT * E], NT),
                                            ONEH[:, 0:NT * K * E].rearrange("p (t k e) -> p t e k", t=NT, k=K),
                                            AX, ALU.add))
            st(nc.vector.tensor_copy(MASKB[:, 0:NT * E], CUM[:, 0:NT * E]))
            st.link(nc.vector.memset(CUMB[:, 0:E], 0.0))
            for t in range(1, NT):
                st.link(nc.vector.tensor_tensor(CUM[:, t * E:(t + 1) * E], CUM[:, (t - 1) * E:t * E],
                                                CUM[:, t * E:(t + 1) * E], ALU.add))
            nc.vector.tensor_copy(CUMB[:, E:(NT + 1) * E], CUM[:, 0:NT * E]).then_inc(chosen_ready, 1)
            nc.vector.tensor_tensor(g3, tp[:, :, 0:K], bc(tp[:, :, 0:1], [P, NT, K]), ALU.subtract).then_inc(gates_sub, 1)

        def route_dve_slots(dve, st, E, K, ntile, bank, rank_ready, gates_exp, slots_ready):
            g3 = v3(GATE[:, 0:NT * K], NT)
            pr = PROD[:, 0:NT * K * E].rearrange("p (t k e) -> p t k e", t=NT, k=K)
            oh = ONEH[:, 0:NT * K * E].rearrange("p (t k e) -> p t k e", t=NT, k=K)
            dve.wait_ge(gates_exp, 1)
            st.link(nc.vector.reduce_sum(GSUM[:, 0:NT], g3, AX))
            st.link(nc.vector.reciprocal(GSUM[:, NT:], GSUM[:, 0:NT]))
            st(nc.vector.tensor_tensor(g3, g3, bc(GSUM[:, NT:].unsqueeze(2), [P, NT, K]), ALU.mult))
            dve.wait_ge(rank_ready, 1)
            n = START[:, 0:E]
            st.link(nc.vector.tensor_scalar(n, bank[:, NT * E:(NT + 1) * E], 1.0 / P,
                                            (P - 1.0) / P - 0.5 + 0.5 / P, ALU.mult, ALU.add))
            st.link(nc.vector.tensor_scalar(n, n, MAGIC, -MAGIC, ALU.add, ALU.add))
            st.link(nc.vector.memset(START[:, E0:E0 + E], 1.0))
            st.link(nc.vector.tensor_tensor_scan(START[:, 2 * E0:2 * E0 + E], START[:, E0:E0 + E], n, 0.0,
                                                 ALU.mult, ALU.add))
            st.link(nc.vector.tensor_tensor(n, START[:, 2 * E0:2 * E0 + E], n, ALU.subtract))
            st.link(nc.vector.tensor_scalar(START[:, E0:E0 + E], n, float(P), None, ALU.mult))
            st.link(nc.vector.tensor_tensor(v3(CUM[:, 0:NT * E], NT), v3(bank[:, 0:NT * E], NT),
                                            bc(START[:, E0:E0 + E].unsqueeze(1), [P, NT, E]), ALU.add))
            for t in range(NT):
                st(nc.vector.tensor_tensor(pr[:, t], oh[:, t],
                                           bc(CUM[:, t * E:(t + 1) * E].unsqueeze(1), [P, K, E]), ALU.mult))
            st.wait()
            st.link(nc.vector.tensor_reduce(v3(SLOTF[:, 0:NT * K], NT), pr, AX, ALU.add))
            nc.vector.tensor_copy(SLOT[:, 0:NT * K], SLOTF[:, 0:NT * K]).then_inc(slots_ready, 1)
            ge = WC[0:1, 0:ntile * E].rearrange("p (i e) -> p i e", i=ntile)
            dve.wait_ge(slots_ready, 1)
            st.link(nc.vector.tensor_tensor(ge, bc(IOTA[0:1, 0:ntile].unsqueeze(2), [1, ntile, E]),
                                            bc(START[0:1, 0:E].unsqueeze(1), [1, ntile, E]), ALU.is_ge))
            st.link(nc.vector.reduce_sum(TEXP[0:1, 0:ntile], ge, AX))
            st.link(nc.vector.tensor_scalar(TEXP[0:1, 0:ntile], TEXP[0:1, 0:ntile], -1.0, None, ALU.add))
            nc.vector.tensor_copy(TEX[0:1, 0:ntile], TEXP[0:1, 0:ntile]).then_inc(slots_ready, 1)

        def rank_pe(pe, E, bank, chosen_ready, rank_ready):
            pe.wait_ge(chosen_ready, 1)
            for t in range(NT):
                nc.tensor.matmul(bank[:, t * E:(t + 1) * E], BEFOREB[:, :], MASKB[:, t * E:(t + 1) * E],
                                 start=True, stop=False)
                nc.tensor.matmul(bank[:, t * E:(t + 1) * E], ONESB[:, :], CUMB[:, t * E:(t + 1) * E],
                                 start=False, stop=True)
            nc.tensor.matmul(bank[:, NT * E:(NT + 1) * E], ONESB[:, :], CUMB[:, NT * E:(NT + 1) * E],
                             start=True, stop=True).then_inc(rank_ready, 1)

        def layernorm_dve(dve, st, stats_ready, rstd_ready, xn_ready):
            mv = v3(MV[:, :], NT)
            for t in range(NT):
                st(nc.vector.bn_stats(STAT[:, 6 * t:6 * t + 6], x3[:, t, :]))
            st.wait()
            for t in range(NT):
                ins = nc.vector.bn_aggr(mv[:, t, :], STAT[:, 6 * t:6 * t + 6])
                if t < NT - 1:
                    st(ins)
            ins.then_inc(stats_ready, 1)
            st.wait()
            dve.wait_ge(rstd_ready, 1)
            for t in range(NT):
                nc.vector.tensor_scalar(xn3[:, t, :], x3[:, t, :], mv[:, t, 0:1], RSTD[:, t:t + 1],
                                        ALU.subtract, ALU.mult).then_inc(xn_ready, 1)

        def layernorm_pool(pool, stats_ready, var_ready, rstd_ready):
            pool.wait_ge(stats_ready, 1)
            nc.gpsimd.tensor_scalar(RSTD[:, :].unsqueeze(2), v3(MV[:, :], NT)[:, :, 1:2], LN_EPS, None,
                                    ALU.add).then_inc(var_ready, 1)
            pool.wait_ge(var_ready, 1)
            nc.gpsimd.tensor_tensor(RSTD[:, :], RSTD[:, :], MHALF[:, 0:NT], ALU.pow).then_inc(rstd_ready, 1)

        ld_x, ld_c, ld_rt, ld_sh, ld_aw, ld_cp, ld_wg, ld_ex, ld_ex2 = (
            sem(n) for n in ("ld_x", "ld_const", "ld_router", "ld_shared", "ld_attn_w", "ld_comp", "ld_wg",
                             "ld_experts", "ld_experts2"))
        n_c = n_rt = n_sh = n_aw = n_ex = n_ex2 = 0
        zero_set, zero_done = sem("zero_set"), sem("zero_done")
        const_set = sem("const_set")
        dve1, act1, pool1 = sem("dve1"), sem("act1"), sem("pool1")
        stats0, var0, rstd0, xn0 = sem("stats0"), sem("var0"), sem("rstd0"), sem("xn0")
        xt_ps, xt_sb = sem("xT_psum"), sem("xT_sbuf")
        lg_ps, lg_sb = sem("logit_psum"), sem("logit_sbuf")
        b1_ps, b1_sb = sem("b1_psum"), sem("b1_sbuf")
        chosen0, rank0, gsub0, gexp0, slots0 = (sem(n) for n in ("chosen0", "rank0", "gates_sub0", "gates_exp0", "slots0"))
        scat0 = sem("scatter0")
        sh_ps, sh_sb, so_ps, so_sb = (sem(n) for n in ("shared_h_psum", "shared_h_sbuf", "shared_o_psum", "shared_o_sbuf"))
        wt_ps, wt_sb, wf_ps, wf_sb = (sem(n) for n in ("wgT_psum", "wgT_sbuf", "fold_psum", "fold_sbuf"))
        kv_ps, kv_sb, v2_ps, v2_sb, qc_ps, qc_sb, ck_ps = (
            sem(n) for n in ("kv_psum", "kv_sbuf", "v2_psum", "v2_sbuf", "qc_psum", "qc_sbuf", "ck_psum"))
        kss, krr, kn_r, kt_ps, kt_sb = (sem(n) for n in ("k_squares", "k_rms", "k_normed", "kT_psum", "kT_sbuf"))
        css, crr, ck_r, ckd, kvp = (sem(n) for n in ("ck_squares", "ck_rms", "ck_ready", "ck_moved", "pool_k"))

        wkv3, wqc3 = v3(WKV, KC), v3(WQC, KC)
        wcp3 = v3(WCP, M * KC)
        wgs3, wos3 = v3(WGS, H), v3(WOS, H // 2)
        sw1 = SW1[:, :].rearrange("p (s k n) -> p s k n", s=NSH, k=KC)
        sw2 = SW2[:, :].rearrange("p (s c n) -> p s c n", s=NSH, c=2)
        va3, v2a3, ck03 = v3(VA[:, :], NT), v3(V2A[:, :], B), v3(CK0[:, :], B)
        HF = T // 2
        shA = v3(TA[:, 0:NSH * HF], NSH)
        shB = v3(TA[:, NSH * HF:2 * NSH * HF], NSH)
        wgT = [TA[:, 2 * NSH * HF + i * HID:2 * NSH * HF + (i + 1) * HID] for i in range(2)]
        kraw3 = v3(KRAW, NT)

        with nc.Block() as block:
            @block.sync
            def _(sp):
                nonlocal n_c, n_rt, n_sh, n_aw, n_ex, n_ex2
                sp.dma_start(x3, a["L0_attn_h"].rearrange("b (j p) d -> p (b j) d", p=P)).then_inc(ld_x, 16)
                for t, n in ((IDN, "ident"), (BEFORE, "before"), (IOTA, "iota"), (WINDOW, "window"),
                             (BLOCKS, "blocks"), (ROPE0, "rope0"), (ROPE1, "rope1")):
                    sp.dma_start(t[:, :], a["table_" + n]).then_inc(ld_c, 16)
                    n_c += 16
                sp.dma_start(v3(RTW[:, :], KC), a["L0_ffn_router_w"].rearrange("(k p) e -> p k e", p=P)).then_inc(ld_rt, 16)
                sp.dma_start(RB[:, :], a["L0_ffn_router_b"].partition_broadcast(P)).then_inc(ld_rt, 16)
                for s in range(NSH):
                    sp.dma_start(sw1[:, s], a["L0_ffn_sw1"][s].rearrange("(k p) n -> p k n", p=P)).then_inc(ld_sh, 16)
                    sp.dma_start(sw2[:, s, 0], a["L0_ffn_sw2"][s, 0:P, :]).then_inc(ld_sh, 16)
                    sp.dma_start(sw2[0:DHB, s, 1], a["L0_ffn_sw2"][s, P:DH, :]).then_inc(ld_sh, 16)
                    sp.dma_start(sw2[DHB:DHB + 1, s, 1], a["L0_ffn_sb2"][s:s + 1, :]).then_inc(ld_sh, 16)
                    n_sh += 64
                sp.dma_start(B1[0:E0, :], a["L0_ffn_rb1"]).then_inc(ld_sh, 16)
                sp.dma_start(B1[E0:E0 + NSH, :], a["L0_ffn_sb1"]).then_inc(ld_sh, 16)
                n_sh += 32
                for k in range(KC):
                    sp.dma_start(wkv3[:, k, 0:D], a["L0_attn_Wk"][k * P:(k + 1) * P, :]).then_inc(ld_aw, 16)
                    sp.dma_start(wkv3[:, k, D:], a["L0_attn_Wv"][k * P:(k + 1) * P, :]).then_inc(ld_aw, 16)
                    sp.dma_start(wqc3[:, k, :], a["L0_attn_Wq_c"][k * P:(k + 1) * P, :]).then_inc(ld_aw, 16)
                col = lambda n: a[n].rearrange("(p o) -> p o", o=1)
                sp.dma_start(KW[:, 0:1], col("L0_attn_q_norm_w")).then_inc(ld_aw, 16)
                sp.dma_start(KW[:, 1:2], col("L0_attn_k_norm_w")).then_inc(ld_aw, 16)
                sp.dma_start(KWR[:, :], a["L0_attn_k_norm_w"].partition_broadcast(NB * B)).then_inc(ld_aw, 16)
                sp.dma_start(SINK[:, 0:H], a["L0_attn_sink"].partition_broadcast(P)).then_inc(ld_aw, 16)
                n_aw = 16 * (3 * KC + 4)
                sp.dma_start(wcp3, a["L0_attn_W_comp"].rearrange("(c p) d -> p c d", p=P)).then_inc(ld_cp, 16)
                sp.dma_start(wgs3, a["L0_attn_Wg"].rearrange("g (r p) i -> p (g r) i", p=P)).then_inc(ld_wg, 16)
                sp.dma_start(wos3, a["L0_attn_Wo"].rearrange("(c p) n -> p c n", p=P)).then_inc(ld_wg, 16)
                sp.dma_start(WQ[:, :], a["L0_attn_Wq_up"]).then_inc(ld_ex, 16)

                def experts(e0, e1, done):
                    for k in range(KC):
                        sp.dma_start(rw3[:, e0:e1, k * DH:(k + 1) * DH],
                                     a["L0_ffn_rw1"][e0:e1, k * P:(k + 1) * P, :].rearrange("e p n -> p e n")).then_inc(done, 16)
                    sp.dma_start(rw3[:, e0:e1, W2A:W2B], a["L0_ffn_rw2"][e0:e1, 0:P, :].rearrange("e p n -> p e n")).then_inc(done, 16)
                    sp.dma_start(rw3[0:DHB, e0:e1, W2B:], a["L0_ffn_rw2"][e0:e1, P:DH, :].rearrange("e p n -> p e n")).then_inc(done, 16)
                    sp.dma_start(rw3[DHB:DHB + 1, e0:e1, W2B:], a["L0_ffn_rb2"][e0:e1, :].unsqueeze(0)).then_inc(done, 16)
                experts(0, ELATE, ld_ex)
                sp.wait_ge(ck_r, 1)
                for b in range(B):
                    rows = CKR[b * NB:(b + 1) * NB, 0:D]
                    sp.dma_start(v2a3[WIN:WIN + NB, b, :], rows).then_inc(ckd, 16)
                    sp.dma_start(ck03[0:NB, b, :], rows).then_inc(ckd, 16)
                sp.wait_ge(wf_ps, H)
                sp.wait_ge(ck_ps, 1)
                sp.wait_ge(qc_ps, 2)
                sp.wait_ge(v2_ps, 1)
                sp.wait_ge(kt_ps, 2)
                experts(ELATE, E0, ld_ex2)
                sp.wait_ge(ckd, 16 * 2 * B)

            @block.gpsimd
            def _(pool):
                st = Steps(pool, pool1)
                nc.gpsimd.memset(ZERO[:, :], 0.0).then_inc(zero_set, 1)
                pool.wait_ge(zero_set, 1)
                nc.gpsimd.memset(MHALF[:, :], -0.5).then_inc(const_set, 1)
                pool.wait_ge(const_set, 1)
                nc.gpsimd.memset(ONESB[:, :], 1.0).then_inc(const_set, 1)
                pool.wait_ge(const_set, 2)
                nc.gpsimd.memset(TA[32:64, NSH * HF:2 * NSH * HF], 1.0).then_inc(const_set, 1)
                pool.wait_ge(const_set, 3)
                nc.gpsimd.memset(QCT[:, NT * P:], 0.0).then_inc(const_set, 1)
                pool.wait_ge(const_set, 4)
                layernorm_pool(pool, stats0, var0, rstd0)

                def scatter(t0, t1):
                    for t in range(t0, t1):
                        for k in range(K0):
                            nc.gpsimd.indirect_dma_start(
                                xs0, bass.IndirectOffsetOnAxis(ap=SLOT[:, t * K0 + k:t * K0 + k + 1], axis=0),
                                xn3[:, t, :], None).then_inc(scat0, 16)
                pool.wait_ge(slots0, 1)
                pool.wait_ge(zero_done, 16 * (NT0 // 4))
                scatter(0, NT // 2)
                pool.wait_ge(css, 1)
                nc.gpsimd.tensor_scalar(CM[0:NB * B, 1:2], CM[0:NB * B, 0:1], 1.0 / D, RMS_EPS, ALU.mult, ALU.add).then_inc(kvp, 1)
                pool.wait_ge(kvp, 1)
                nc.gpsimd.tensor_tensor(CM[0:NB * B, 2:3], CM[0:NB * B, 1:2], MHALF[0:NB * B, 0:1], ALU.pow).then_inc(crr, 1)
                pool.wait_ge(kss, 1)
                nc.gpsimd.tensor_scalar(RR[:, 0:NT], SSQ[:, 0:NT], 1.0 / D, RMS_EPS, ALU.mult, ALU.add).then_inc(kvp, 1)
                pool.wait_ge(kvp, 2)
                nc.gpsimd.tensor_tensor(RR[:, NT:2 * NT], RR[:, 0:NT], MHALF[:, 0:NT], ALU.pow).then_inc(krr, 1)
                scatter(NT // 2, NT)

            @block.scalar
            def _(act):
                act.wait_ge(zero_set, 1)
                for i in range(NT0 // 4):
                    act.dma_start(xs0[i * 4 * P:(i + 1) * 4 * P, :].rearrange("(c p) d -> p c d", p=P),
                                  bc(ZERO[:, :].unsqueeze(1), [P, 4, HID])).then_inc(zero_done, 16)
                for t in range(NT):
                    act.wait_ge(xt_ps, t + 1)
                    nc.scalar.activation(xnT3[:, :, t * P:(t + 1) * P], v3(ps[t % 2][:, 0:HID], KC), ACT.Copy).then_inc(xt_sb, 1)
                act.wait_ge(b1_ps, 1)
                nc.scalar.activation(B1A[:, :], ps[3][:, 0:E0 + NSH], ACT.Copy).then_inc(b1_sb, 1)
                nc.scalar.activation(B1B[:, :], ps[3][0:DHB, 64:64 + E0 + NSH], ACT.Copy).then_inc(b1_sb, 1)
                act.wait_ge(b1_sb, 2)
                act.wait_ge(const_set, 4)

                def shared_relu(i):
                    hf, s, c = i // 4, i // 2 % 2, i % 2
                    act.wait_ge(sh_ps, i + 1)
                    if hf and not s and not c:
                        act.wait_ge(so_ps, NT // 2)
                    if c == 0:
                        nc.scalar.activation(shA[:, s, :], ps[4 + i % 2][:, :], ACT.Relu,
                                             bias=B1A[:, E0 + s:E0 + s + 1]).then_inc(sh_sb, 1)
                    else:
                        nc.scalar.activation(shB[0:DHB, s, :], ps[4 + i % 2][0:DHB, :], ACT.Relu,
                                             bias=B1B[:, E0 + s:E0 + s + 1]).then_inc(sh_sb, 1)
                for i in range(4):
                    shared_relu(i)
                act.wait_ge(gsub0, 1)
                nc.scalar.activation(GATE[:, :], GATE[:, :], ACT.Exp).then_inc(gexp0, 1)
                for i in range(4, 8):
                    shared_relu(i)
                for n in range(2):
                    act.wait_ge(qc_ps, n + 1)
                    nc.scalar.activation(QCT[:, n * 512:(n + 1) * 512], ps[4 + n][0:QC, :], ACT.Copy).then_inc(qc_sb, 1)
                act.wait_ge(v2_ps, 1)
                nc.scalar.activation(V2A[0:WIN, :], ps[2][0:WIN, :], ACT.Copy).then_inc(v2_sb, 1)
                for h in range(H):
                    act.wait_ge(wt_ps, h + 1)
                    if h >= 2:
                        act.wait_ge(wf_ps, h - 1)
                    nc.scalar.activation(wgT[h % 2], ps[4 + h % 2][:, 0:HID], ACT.Copy).then_inc(wt_sb, 1)

            @block.vector
            def _(dve):
                st = Steps(dve, dve1)
                dve.wait_ge(ld_c, n_c)
                nc.vector.tensor_copy(BEFOREB[:, :], BEFORE[:, :]).then_inc(dve1, 1)
                st.n += 1
                dve.wait_ge(ld_x, 16)
                layernorm_dve(dve, st, stats0, rstd0, xn0)
                dve.wait_ge(lg_ps, 1)
                dve.wait_ge(ld_rt, 32)
                st.link(nc.vector.tensor_tensor(v3(LOGIT[:, :], NT), v3(ps[2][:, 0:NT * E0], NT),
                                                bc(RB[:, :].unsqueeze(1), [P, NT, E0]), ALU.add))
                route_dve(dve, st, E0, K0, chosen0, gsub0)
                route_dve_slots(dve, st, E0, K0, NT0, ps[3], rank0, gexp0, slots0)

                def shared_add(t):
                    dve.wait_ge(so_ps, t + 1)
                    nc.vector.scalar_tensor_tensor(out=x3[:, t, :], in0=ps[t % 2][:, 0:HID], scalar=1.0 / NSH,
                                                   in1=x3[:, t, :], op0=ALU.mult, op1=ALU.add).then_inc(so_sb, 1)
                for t in range(NT):
                    shared_add(t)
                dve.wait_ge(ck_ps, 1)
                dve.wait_ge(ld_aw, n_aw)
                ckn = CKR[:, 0:D]
                st.link(nc.vector.tensor_copy(CKR[:, D:], ps[3][0:NB * B, 0:D]))
                nc.vector.scalar_tensor_tensor(out=ckn, in0=CKR[:, D:], scalar=1.0, in1=CKR[:, D:], op0=ALU.mult,
                                               op1=ALU.mult, accum_out=CM[0:NB * B, 0:1]).then_inc(css, 1)
                dve.wait_ge(css, 1)
                for t in range(NT):
                    dve.wait_ge(kv_ps, t + 1)
                    st(nc.vector.tensor_copy(kraw3[:, t, :], ps[6 + t % 2][:, 0:D]))
                    nc.vector.tensor_copy(va3[:, t, :], ps[6 + t % 2][:, D:2 * D]).then_inc(kv_sb, 1)
                st.wait()
                sq = KTMP[:, 0:D]
                for t in range(NT):
                    ins = nc.vector.scalar_tensor_tensor(out=v3(KTMP, NT)[:, t, :], in0=kraw3[:, t, :], scalar=1.0, in1=kraw3[:, t, :],
                                                         op0=ALU.mult, op1=ALU.mult, accum_out=SSQ[:, t:t + 1])
                    if t < NT - 1:
                        st(ins)
                ins.then_inc(kss, 1)
                st.wait()
                dve.wait_ge(kss, 1)
                k4 = KRAW.rearrange("p (b j d) -> p b j d", b=B, j=TPB)
                k1, k2 = k4[:, :, :, 0:HR], k4[:, :, :, HR:ROPE]
                tmp = [KTMP[:, i * NT * HR:(i + 1) * NT * HR].rearrange("p (b j d) -> p b j d", b=B, j=TPB) for i in range(4)]
                cs = [bc(v3(ROPE0[:, i * TPB * HR:(i + 1) * TPB * HR], TPB).unsqueeze(1), [P, B, TPB, HR]) for i in range(2)]
                for dst, src, c in ((0, k1, 0), (1, k2, 1), (2, k1, 1), (3, k2, 0)):
                    for b in range(B):
                        st(nc.vector.tensor_tensor(tmp[dst][:, b], src[:, b], cs[c][:, b], ALU.mult))
                st.wait()
                st(nc.vector.tensor_tensor(k1, tmp[0], tmp[1], ALU.subtract))
                st(nc.vector.tensor_tensor(k2, tmp[2], tmp[3], ALU.add))
                st.link(nc.vector.tensor_tensor(KW[:, 2:3], KW[:, 0:1], KW[:, 1:2], ALU.mult))
                dve.wait_ge(crr, 1)
                nc.vector.scalar_tensor_tensor(out=ckn, in0=CKR[:, D:], scalar=CM[0:NB * B, 2:3], in1=KWR[:, :],
                                               op0=ALU.mult, op1=ALU.mult).then_inc(ck_r, 1)
                dve.wait_ge(krr, 1)
                nc.vector.tensor_tensor(kraw3, kraw3, bc(RR[:, NT:].unsqueeze(2), [P, NT, D]), ALU.mult).then_inc(kn_r, 1)
                for h in range(H):
                    dve.wait_ge(wf_ps, h + 1)
                    nc.vector.tensor_copy(wc3[:, h, :], ps[6 + h % 2][:, 0:HID]).then_inc(wf_sb, 1)
                for half in range(2):
                    dve.wait_ge(kt_ps, half + 1)
                    b4 = ps[half][:, :].rearrange("p (b j t) -> p b j t", b=2, j=TPB)
                    dst = kc3[:, 2 * half:2 * half + 2, :]
                    w = KW[:, 2:3]
                    nc.vector.tensor_scalar(dst[:, :, 0:P], b4[:, :, 0, :], w, None, ALU.mult).then_inc(kt_sb, 1)
                    nc.vector.tensor_scalar(dst[:, :, P + NB:2 * P + NB], b4[:, :, 1, :], w, None, ALU.mult).then_inc(kt_sb, 1)
                    nc.vector.tensor_scalar(dst[:, :, 2 * P + NB:2 * P + NB + WIN], b4[:, :, 0, P - WIN:], w, None, ALU.mult).then_inc(kt_sb, 1)
                dve.wait_ge(kt_ps, 3)
                c3 = v3(ps[2][:, 0:B * NB], B)
                nc.vector.tensor_scalar(kc3[:, :, P:P + NB], c3, KW[:, 0:1], None, ALU.mult).then_inc(kt_sb, 1)
                nc.vector.tensor_scalar(kc3[:, :, KROW - NB:], c3, KW[:, 0:1], None, ALU.mult).then_inc(kt_sb, 1)
                m0 = SINK[:, H:2 * H]
                st.link(nc.vector.tensor_scalar(m0, SINK[:, 0:H], 0.0, None, ALU.max))
                st(nc.vector.tensor_tensor(SINK[:, 2 * H:3 * H], SINK[:, 0:H], m0, ALU.subtract))
                st.link(nc.vector.tensor_scalar(m0, m0, -1.0, None, ALU.mult))

            @block.tensor
            def _(pe):
                pe.wait_ge(ld_c, n_c)
                for t in range(NT):
                    pe.wait_ge(xn0, t + 1)
                    if t >= 2:
                        pe.wait_ge(xt_sb, t - 1)
                    for k in range(KC):
                        ins = nc.tensor.transpose(ps[t % 2][:, k * P:(k + 1) * P], xn3[:, t, k * P:(k + 1) * P], IDN[:, :])
                    ins.then_inc(xt_ps, 1)
                pe.wait_ge(ld_sh, n_sh)
                nb = E0 + NSH
                nc.tensor.transpose(ps[3][:, 0:nb], B1[:, 0:P], IDN[0:nb, 0:nb])
                nc.tensor.transpose(ps[3][0:DHB, 64:64 + nb], B1[:, P:DH], IDN[0:nb, 0:nb]).then_inc(b1_ps, 1)
                pe.wait_ge(ld_rt, 32)
                pe.wait_ge(xt_sb, NT)
                for t in range(NT):
                    for k in range(KC):
                        ins = nc.tensor.matmul(ps[2][:, t * E0:(t + 1) * E0], xnT3[:, k, t * P:(t + 1) * P],
                                               v3(RTW[:, :], KC)[:, k, :], start=(k == 0), stop=(k == KC - 1))
                ins.then_inc(lg_ps, 1)

                def shared_up(hf):
                    for s in range(NSH):
                        for c in range(2):
                            i = 4 * hf + 2 * s + c
                            if i >= 2:
                                pe.wait_ge(sh_sb, i - 1)
                            n = P if c == 0 else DHB
                            for k in range(KC):
                                ins = nc.tensor.matmul(ps[4 + i % 2][0:n, :], sw1[:, s, k, c * P:c * P + n],
                                                       xnT3[:, k, hf * HF:(hf + 1) * HF], start=(k == 0), stop=(k == KC - 1))
                            ins.then_inc(sh_ps, 1)

                def shared_down(hf):
                    pe.wait_ge(sh_sb, 4 * hf + 4)
                    for i in range(NT // 2):
                        t = hf * NT // 2 + i
                        if t >= 2:
                            pe.wait_ge(so_sb, t - 1)
                        for s in range(NSH):
                            nc.tensor.matmul(ps[t % 2][:, 0:HID], shA[:, s, i * P:(i + 1) * P], sw2[:, s, 0],
                                             start=(s == 0), stop=False)
                            ins = nc.tensor.matmul(ps[t % 2][:, 0:HID], shB[0:DHB + 1, s, i * P:(i + 1) * P],
                                                   sw2[0:DHB + 1, s, 1], start=False, stop=(s == NSH - 1))
                        ins.then_inc(so_ps, 1)
                shared_up(0)
                pe.wait_ge(b1_sb, 2)
                rank_pe(pe, E0, ps[3], chosen0, rank0)
                shared_down(0)
                shared_up(1)
                shared_down(1)
                pe.wait_ge(ld_cp, 16)
                pe.wait_ge(slots0, 1)
                for c in range(M * KC):
                    m, k = c // KC, c % KC
                    ins = nc.tensor.matmul(ps[3][0:NB * B, 0:D], xnT3[:, k, m:T:M], wcp3[:, c, :],
                                           start=(c == 0), stop=(c == M * KC - 1))
                ins.then_inc(ck_ps, 1)
                pe.wait_ge(ld_aw, n_aw)
                for t in range(NT):
                    if t >= 2:
                        pe.wait_ge(kv_sb, t - 1)
                    for k in range(KC):
                        ins = nc.tensor.matmul(ps[6 + t % 2][:, 0:2 * D], xnT3[:, k, t * P:(t + 1) * P], wkv3[:, k, :],
                                               start=(k == 0), stop=(k == KC - 1))
                    ins.then_inc(kv_ps, 1)
                pe.wait_ge(sh_sb, 8)
                for n in range(2):
                    for k in range(KC):
                        ins = nc.tensor.matmul(ps[4 + n][0:QC, :], wqc3[:, k, :], xnT3[:, k, n * 512:(n + 1) * 512],
                                               start=(k == 0), stop=(k == KC - 1))
                    ins.then_inc(qc_ps, 1)
                for b in range(B):
                    for k in range(KC):
                        lo = b * S + P - WIN
                        ins = nc.tensor.matmul(ps[2][0:WIN, b * D:(b + 1) * D], xnT3[:, k, lo:lo + WIN], wkv3[:, k, D:],
                                               start=(k == 0), stop=(k == KC - 1))
                ins.then_inc(v2_ps, 1)
                pe.wait_ge(ld_wg, 32)
                pe.wait_ge(kv_sb, NT)
                pe.wait_ge(qc_sb, 2)

                def fold(h):
                    pe.wait_ge(wt_sb, h + 1)
                    if h >= 2:
                        pe.wait_ge(wf_sb, h - 1)
                    for k in range(KC):
                        ins = nc.tensor.matmul(ps[6 + h % 2][:, 0:HID], wgT[h % 2][:, k * P:(k + 1) * P],
                                               wos3[:, h // 4 * KC + k, :], start=(k == 0), stop=(k == KC - 1))
                    ins.then_inc(wf_ps, 1)
                for h in range(H):
                    if h >= 2:
                        pe.wait_ge(wt_sb, h - 1)
                    for k in range(KC):
                        ins = nc.tensor.transpose(ps[4 + h % 2][:, k * P:(k + 1) * P], wgs3[:, h, k * P:(k + 1) * P], IDN[:, :])
                    ins.then_inc(wt_ps, 1)
                    if h >= 1:
                        fold(h - 1)
                fold(H - 1)
                pe.wait_ge(kn_r, 1)
                pe.wait_ge(so_sb, NT)
                for half in range(2):
                    for i in range(NT // 2):
                        ins = nc.tensor.transpose(ps[half][:, i * P:(i + 1) * P], kraw3[:, half * NT // 2 + i, :], IDN[:, :])
                    ins.then_inc(kt_ps, 1)
                pe.wait_ge(ck_r, 1)
                pe.wait_ge(v2_sb, 1)
                nc.tensor.transpose(ps[2][:, 0:B * NB], CKR[:, 0:D], IDN[0:B * NB, 0:B * NB]).then_inc(kt_ps, 1)

        tile_sems = ([sem(f"tile_loaded{i}") for i in range(4)], [sem(f"tile_stored{i}") for i in range(2)],
                     [sem("tile_" + n) for n in ("xT_psum", "xT_sbuf", "h_psum", "h_sbuf", "hT_psum", "hT_sbuf",
                                                 "y_psum", "y_sbuf", "silu")])

        def expert_block(before, before_mid, ntile, xs, ys, loads, scattered, n_scattered, stages):
            ld, stq, (xT_ps, xT_sb, h_ps, h_sb, hT_ps, hT_sb, y_ps, y_sb, mid) = tile_sems

            def await_tiles(eng, s, n):
                eng.wait_ge(s, n + before)

            def await_dma(eng, s, n, rings):
                eng.wait_ge(s, n + before * 16 // rings)
            SK = 3
            G0 = 5
            xt = [TA[:, i * HID:(i + 1) * HID] for i in range(4)]
            xT = [TA[:, (4 + i) * HID:(5 + i) * HID] for i in range(2)]
            hs = [TA[:, (6 + i) * HID:(7 + i) * HID] for i in range(2)]
            hT = [TA[:, (8 + i) * HID:(9 + i) * HID] for i in range(2)]
            yt = [TA[:, (10 + i) * HID:(11 + i) * HID] for i in range(2)]

            def experts(engine, g, n):
                return nc.values_load_multi_w_load_instructions(
                    TEX[0:1, bass.ds(g, n)], [engine], min_val=0, max_val=stages["E"] - 1,
                    skip_runtime_bounds_check_because="a count of the experts that start at a tile or before, less one")[1]

            def run(eng, step, engine=None, lags=()):
                def outside(g):
                    on = lambda lag: 0 <= g - lag < ntile
                    e = {lag: experts(engine, g - lag, 1)[0] for lag in lags if on(lag)}
                    step(g, g % 4, lambda n, lag: (g - lag) // n, on, e.get)
                for g in range(G0):
                    outside(g)
                n4 = (ntile - G0) // 4
                with eng.Fori(0, n4) as i:
                    e = {}
                    if lags:
                        first, n = G0 - max(lags), 4 + max(lags) - min(lags)
                        e = dict(zip(range(first, first + n), experts(engine, i * 4 + first, n)))
                    for c in range(G0, G0 + 4):
                        step(i * 4 + c, c % 4, lambda n, lag: i * (4 // n) + (c - lag) // n, lambda lag: True,
                             lambda lag: e.get(c - lag))
                for g in range(G0 + 4 * n4, ntile + SK):
                    outside(g)

            def early(g, n):
                return isinstance(g, int) and g < n

            with nc.Block() as block:
                @block.sync
                def _(sp):
                    sp.wait_ge(scattered, n_scattered)
                    for s, n in loads:
                        sp.wait_ge(s, n)

                    def step(g, q, rounds, on, expert):
                        if on(0):
                            if not early(g, 4):
                                await_tiles(sp, xT_ps, g - 3)
                            sp.dma_start(xt[q], xs[bass.ds(g * P, P), :]).then_inc(ld[q], 16)
                    run(sp, step)

                @block.tensor
                def _(pe):
                    for s, n in loads:
                        pe.wait_ge(s, n)

                    def step(g, q, rounds, on, expert):
                        if on(0):
                            await_dma(pe, ld[q], rounds(4, 0) * 16 + 16, 4)
                            for k in range(KC):
                                ins = nc.tensor.transpose(ps[q % 2][:, k * P:(k + 1) * P], xt[q][:, k * P:(k + 1) * P], IDN[:, :])
                            ins.then_inc(xT_ps, 1)
                        if on(1):
                            await_tiles(pe, xT_sb, g)
                            stages["up"](expert(1), ps[2 + (q + 1) % 2], xT[(q + 1) % 2]).then_inc(h_ps, 1)
                        if on(2):
                            await_tiles(pe, h_sb, g - 1)
                            stages["turn"](ps[4 + q % 2], hs[q % 2]).then_inc(hT_ps, 1)
                        if on(3):
                            await_tiles(pe, hT_sb, g - 2)
                            if not early(g, 5):
                                await_tiles(pe, y_sb, g - 4)
                            stages["down"](expert(3), ps[6 + (q + 1) % 2], hT[(q + 1) % 2]).then_inc(y_ps, 1)
                    run(pe, step, mybir.EngineType.PE, (1, 3))

                @block.scalar
                def _(act):
                    def step(g, q, rounds, on, expert):
                        if on(0):
                            await_tiles(act, xT_ps, g + 1)
                            if not early(g, 2):
                                await_tiles(act, h_ps, g - 1)
                            nc.scalar.activation(xT[q % 2], ps[q % 2][:, 0:HID], ACT.Copy).then_inc(xT_sb, 1)
                        if stages["act_mid"] and on(1):
                            await_tiles(act, h_ps, g)
                            if not early(g, 3):
                                await_tiles(act, hT_ps, g - 2)
                            stages["act_mid"](ps[2 + (q + 1) % 2], hs[(q + 1) % 2]).then_inc(mid, 1)
                        if on(2):
                            await_tiles(act, hT_ps, g - 1)
                            if not early(g, 4):
                                await_tiles(act, y_ps, g - 3)
                            stages["act_turn"](expert(2), ps[4 + q % 2], hT[q % 2], hT_sb)
                        if on(3):
                            await_tiles(act, y_sb, g - 2)
                            act.dma_start(ys[bass.ds((g - 3) * P, P), :], yt[(q + 1) % 2]).then_inc(stq[(q + 1) % 2], 16)
                    run(act, step, mybir.EngineType.Activation, (2,) if stages["bias"] else ())
                    await_dma(act, stq[0], 16 * (ntile // 2), 2)
                    await_dma(act, stq[1], 16 * (ntile // 2), 2)

                @block.vector
                def _(dve):
                    def step(g, q, rounds, on, expert):
                        if on(1):
                            if stages["act_mid"]:
                                dve.wait_ge(mid, g + before_mid)
                            else:
                                await_tiles(dve, h_ps, g)
                            if not early(g, 3):
                                await_tiles(dve, hT_ps, g - 2)
                            stages["dve_mid"](ps[2 + (q + 1) % 2], hs[(q + 1) % 2]).then_inc(h_sb, 1)
                        if on(3):
                            await_tiles(dve, y_ps, g - 2)
                            if not early(g, 5):
                                await_dma(dve, stq[(q + 1) % 2], rounds(2, 3) * 16, 2)
                            nc.vector.tensor_copy(yt[(q + 1) % 2], ps[6 + (q + 1) % 2][:, 0:HID]).then_inc(y_sb, 1)
                    run(dve, step)

        def up0(e, bank, xt):
            w = rw3[:, bass.ds(e, 1), :]
            for k in range(KC):
                ins = nc.tensor.matmul(bank[:, 0:DH], xt[:, k * P:(k + 1) * P], w[:, 0, k * DH:(k + 1) * DH],
                                       start=(k == 0), stop=(k == KC - 1))
            return ins

        def turn0(bank, h):
            nc.tensor.transpose(bank[:, 0:P], h[:, 0:P], IDN[:, :])
            return nc.tensor.transpose(bank[0:DHB, P:2 * P], h[:, P:DH], IDN[:, :])

        def act_turn0(e, bank, hT, done):
            nc.scalar.activation(hT[:, 0:P], bank[:, 0:P], ACT.Relu, bias=B1A[:, bass.ds(e, 1)])
            nc.scalar.activation(hT[0:DHB, P:2 * P], bank[0:DHB, P:2 * P], ACT.Relu, bias=B1B[:, bass.ds(e, 1)]).then_inc(done, 1)

        def down0(e, bank, hT):
            w = rw3[:, bass.ds(e, 1), :]
            nc.tensor.matmul(bank[:, 0:HID], hT[:, 0:P], w[:, 0, W2A:W2B], start=True, stop=False)
            return nc.tensor.matmul(bank[:, 0:HID], hT[0:DHB + 1, P:2 * P], w[0:DHB + 1, 0, W2B:EW0], start=False, stop=True)

        ones_set = sem("ones_set")
        with nc.Block() as block:
            @block.gpsimd
            def _(pool):
                for i in range(2):
                    nc.gpsimd.memset(TA[32:64, (8 + i) * HID + P:(9 + i) * HID], 1.0).then_inc(ones_set, 1)
                    pool.wait_ge(ones_set, i + 1)

        expert_block(0, 0, NT0, xs0, ys0, [(ld_ex, 16 * 6), (ld_ex2, 16 * 5)], scat0, 16 * NT * K0,
                     dict(E=E0, up=up0, turn=turn0, down=down0, act_mid=None, bias=True, act_turn=act_turn0,
                          dve_mid=lambda bank, h: nc.vector.tensor_copy(h[:, 0:DH], bank[:, 0:DH])))
        base = E1 * EW1
        o1 = base

        def cut1(n):
            nonlocal o1
            o1 += n
            return RW[:, o1 - n:o1]
        PB = cut1(TPB * H * NKEY).rearrange("p (j h n) -> p j h n", j=TPB, h=H)
        QB = [cut1(H * D) for _ in range(2)]
        QTB = [cut1(4 * P) for _ in range(2)]
        PTB = [cut1(4 * P) for _ in range(2)]
        AOB = [cut1(4 * P) for _ in range(2)]
        WR1 = cut1(6 * HID)
        YG = [XN[:, j * K0 * HID:(j + 1) * K0 * HID] for j in range(2)]
        NSW = [P, P + WIN]
        gates0 = v3(GATE[:, :], NT)
        rw13 = v3(RW[:, 0:base], E1)

        ld_e1, ld_w1 = sem("ld_experts1"), sem("ld_attn1")
        zero1 = sem("zero1_done")
        dve2p, dve2l, dve2e = sem("dve2_head"), sem("dve2_loop"), sem("dve2_tail")
        es_ok = sem("sink_exp")
        (qcs_ok, v_ok, v_half, q_ps, q_ev, qss, qpow, q_mul, q_rot, qn, t_ps, t_sb, s_ps, th, s_ev, e_sb, pn, csub, cexp, cn,
         pt_ps, pt_sb, pv_ps, ao_sb, opg, op_sb, idx_ok, comb) = (
            sem("a_" + n) for n in (
                "qc_copied", "values_copied", "values_half", "q_psum", "q_sbuf", "q_squares", "q_mean", "q_products", "q_rotated", "q_normed",
                "qT_psum", "qT_sbuf", "scores_psum", "tanh", "scores_read", "exp", "probs", "blocks_sub", "blocks_exp",
                "blocks_probs", "pT_psum", "pT_sbuf", "out_psum", "out_sbuf", "proj_group", "proj_read", "slots_tile",
                "combined"))
        gat = [sem(f"a_gathered{j}") for j in range(TPB)]
        NSTEP = NT + 3

        def wait(eng, s, n):
            if not isinstance(n, int) or n > 0:
                eng.wait_ge(s, n)

        def run_attention(eng, step):
            def outside(g, section):
                step(g, g % 2, lambda lag: (g - lag) // 2, lambda lag: 0 <= g - lag < NT, section)
            for g in range(-1, 4):
                outside(g, (0, 0))
            with eng.Fori(0, (NT - 4) // 2) as i:
                for c in range(4, 6):
                    step(i * 2 + c, c % 2, lambda lag: i + (c - lag) // 2, lambda lag: True, (1, i))
            for g in range(NT, NSTEP):
                outside(g, (2, 0))

        with nc.Block() as block:
            @block.sync
            def _(sp):
                for e in range(E1):
                    w = rw13[:, e, :]
                    for k in range(KC):
                        for m, n in enumerate(("L1_ffn_wi_0", "L1_ffn_wi_1")):
                            sp.dma_start(w[:, (2 * k + m) * MI:(2 * k + m + 1) * MI], a[n][e, k * P:(k + 1) * P, :]).then_inc(ld_e1, 16)
                        sp.dma_start(w[:, 2 * KC * MI + k * HID:2 * KC * MI + (k + 1) * HID],
                                     a["L1_ffn_wo"][e, k * P:(k + 1) * P, :]).then_inc(ld_e1, 16)
                for i, (n, r) in enumerate((("Wq", 0), ("Wq", P), ("Wk", 0), ("Wv", 0), ("Wo", 0), ("Wo", P))):
                    sp.dma_start(WR1[:, i * HID:(i + 1) * HID], a["L1_attn_" + n][r:r + P, :]).then_inc(ld_w1, 16)

            @block.gpsimd
            def _(pool):
                qcs = v3(QCS[:, :], TPB)
                vown = v3(VOWN[:, :], TPB)
                cos, sin = (v3(ROPE0[:, i * TPB * HR:(i + 1) * TPB * HR], TPB) for i in range(2))
                tmp = [v3(TA[:, i * H * HR:(i + 1) * H * HR], H) for i in range(4)]

                def step(g, j, batch, on, section):
                    ja = 1 - j
                    if on(2):
                        wait(pool, gat[ja], (batch(3) + 1) * (16 * K0))
                        nc.gpsimd.tensor_copy(IDX[:, :], SLOT[:, bass.ds((g - 2) * K0, K0)]).then_inc(idx_ok, 1)
                        pool.wait_ge(idx_ok, g - 1)
                        wait(pool, comb, g - 3)
                    if on(1):
                        wait(pool, pv_ps, (g - 2) * NPAIR)
                        nc.gpsimd.tensor_copy(vown[:, ja, :], VA[:, bass.ds((g - 1) * D, D)]).then_inc(v_half, 1)
                        if ja:
                            nc.gpsimd.tensor_copy(V2[:, :], V2A[:, bass.ds(batch(1) * D, D)]).then_inc(v_ok, 1)
                        else:
                            nc.gpsimd.tensor_copy(CKS[:, :], CK0[:, bass.ds(batch(1) * D, D)]).then_inc(v_ok, 1)
                    if on(-1):
                        wait(pool, q_ps, g * NG)
                        nc.gpsimd.tensor_copy(qcs[:, ja, :], QCT[:, bass.ds((g + 1) * P, P)]).then_inc(qcs_ok, 1)
                    if on(0):
                        pool.wait_ge(qss, g + 1)
                        wait(pool, qn, g)
                        nc.gpsimd.tensor_tensor(RR[:, :], RR[:, :], MHALF[:, 0:H], ALU.pow).then_inc(qpow, 1)
                        q3 = v3(QB[j], H)
                        x1, x2 = q3[:, :, 0:HR], q3[:, :, HR:ROPE]
                        c, s = (bc(t[:, j, :].unsqueeze(1), [P, H, HR]) for t in (cos, sin))
                        for i, (x, w) in enumerate(((x1, c), (x2, s), (x1, s), (x2, c))):
                            nc.gpsimd.tensor_tensor(tmp[i], x, w, ALU.mult).then_inc(q_mul, 1)
                        pool.wait_ge(q_mul, g * 4 + 4)
                        nc.gpsimd.tensor_tensor(x1, tmp[0], tmp[1], ALU.subtract).then_inc(q_rot, 1)
                        nc.gpsimd.tensor_tensor(x2, tmp[2], tmp[3], ALU.add).then_inc(q_rot, 1)
                    if on(2):
                        for k in range(K0):
                            nc.gpsimd.indirect_dma_start(YG[j][:, k * HID:(k + 1) * HID], None, ys0,
                                                         bass.IndirectOffsetOnAxis(ap=IDX[:, k:k + 1], axis=0)).then_inc(gat[j], 16)
                run_attention(pool, step)

            @block.tensor
            def _(pe):
                wq3 = v3(WQ[:, :], NG)
                qcs = v3(QCS[:, :], TPB)
                vown = v3(VOWN[:, :], TPB)

                def step(g, j, batch, on, section):
                    ja = 1 - j

                    def queries(k):
                        if on(-1):
                            pe.wait_ge(qcs_ok, g + 2)
                            wait(pe, q_ev, (g + 1) * NG + k)
                            nc.tensor.matmul(ps[0][:, :], qcs[:, ja, :], wq3[:, k, :], start=True, stop=True).then_inc(q_ps, 1)

                    def turn_queries(k):
                        if on(1):
                            pe.wait_ge(qn, g)
                            wait(pe, t_sb, (g - 1) * NG + k)
                            q3 = v3(QB[ja], H)
                            for h in range(4):
                                ins = nc.tensor.transpose(ps[1][:, h * P:(h + 1) * P], q3[:, 4 * k + h, :], IDN[:, :])
                            ins.then_inc(t_ps, 1)

                    def scores(p):
                        if on(1):
                            pe.wait_ge(t_sb, (g - 1) * NG + (p // 2 + 1))
                            wait(pe, s_ev, (g - 1) * NPAIR + (p - 1))
                            n = NSW[ja] + NB
                            keys = KCAT[:, bass.ds(batch(1) * KROW + (P + NB if ja else 0), n)]
                            for i in range(2):
                                h = 2 * p + i
                                ins = nc.tensor.matmul(ps[2 + p % 2][:, i * NKEY:i * NKEY + n],
                                                       QTB[h // 4 % 2][:, h % 4 * P:(h % 4 + 1) * P], keys, start=True, stop=True)
                            ins.then_inc(s_ps, 1)

                    def turn_probs(p):
                        if on(2):
                            pe.wait_ge(pn, (g - 2) * NPAIR + (p + 1))
                            pe.wait_ge(cn, (g - 2) * 2 + (p // 4 + 1))
                            wait(pe, pt_sb, (g - 2) * NPAIR + (p - 1))
                            n = NSW[j] + NB
                            for i in range(2):
                                nc.tensor.transpose(ps[4 + p % 2][:, i * P:(i + 1) * P], PB[:, j, 2 * p + i, 0:P], IDN[:, :])
                                ins = nc.tensor.transpose(ps[4 + p % 2][0:n - P, (2 + i) * P:(3 + i) * P],
                                                          PB[:, j, 2 * p + i, P:n], IDN[:, :])
                            ins.then_inc(pt_ps, 1)

                    def values(p):
                        if on(2):
                            pe.wait_ge(v_ok, g - 1)
                            pe.wait_ge(v_half, g - 1)
                            pe.wait_ge(pt_sb, (g - 2) * NPAIR + (p + 1))
                            if p % 2 == 0:
                                wait(pe, ao_sb, (g - 2) * NG + p // 2)
                            n = NSW[j] + NB - P
                            for i in range(2):
                                o = ps[6][:, (2 * p + i) % 4 * P:((2 * p + i) % 4 + 1) * P]
                                nc.tensor.matmul(o, vown[:, j, :], PTB[p % 2][:, i * P:(i + 1) * P], start=True, stop=False)
                                ins = nc.tensor.matmul(o, V2[:, :] if j else CKS[:, :], PTB[p % 2][0:n, (2 + i) * P:(3 + i) * P],
                                                       start=False, stop=True)
                            ins.then_inc(pv_ps, 1)

                    def project(k):
                        if on(2):
                            pe.wait_ge(ao_sb, (g - 2) * NG + (k + 1))
                            if k == 0:
                                wait(pe, op_sb, g - 2)
                            for h in range(4):
                                ins = nc.tensor.matmul(ps[7][:, 0:HID], AOB[k % 2][:, h * P:(h + 1) * P], wc3[:, 4 * k + h, :],
                                                       start=(k + h == 0), stop=(k == NG - 1 and h == 3))
                            ins.then_inc(opg, 1)

                    turn_queries(0)
                    for p in range(NPAIR):
                        if p % 2 == 0 and p // 2 + 1 < NG:
                            turn_queries(p // 2 + 1)
                        scores(p)
                        turn_probs(p)
                        if p >= NPAIR - NG:
                            queries(p - (NPAIR - NG))
                        if p >= 1:
                            values(p - 1)
                        if p >= 3 and p % 2:
                            project((p - 3) // 2)
                    values(NPAIR - 1)
                    project(NG - 1)
                run_attention(pe, step)

            @block.scalar
            def _(act):
                for i in range(NT1 // 4):
                    act.dma_start(xs1[i * 4 * P:(i + 1) * 4 * P, :].rearrange("(c p) d -> p c d", p=P),
                                  bc(ZERO[:, :].unsqueeze(1), [P, 4, HID])).then_inc(zero1, 16)
                nc.scalar.activation(SINK[:, 3 * H:], SINK[:, 2 * H:3 * H], ACT.Exp).then_inc(es_ok, 1)

                def step(g, j, batch, on, section):
                    ja = 1 - j
                    nsw = NSW[ja]

                    def queries(k):
                        if on(-1):
                            act.wait_ge(q_ps, (g + 1) * NG + (k + 1))
                            wait(act, t_ps, g * NG)
                            nc.scalar.activation(QB[ja][:, k * 512:(k + 1) * 512], ps[0][:, :], ACT.Copy).then_inc(q_ev, 1)

                    def probs(p):
                        if on(1):
                            act.wait_ge(s_ps, (g - 1) * NPAIR + (p + 1))
                            wait(act, pt_ps, (g - 3) * NPAIR + (p + 1))
                            sc = v3(ps[2 + p % 2][:, 0:2 * NKEY], 2)
                            pb = PB[:, ja, 2 * p:2 * p + 2, :]
                            nc.scalar.activation(pb[:, :, 0:nsw], sc[:, :, 0:nsw], ACT.Tanh, scale=SCALE / CAP).then_inc(th, 1)
                            nc.scalar.activation(pb[:, :, nsw:nsw + NB], sc[:, :, nsw:nsw + NB], ACT.Copy, scale=SCALE).then_inc(s_ev, 1)
                            act.wait_ge(th, (g - 1) * NPAIR + (p + 1))
                            for i in range(2):
                                h = 2 * p + i
                                ins = nc.scalar.activation(pb[:, i, 0:nsw], pb[:, i, 0:nsw], ACT.Exp, scale=CAP, bias=SINK[:, H + h:H + h + 1])
                            ins.then_inc(e_sb, 1)

                    def probs_T(p):
                        if on(2):
                            act.wait_ge(pt_ps, (g - 2) * NPAIR + (p + 1))
                            wait(act, pv_ps, (g - 2) * NPAIR + (p - 1))
                            n = NSW[j] + NB - P
                            nc.scalar.activation(PTB[p % 2][:, 0:2 * P], ps[4 + p % 2][:, 0:2 * P], ACT.Copy)
                            nc.scalar.activation(PTB[p % 2][0:n, 2 * P:], ps[4 + p % 2][0:n, 2 * P:], ACT.Copy).then_inc(pt_sb, 1)

                    def outs(k):
                        if on(2):
                            act.wait_ge(pv_ps, (g - 2) * NPAIR + (2 * k + 2))
                            wait(act, opg, (g - 2) * NG + (k - 1))
                            nc.scalar.activation(AOB[k % 2], ps[6][:, :], ACT.Copy).then_inc(ao_sb, 1)

                    def blocks(half):
                        if on(1):
                            act.wait_ge(csub, (g - 1) * 2 + (half + 1))
                            cb = PB[:, ja, 8 * half:8 * half + 8, nsw:nsw + NB]
                            nc.scalar.activation(cb, cb, ACT.Exp)
                            nc.scalar.activation(CM[:, 24:32], CM[:, 16:24], ACT.Exp).then_inc(cexp, 1)

                    for p in range(NPAIR):
                        probs(p)
                        probs_T(p)
                        if p >= NPAIR - NG:
                            queries(p - (NPAIR - NG))
                        if p >= 2 and p % 2 == 0:
                            outs(p // 2 - 1)
                        if p == 6:
                            blocks(0)
                    outs(NG - 1)
                    blocks(1)
                run_attention(act, step)
                act.wait_ge(zero1, 16 * (NT1 // 4))

            @block.vector
            def _(dve):
                PER_STEP = NPAIR * 4 + 2 * 6 + H + (K0 - 1)
                sections = {}

                def step(g, j, batch, on, section):
                    kind, i = section
                    if kind not in sections:
                        sections[kind] = Steps(dve, (dve2p, dve2l, dve2e)[kind], i * (2 * PER_STEP) if kind == 1 else 0)
                    st = sections[kind]
                    ja = 1 - j
                    nsw = NSW[ja]

                    def queries_T(k):
                        if on(1):
                            dve.wait_ge(t_ps, (g - 1) * NG + (k + 1))
                            wait(dve, s_ps, (g - 1) * NPAIR + (2 * k - 2))
                            nc.vector.tensor_copy(QTB[k % 2], ps[1][:, :]).then_inc(t_sb, 1)

                    def norm(p):
                        if on(1):
                            dve.wait_ge(e_sb, (g - 1) * NPAIR + (p + 1))
                            hs = slice(2 * p, 2 * p + 2)
                            for h in range(2 * p, 2 * p + 2):
                                pb = PB[:, ja, h, 0:nsw]
                                st(nc.vector.scalar_tensor_tensor(out=pb, in0=pb, scalar=1.0, in1=WINDOW[:, 0:nsw], op0=ALU.mult,
                                                                  op1=ALU.mult, accum_out=LSUM[:, h:h + 1]))
                            st.wait()
                            st.link(nc.vector.tensor_tensor(LSUM[:, H + 2 * p:H + 2 * p + 2], LSUM[:, hs],
                                                            SINK[:, 3 * H + 2 * p:3 * H + 2 * p + 2], ALU.add))
                            st.link(nc.vector.reciprocal(LSUM[:, 2 * H + 2 * p:2 * H + 2 * p + 2], LSUM[:, H + 2 * p:H + 2 * p + 2]))
                            for h in range(2 * p, 2 * p + 2):
                                pb = PB[:, ja, h, 0:nsw]
                                ins = nc.vector.tensor_scalar(pb, pb, LSUM[:, 2 * H + h:2 * H + h + 1], None, ALU.mult)
                            ins.then_inc(pn, 1)

                    def blocks_sub(half):
                        if on(1):
                            dve.wait_ge(s_ev, (g - 1) * NPAIR + (4 * half + 4))
                            cb = PB[:, ja, 8 * half:8 * half + 8, nsw:nsw + NB]
                            sk = SINK[:, 8 * half:8 * half + 8]
                            st.link(nc.vector.tensor_tensor(cb, cb, bc(v3(BLOCKS[:, :], TPB)[:, ja, :].unsqueeze(1), [P, 8, NB]), ALU.add))
                            st.link(nc.vector.reduce_max(CM[:, 0:8], cb, AX))
                            st.link(nc.vector.tensor_tensor(CM[:, 8:16], CM[:, 0:8], sk, ALU.max))
                            nc.vector.tensor_tensor(CM[:, 16:24], sk, CM[:, 8:16], ALU.subtract)
                            nc.vector.tensor_tensor(cb, cb, bc(CM[:, 8:16].unsqueeze(2), [P, 8, NB]), ALU.subtract).then_inc(csub, 1)

                    def blocks_norm(half):
                        if on(1):
                            dve.wait_ge(cexp, (g - 1) * 2 + (half + 1))
                            cb = PB[:, ja, 8 * half:8 * half + 8, nsw:nsw + NB]
                            st.link(nc.vector.reduce_sum(CM[:, 32:40], cb, AX))
                            st.link(nc.vector.tensor_tensor(CM[:, 40:48], CM[:, 32:40], CM[:, 24:32], ALU.add))
                            st.link(nc.vector.reciprocal(CM[:, 48:56], CM[:, 40:48]))
                            nc.vector.tensor_tensor(cb, cb, bc(CM[:, 48:56].unsqueeze(2), [P, 8, NB]), ALU.mult).then_inc(cn, 1)

                    def squares():
                        if on(0):
                            dve.wait_ge(q_ev, g * NG + NG)
                            wait(dve, qn, g)
                            q3 = v3(QB[j], H)
                            for h in range(H):
                                ins = nc.vector.scalar_tensor_tensor(out=TA[:, h * D:(h + 1) * D], in0=q3[:, h, :], scalar=1.0,
                                                                     in1=q3[:, h, :], op0=ALU.mult, op1=ALU.mult, accum_out=SSQ[:, h:h + 1])
                                st(ins)
                            st.wait()
                            nc.vector.tensor_scalar(RR[:, :], SSQ[:, :], 1.0 / D, RMS_EPS, ALU.mult, ALU.add).then_inc(qss, 1)

                    def query_norm():
                        if on(0):
                            dve.wait_ge(qpow, g + 1)
                            dve.wait_ge(q_rot, g * 2 + 2)
                            q3 = v3(QB[j], H)
                            nc.vector.tensor_tensor(q3, q3, bc(RR[:, :].unsqueeze(2), [P, H, D]), ALU.mult).then_inc(qn, 1)

                    def take_out():
                        if on(3):
                            x = X[:, bass.ds((g - 3) * HID, HID)]
                            dve.wait_ge(opg, (g - 3) * NG + NG)
                            nc.vector.tensor_tensor(x, ps[7][:, 0:HID], x, ALU.add).then_inc(op_sb, 1)

                    def combine():
                        if on(3):
                            x = X[:, bass.ds((g - 3) * HID, HID)]
                            dve.wait_ge(op_sb, g - 2)
                            dve.wait_ge(gat[ja], (batch(3) + 1) * (16 * K0))
                            for k in range(K0):
                                ins = nc.vector.scalar_tensor_tensor(out=x, in0=YG[ja][:, k * HID:(k + 1) * HID],
                                                                     scalar=GATE[:, bass.ds((g - 3) * K0 + k, 1)], in1=x,
                                                                     op0=ALU.mult, op1=ALU.add)
                                if k < K0 - 1:
                                    st.link(ins)
                            ins.then_inc(comb, 1)

                    queries_T(0)
                    squares()
                    for p in range(NPAIR):
                        if p % 2 == 0 and p // 2 + 1 < NG:
                            queries_T(p // 2 + 1)
                        if p == 1:
                            take_out()
                        if p >= 1:
                            norm(p - 1)
                        if p == 4:
                            combine()
                        if p == 6:
                            query_norm()
                        if p == 5:
                            blocks_sub(0)
                        if p == 7:
                            blocks_norm(0)
                    norm(NPAIR - 1)
                    blocks_sub(1)
                    blocks_norm(1)
                    if kind == 1 and j == 1:
                        assert st.n == 2 * PER_STEP, (st.n, PER_STEP)
                dve.wait_ge(es_ok, 1)
                run_attention(dve, step)

        o1 = base
        NHK = H1 + HKV
        QKV = cut1(NT * 2 * HID)
        WT1 = cut1(KC * 2 * HID)
        WOT = cut1(KC * HID)
        TMPL = cut1(NT * NHK * D1)
        VOUT = cut1(NT * HID)
        FEAT = cut1(NT * NHK * D1)
        o1 = E1 * EW1 + 13824
        BQKV, BO, RBD = TA[:, 0:2 * HID], TA[:, 2 * HID:3 * HID], TA[:, 3 * HID:3 * HID + HKV * R1]
        SSN = TA[:, 1024:1024 + NT * NHK]
        DT = [TA[:, 1536 + i * 3 * P:1536 + (i + 1) * 3 * P] for i in range(2)]
        OT = [TA[:, 2304 + i * HID:2304 + (i + 1) * HID] for i in range(2)]
        RBT = TA[0:HKV * R1, 2816:2816 + P]
        MEET = xnT[:, 0:NT * H1 * HKV]
        VIN = WC[:, 0:NT * HID]
        hst, hld = sem("b_heads_stored"), [sem(f"b_heads_loaded{b}") for b in range(B)]
        qkv3 = v3(QKV, NT)

        ld_s1, ld_r1 = sem("ld_small1"), sem("ld_rand1")
        (rb_zero, c1_set, dve3, stats1, var1, rstd1, xn1, x1t_ps, x1t_sb, lg1_ps, wt1_ps, wt1_sb, qkv_ps, qkv_sb,
         chosen1, rank1, gsub1, gexp1, slots1, scat1, ssum, sspow, d_ok, dT_ps, dT_sb, u_ps, u_ok, sin_ok, o_ok,
         oT_ps, oT_sb, ao_ps, ao_rd) = (
            sem("b_" + n) for n in (
                "rand_zero", "const", "dve", "stats", "var", "rstd", "xn", "xT_psum", "xT_sbuf", "logits", "wT_psum", "wT_sbuf",
                "qkv_psum", "qkv_sbuf", "chosen", "rank", "gates_sub", "gates_exp", "slots", "scatter", "squares",
                "norms", "differences", "dT_psum", "dT_sbuf", "angles_psum", "angles", "cosines", "outs", "oT_psum", "oT_sbuf",
                "proj", "proj_read"))
        with nc.Block() as block:
            @block.sync
            def _(sp):
                sp.dma_start(v3(RTW[:, 0:KC * E1], KC), a["L1_ffn_gate_kernel"].rearrange("(k p) e -> p k e", p=P)).then_inc(ld_s1, 16)
                for n, lo, w in (("bq", 0, HID), ("bk", HID, P), ("bv", HID + P, P)):
                    sp.dma_start(BQKV[:, lo:lo + w], a["L1_attn_" + n].partition_broadcast(P)).then_inc(ld_s1, 16)
                sp.dma_start(BO, a["L1_attn_bo"].partition_broadcast(P)).then_inc(ld_s1, 16)
                sp.wait_ge(rb_zero, 1)
                for h in range(HKV):
                    sp.dma_start(RBT[h * R1:(h + 1) * R1, h * D1:(h + 1) * D1], a["L1_attn_rand_matrix"]).then_inc(ld_r1, 16)
                for b in range(B):
                    for j in range(TPB):
                        t = b * TPB + j
                        sp.wait_ge(o_ok, t + 1)
                        sp.dma_start(heads1[t * P:(t + 1) * P, :], VOUT[:, t * HID:(t + 1) * HID]).then_inc(hst, 16)
                    sp.wait_ge(hst, 16 * TPB * (b + 1))
                    for j in range(TPB):
                        t = b * TPB + j
                        hh = H1 // TPB
                        src = heads1[b * S:(b + 1) * S, j * hh * D1:(j + 1) * hh * D1].rearrange("(g l) (h d) -> h g l d", l=H1, d=D1)
                        sp.dma_start(VIN[:, t * HID:(t + 1) * HID].rearrange("p (l d) -> p l d", l=H1), src).then_inc(hld[b], 16)
                sp.wait_ge(ld_s1, 16 * 5)
                sp.wait_ge(ld_r1, 16 * HKV)

            @block.gpsimd
            def _(pool):
                nc.gpsimd.memset(RBT, 0.0).then_inc(rb_zero, 1)
                layernorm_pool(pool, stats1, var1, rstd1)
                pool.wait_ge(slots1, 1)
                for t in range(NT):
                    for k in range(K1):
                        nc.gpsimd.indirect_dma_start(
                            xs1, bass.IndirectOffsetOnAxis(ap=SLOT[:, t * K1 + k:t * K1 + k + 1], axis=0),
                            xn3[:, t, :], None).then_inc(scat1, 16)
                pool.wait_ge(ssum, 1)
                nc.gpsimd.tensor_tensor(SSN, SSN, MHALF[:, :], ALU.pow).then_inc(sspow, 1)

            @block.scalar
            def _(act):
                act.wait_ge(wt1_ps, 1)
                for k in range(KC):
                    nc.scalar.activation(WT1[:, k * 2 * HID:(k + 1) * 2 * HID], ps[2 + k][:, :], ACT.Copy).then_inc(wt1_sb, 1)
                nc.scalar.activation(WOT, ps[4][:, :], ACT.Copy).then_inc(wt1_sb, 1)
                nc.scalar.activation(RBD, ps[5][:, 0:HKV * R1], ACT.Copy).then_inc(wt1_sb, 1)
                for t in range(NT):
                    act.wait_ge(x1t_ps, t + 1)
                    nc.scalar.activation(xnT3[:, :, t * P:(t + 1) * P], v3(ps[t % 2][:, 0:HID], KC), ACT.Copy).then_inc(x1t_sb, 1)
                act.wait_ge(gsub1, 1)
                nc.scalar.activation(GATE[:, 0:NT * K1], GATE[:, 0:NT * K1], ACT.Exp).then_inc(gexp1, 1)
                for t in range(NT):
                    act.wait_ge(dT_ps, t + 1)
                    wait(act, u_ps, t - 1)
                    nc.scalar.activation(DT[t % 2], ps[t % 2][:, 0:3 * P], ACT.Copy).then_inc(dT_sb, 1)
                act.wait_ge(u_ok, 1)
                nc.scalar.activation(FEAT, FEAT, ACT.Sin, scale=2 * 3.1415925).then_inc(sin_ok, 1)
                for t in range(NT):
                    act.wait_ge(oT_ps, t + 1)
                    wait(act, ao_ps, t - 1)
                    nc.scalar.activation(OT[t % 2], ps[4 + t % 2][:, 0:HID], ACT.Copy).then_inc(oT_sb, 1)

            @block.vector
            def _(dve):
                st = Steps(dve, dve3)
                layernorm_dve(dve, st, stats1, rstd1, xn1)
                dve.wait_ge(lg1_ps, 1)
                st.link(nc.vector.tensor_copy(LOGIT[:, 0:NT * E1], ps[2][:, 0:NT * E1]))
                route_dve(dve, st, E1, K1, chosen1, gsub1)
                route_dve_slots(dve, st, E1, K1, NT1, ps[3], rank1, gexp1, slots1)
                dve.wait_ge(ld_s1, 16 * 5)
                for t in range(NT):
                    dve.wait_ge(qkv_ps, t + 1)
                    nc.vector.tensor_tensor(qkv3[:, t, :], ps[6 + t % 2][:, :], BQKV, ALU.add).then_inc(qkv_sb, 1)
                dve.wait_ge(qkv_sb, NT)
                hd = D1 // 2
                q5 = QKV.rearrange("p (b j n) -> p b j n", b=B, j=TPB)[:, :, :, 0:NHK * D1]
                cos, sin = (v3(ROPE1[:, i * TPB * hd:(i + 1) * TPB * hd], TPB) for i in range(2))
                nt4 = NHK * hd
                for t in range(NT):
                    jt = t % TPB
                    q = v3(qkv3[:, t, 0:NHK * D1], NHK)
                    y1, y2 = q[:, :, 0:hd], q[:, :, hd:]
                    tmp = [v3(TMPL[:, i * nt4:(i + 1) * nt4], NHK) for i in range(4 * (t % 4), 4 * (t % 4) + 4)]
                    c, s = (bc(w[:, jt, :].unsqueeze(1), [P, NHK, hd]) for w in (cos, sin))
                    for i, (y, w) in enumerate(((y1, c), (y2, s), (y1, s), (y2, c))):
                        st(nc.vector.tensor_tensor(tmp[i], y, w, ALU.mult))
                    st.wait()
                    st(nc.vector.tensor_tensor(y1, tmp[0], tmp[1], ALU.subtract))
                    st(nc.vector.tensor_tensor(y2, tmp[3], tmp[2], ALU.add))
                st.wait()
                tm3 = v3(TMPL, NT)
                st.link(nc.vector.tensor_tensor(tm3, qkv3[:, :, 0:NHK * D1], qkv3[:, :, 0:NHK * D1], ALU.mult))
                st.link(nc.vector.tensor_reduce(SSN, TMPL.rearrange("p (n d) -> p n d", d=D1), AX, ALU.add))
                nc.vector.tensor_scalar(SSN, SSN, 1e-12, None, ALU.max).then_inc(ssum, 1)
                dve.wait_ge(sspow, 1)
                for t in range(NT):
                    q = v3(qkv3[:, t, 0:NHK * D1], NHK)
                    nc.vector.tensor_tensor(q, q, bc(SSN[:, t * NHK:(t + 1) * NHK].unsqueeze(2), [P, NHK, D1]), ALU.mult).then_inc(d_ok, 1)
                fr = TMPL.rearrange("p (t n f) -> p t n f", t=NT, n=NHK)
                for i in range(NT // 2):
                    dve.wait_ge(u_ps, 2 * i + 2)
                    u = ps[2 + i][:, 0:2 * NHK * R1].rearrange("p (t n f) -> p t n f", t=2, n=NHK)
                    for half, turn in ((0, 0.0), (1, 0.25)):
                        st(nc.vector.tensor_scalar(fr[:, 2 * i:2 * i + 2, :, half * R1:(half + 1) * R1], u, 1.0 / (2 * np.pi), turn,
                                                   ALU.mult, ALU.add))
                st.wait()
                st.link(nc.vector.tensor_scalar(FEAT, TMPL, MAGIC, -MAGIC, ALU.add, ALU.add))
                st.link(nc.vector.tensor_tensor(FEAT, TMPL, FEAT, ALU.subtract))
                nc.vector.tensor_scalar(FEAT, FEAT, 0.5, -0.5, ALU.min, ALU.max).then_inc(u_ok, 1)
                dve.wait_ge(sin_ok, 1)
                ft = FEAT.rearrange("p (t n f) -> p t n f", t=NT, n=NHK)
                pr = TMPL[:, 0:H1 * HKV * D1]
                prf = pr.rearrange("p (h k f) -> p h k f", h=H1, k=HKV)
                prd = pr.rearrange("p (h d k) -> p h d k", h=H1, d=D1)
                for t in range(NT):
                    w = MEET[:, t * H1 * HKV:(t + 1) * H1 * HKV].rearrange("p (h k) -> p h k", h=H1)
                    vd = v3(qkv3[:, t, HID + P:], HKV).rearrange("p k d -> p d k")
                    st.link(nc.vector.tensor_tensor(prf, bc(ft[:, t, 0:H1].unsqueeze(2), [P, H1, HKV, D1]),
                                                    bc(ft[:, t, H1:].unsqueeze(1), [P, H1, HKV, D1]), ALU.mult))
                    st.link(nc.vector.tensor_reduce(w, prf, AX, ALU.add))
                    st.link(nc.vector.tensor_scalar(w, w, float(H1 // HKV) / D1, None, ALU.mult))
                    st.link(nc.vector.tensor_tensor(prd, bc(w.unsqueeze(2), [P, H1, D1, HKV]),
                                                    bc(vd.unsqueeze(1), [P, H1, D1, HKV]), ALU.mult))
                    nc.vector.tensor_reduce(v3(VOUT[:, t * HID:(t + 1) * HID], H1), prd, AX, ALU.add).then_inc(o_ok, 1)
                    dve.wait_ge(o_ok, t + 1)
                for t in range(NT):
                    st.link(nc.vector.tensor_tensor(x3[:, t, :], x3[:, t, :], BO, ALU.add))
                    dve.wait_ge(ao_ps, t + 1)
                    nc.vector.tensor_tensor(x3[:, t, :], ps[6 + t % 2][:, 0:HID], x3[:, t, :], ALU.add).then_inc(ao_rd, 1)

            @block.tensor
            def _(pe):
                pe.wait_ge(ld_w1, 16 * 6)
                for k in range(KC):
                    for i in range(4):
                        nc.tensor.transpose(ps[2 + k][:, i * P:(i + 1) * P], WR1[:, i * HID + k * P:i * HID + (k + 1) * P], IDN[:, :])
                for k in range(KC):
                    for i in range(2):
                        nc.tensor.transpose(ps[4][:, (2 * k + i) * P:(2 * k + i + 1) * P],
                                                  WR1[:, (4 + i) * HID + k * P:(4 + i) * HID + (k + 1) * P], IDN[:, :])
                pe.wait_ge(ld_r1, 16 * HKV)
                nc.tensor.transpose(ps[5][:, 0:HKV * R1], RBT, IDN[0:HKV * R1, 0:HKV * R1]).then_inc(wt1_ps, 1)
                for t in range(NT):
                    pe.wait_ge(xn1, t + 1)
                    wait(pe, x1t_sb, t - 1)
                    for k in range(KC):
                        ins = nc.tensor.transpose(ps[t % 2][:, k * P:(k + 1) * P], xn3[:, t, k * P:(k + 1) * P], IDN[:, :])
                    ins.then_inc(x1t_ps, 1)
                pe.wait_ge(x1t_sb, NT)
                pe.wait_ge(ld_s1, 16 * 5)
                pe.wait_ge(wt1_sb, 4)
                for t in range(NT):
                    for k in range(KC):
                        ins = nc.tensor.matmul(ps[2][:, t * E1:(t + 1) * E1], xnT3[:, k, t * P:(t + 1) * P],
                                               RTW[:, k * E1:(k + 1) * E1], start=(k == 0), stop=(k == KC - 1))
                ins.then_inc(lg1_ps, 1)

                def qkv(t):
                    wait(pe, qkv_sb, t - 1)
                    for k in range(KC):
                        ins = nc.tensor.matmul(ps[6 + t % 2][:, :], xnT3[:, k, t * P:(t + 1) * P],
                                               WT1[:, k * 2 * HID:(k + 1) * 2 * HID], start=(k == 0), stop=(k == KC - 1))
                    ins.then_inc(qkv_ps, 1)
                qkv(0)
                qkv(1)
                rank_pe(pe, E1, ps[3], chosen1, rank1)
                for t in range(2, NT):
                    qkv(t)
                pe.wait_ge(slots1, 2)

                def angles(t):
                    pe.wait_ge(dT_sb, t + 1)
                    for c in range(3):
                        lo = t % 2 * NHK * R1 + c * HKV * R1
                        ins = nc.tensor.matmul(ps[2 + t // 2][:, lo:lo + HKV * R1], DT[t % 2][:, c * P:(c + 1) * P], RBD,
                                               start=True, stop=True)
                    ins.then_inc(u_ps, 1)
                for t in range(NT):
                    pe.wait_ge(d_ok, t + 1)
                    wait(pe, dT_sb, t - 1)
                    for c in range(3):
                        ins = nc.tensor.transpose(ps[t % 2][:, c * P:(c + 1) * P], qkv3[:, t, c * P:(c + 1) * P], IDN[:, :])
                    ins.then_inc(dT_ps, 1)
                    if t:
                        angles(t - 1)
                angles(NT - 1)

                def project1(t):
                    pe.wait_ge(oT_sb, t + 1)
                    wait(pe, ao_rd, t - 1)
                    for k in range(KC):
                        ins = nc.tensor.matmul(ps[6 + t % 2][:, 0:HID], OT[t % 2][:, k * P:(k + 1) * P], WOT[:, k * HID:(k + 1) * HID],
                                               start=(k == 0), stop=(k == KC - 1))
                    ins.then_inc(ao_ps, 1)
                for t in range(NT):
                    pe.wait_ge(hld[t // TPB], 16 * TPB)
                    wait(pe, oT_sb, t - 1)
                    for k in range(KC):
                        ins = nc.tensor.transpose(ps[4 + t % 2][:, k * P:(k + 1) * P], VIN[:, t * HID + k * P:t * HID + (k + 1) * P], IDN[:, :])
                    ins.then_inc(oT_ps, 1)
                    if t:
                        project1(t - 1)
                project1(NT - 1)

        def up1(e, bank, xt):
            w = rw13[:, bass.ds(e, 1), :]
            for k in range(KC):
                ins = nc.tensor.matmul(bank[:, :], xt[:, k * P:(k + 1) * P], w[:, 0, k * 2 * MI:(k + 1) * 2 * MI],
                                       start=(k == 0), stop=(k == KC - 1))
            return ins

        def turn1(bank, h):
            for k in range(KC):
                ins = nc.tensor.transpose(bank[:, k * P:(k + 1) * P], h[:, k * P:(k + 1) * P], IDN[:, :])
            return ins

        def act_turn1(e, bank, hT, done):
            nc.scalar.activation(hT, bank[:, 0:MI], ACT.Copy).then_inc(done, 1)

        def down1(e, bank, hT):
            w = rw13[:, bass.ds(e, 1), :]
            for k in range(KC):
                ins = nc.tensor.matmul(bank[:, 0:HID], hT[:, k * P:(k + 1) * P],
                                       w[:, 0, 2 * KC * MI + k * HID:2 * KC * MI + (k + 1) * HID], start=(k == 0), stop=(k == KC - 1))
            return ins

        expert_block(NT0, 0, NT1, xs1, ys1, [(ld_e1, 16 * 3 * KC * E1)], scat1, 16 * NT * K1,
                     dict(E=E1, up=up1, turn=turn1, down=down1, bias=False, act_turn=act_turn1,
                          act_mid=lambda bank, h: nc.scalar.activation(h, bank[:, 0:MI], ACT.Silu),
                          dve_mid=lambda bank, h: nc.vector.tensor_tensor(h, bank[:, MI:2 * MI], h, ALU.mult)))

        fgat = [sem(f"f_gathered{b}") for b in range(B)]
        f_ok, f_st, fdve = sem("f_combined"), sem("f_stored"), sem("f_dve")
        with nc.Block() as block:
            @block.gpsimd
            def _(pool):
                for t in range(NT):
                    for k in range(K1):
                        i = t * K1 + k
                        nc.gpsimd.indirect_dma_start(XN[:, i * HID:(i + 1) * HID], None, ys1,
                                                     bass.IndirectOffsetOnAxis(ap=SLOT[:, i:i + 1], axis=0)).then_inc(fgat[t // TPB], 16)

            @block.vector
            def _(dve):
                st = Steps(dve, fdve)
                for t in range(NT):
                    dve.wait_ge(fgat[t // TPB], 16 * TPB * K1)
                    for k in range(K1):
                        i = t * K1 + k
                        ins = nc.vector.scalar_tensor_tensor(out=x3[:, t, :], in0=XN[:, i * HID:(i + 1) * HID], scalar=GATE[:, i:i + 1],
                                                             in1=x3[:, t, :], op0=ALU.mult, op1=ALU.add)
                        if k < K1 - 1:
                            st.link(ins)
                    ins.then_inc(f_ok, 1)

            @block.sync
            def _(sp):
                rows = out.rearrange("b (j p) d -> (b j) p d", p=P)
                for t in range(NT):
                    sp.wait_ge(f_ok, t + 1)
                    sp.dma_start(rows[t], x3[:, t, :]).then_inc(f_st, 16)
                sp.wait_ge(f_st, 16 * NT)


INPUTS = ["L0_attn_h", "L0_attn_Wq_c", "L0_attn_Wq_up", "L0_attn_Wk", "L0_attn_Wv", "L0_attn_W_comp", "L0_attn_q_norm_w",
          "L0_attn_k_norm_w", "L0_attn_sink", "L0_attn_Wg", "L0_attn_Wo", "L0_ffn_sw1", "L0_ffn_sb1", "L0_ffn_sw2", "L0_ffn_sb2",
          "L0_ffn_rw1", "L0_ffn_rb1", "L0_ffn_rw2", "L0_ffn_rb2", "L0_ffn_router_w", "L0_ffn_router_b", "L1_attn_Wq", "L1_attn_bq",
          "L1_attn_Wk", "L1_attn_bk", "L1_attn_Wv", "L1_attn_bv", "L1_attn_Wo", "L1_attn_bo", "L1_attn_rand_matrix",
          "L1_ffn_gate_kernel", "L1_ffn_wi_0", "L1_ffn_wi_1", "L1_ffn_wo"]


def kernel(**inputs):
    import concourse.bacc as bacc
    from concourse.bass_utils import run_bass_kernel_spmd

    nc = bacc.Bacc("TRN2", target_bir_lowering=False, num_devices=1)
    arrays = {n: np.ascontiguousarray(inputs[n]) for n in INPUTS}
    arrays.update(constants())
    args = {n: nc.dram_tensor(n, v.shape, mybir.dt.from_np(v.dtype), kind="ExternalInput").ap() for n, v in arrays.items()}
    out = nc.dram_tensor("out", (B, S, HID), F32, kind="ExternalOutput").ap()
    build(nc, args, out)
    r = run_bass_kernel_spmd(nc, [arrays], core_ids=[0])
    return r.results[0]["out"]
```

```python
from contextlib import ExitStack

import numpy as np

import concourse.bass as bass
from concourse import mybir

F32 = mybir.dt.float32
BF16 = mybir.dt.bfloat16
I32 = mybir.dt.int32
U32 = mybir.dt.uint32
ALU = mybir.AluOpType
ACT = mybir.ActivationFunctionType
AX = mybir.AxisListType.X

P = 128
B, S, HID = 4, 256, 256
T = B * S
NT = T // P
KC = HID // P
TPB = S // P
LN_EPS, RMS_EPS = 1e-5, 1e-6

H, D, QC, M, ROPE, WIN, CAP = 16, 128, 64, 16, 64, 64, 50.0
HR = ROPE // 2
NB = S // M
SCALE = 1.0 / float(np.sqrt(np.float32(D)))
NKEY = P + WIN + NB
KROW = P + NB + NKEY
NPAIR = H // 2
NG = H // 4

E0, K0, DH, NSH = 32, 6, 176, 2
DHB = DH - P
W1A, W1B, W2A, W2B, EW0 = 0, DH, 2 * DH, 2 * DH + HID, 2 * DH + 2 * HID
NT0 = 2 * ((T * K0 // P + E0 + 1) // 2)

H1, D1, HKV, E1, K1, MI = 16, 16, 8, 8, 2, 256
R1 = 8
EW1 = KC * 2 * MI + KC * HID
NT1 = 2 * ((T * K1 // P + E1 + 1) // 2)
MAGIC = 1.5 * 2.0 ** 23


def constants():
    f = np.float32
    t = np.arange(S, dtype=f)[:, None]
    c = {}
    a0 = t * (f(1) / f(10000.0) ** (np.arange(0, ROPE, 2, dtype=f) / f(ROPE)))[None]
    a1 = t * (f(1) / f(10000.0) ** (np.arange(0, D1, 2, dtype=f) / f(D1)))[None]
    tile = lambda a: a.reshape(TPB, P, -1).transpose(1, 0, 2).reshape(P, -1)
    c["rope0"] = np.concatenate([tile(np.cos(a0)), tile(np.sin(a0))], 1)
    c["rope1"] = np.concatenate([tile(np.cos(a1)), tile(np.sin(a1))], 1)
    p = np.arange(P)
    own = (p[None] <= p[:, None]) & (p[:, None] - p[None] < WIN)
    prev = np.arange(WIN)[None] > p[:, None]
    c["window"] = np.concatenate([own, prev], 1)
    end = np.arange(NB) * M + M - 1
    c["blocks"] = np.concatenate([np.where(end[None] < (p + j * P)[:, None], 0.0, -1e30) for j in range(TPB)], 1)
    c["ident"] = np.eye(P)
    c["before"] = p[:, None] < p[None]
    c["iota"] = np.tile(np.arange(NT0)[None], (P, 1))
    return {"table_" + k: np.ascontiguousarray(v, dtype=f) for k, v in c.items()}


class Steps:

    def __init__(self, eng, sem, base=0):
        self.eng, self.sem, self.base, self.n = eng, sem, base, 0

    def __call__(self, ins):
        ins.then_inc(self.sem, 1)
        self.n += 1

    def wait(self):
        self.eng.wait_ge(self.sem, self.base + self.n)

    def link(self, ins):
        self(ins)
        self.wait()


def bc(ap, shape):
    return ap.to_broadcast(shape)


def build(nc, a, out):
    ctx = ExitStack()
    sb = lambda name, cols, dt=F32, rows=P: ctx.enter_context(nc.sbuf_tensor(name, [rows, cols], dt))
    sem = lambda name: ctx.enter_context(nc.semaphore(name))
    v3 = lambda ap, n: ap.rearrange("p (a b) -> p a b", a=n)

    with ctx:
        xs0 = nc.dram_tensor("sorted_x0", [NT0 * P, HID], F32).ap()
        ys0 = nc.dram_tensor("sorted_y0", [NT0 * P, HID], F32).ap()
        xs1 = nc.dram_tensor("sorted_x1", [NT1 * P, HID], F32).ap()
        ys1 = nc.dram_tensor("sorted_y1", [NT1 * P, HID], F32).ap()
        heads1 = nc.dram_tensor("heads1", [T, HID], F32).ap()

        RW = sb("expert_weights", E0 * EW0)
        X = sb("residual", NT * HID)
        XN = sb("normed", 2 * NT * HID)
        WC = sb("out_weights", H * HID)
        WQ = sb("q_up_weights", H * D, rows=QC)
        SW1 = sb("shared_w1", NSH * KC * DH)
        SW2 = sb("shared_w2", NSH * 2 * HID)
        TA = sb("tiles", 3072)
        VA = sb("values", NT * D)
        V2A = sb("values_before", B * D, rows=WIN + NB)
        CK0 = sb("blocks_at_zero", B * D, rows=NB)
        QCT = sb("qc_T", (NT + 1) * P, rows=QC)
        KCAT = sb("keys", B * KROW)
        VOWN = sb("values_tile", TPB * D)
        V2 = sb("values_before_tile", D, rows=WIN + NB)
        CKS = sb("blocks_tile", D, rows=NB)
        QCS = sb("qc_tile", TPB * P, rows=QC)
        IDN = sb("ident", P)
        WINDOW = sb("window", P + WIN)
        BLOCKS = sb("blocks_valid", TPB * NB)
        BEFORE = sb("before", P)
        BEFOREB = sb("before_bf16", P, BF16)
        ONESB = sb("ones_bf16", P, BF16)
        IOTA = sb("iota", NT0)
        ROPE0 = sb("rope0", 2 * TPB * HR)
        ROPE1 = sb("rope1", 2 * TPB * D1 // 2)
        ZERO = sb("zeros", HID)
        MHALF = sb("minus_half", NT * (H1 + HKV))
        RB = sb("router_bias", E0)
        RTW = sb("router_w", KC * E0)
        TOP = sb("top8", NT * 8)
        TOPI = sb("top8_index", NT * 8, U32)
        TOPF = sb("top8_float", NT * 8)
        GATE = sb("gates", NT * K0)
        GSUM = sb("gate_sums", 2 * NT)
        SLOTF = sb("slots_float", NT * K0)
        SLOT = sb("slots", NT * K0, I32)
        IDX = sb("slots_tile", K0, I32)
        MASKB = sb("chosen_bf16", NT * E0, BF16)
        CUMB = sb("chosen_before_bf16", (NT + 1) * E0, BF16)
        START = sb("starts", 4 * E0)
        TEXP = sb("tile_expert_float", NT0)
        TEX = sb("tile_expert", NT0, I32)
        B1A = sb("expert_b1_T", E0 + NSH)
        B1B = sb("expert_b1_T2", E0 + NSH, rows=DHB)
        STAT = sb("ln_stats", NT * 6)
        MV = sb("ln_mean_var", NT * 2)
        RSTD = sb("rstd", NT)
        RR = sb("rms", H)
        SSQ = sb("sum_squares", H)
        KW = sb("norm_columns", 4)
        SINK = sb("sinks", 4 * H)
        LSUM = sb("prob_sums", 4 * H)
        CM = sb("block_max", 4 * H)
        ps = [ctx.enter_context(nc.psum_tensor(f"bank{i}", [P, 512], F32)) for i in range(8)]

        xn, xnT = XN[:, 0:NT * HID], XN[:, NT * HID:]
        x3, xn3 = v3(X[:, :], NT), v3(xn, NT)
        xnT3 = v3(xnT, KC)
        rw3 = v3(RW[:, :], E0)
        wc3 = v3(WC[:, :], H)
        kc3 = v3(KCAT[:, :], B)

        ELATE = 17
        tail = RW[:, ELATE * EW0:]
        o = 0

        def cut(n):
            nonlocal o
            o += n
            return tail[:, o - n:o]
        WCP = cut(M * KC * D)
        WGS = cut(H * HID)
        WOS = cut(H // 2 * HID)
        WKV = cut(KC * 2 * D)
        WQC = cut(KC * QC)
        EMID, EEND = ELATE + M * KC * D // EW0, ELATE + (M * KC * D + H * HID + H // 2 * HID) // EW0
        KRAW, KTMP = TA[:, 0:NT * D], TA[:, NT * D:2 * NT * D]
        o2 = 2 * NT * K0 * E0
        B1 = WC[0:E0 + NSH, o2:o2 + DH]
        KWR = TA[0:NB * B, 2816:2816 + D]
        LOGIT = WC[:, o2 + DH + D:o2 + DH + D + NT * E0]
        CUM = WC[:, o2 + DH + D + NT * E0:o2 + DH + D + 2 * NT * E0]
        CKR = TA[0:NB * B, 2560:2560 + 2 * D]
        ONEH, PROD = WC[:, 0:NT * K0 * E0], WC[:, NT * K0 * E0:2 * NT * K0 * E0]

        ln_stats, ln_var, ln_rstd, xn_ok = (sem("norm_" + n) for n in ("stats", "var", "rstd", "done"))
        chosen, rank_ok, gates_sub, gates_exp, slots_ok = (sem("route_" + n) for n in ("chosen", "rank", "gates_sub", "gates_exp", "slots"))

        def route_dve(dve, st, E, K):
            lg, tp, ti = v3(LOGIT[:, 0:NT * E], NT), v3(TOP[:, :], NT), v3(TOPI[:, :], NT)
            tf, g3 = v3(TOPF[:, :], NT), v3(GATE[:, 0:NT * K], NT)
            oh = ONEH[:, 0:NT * K * E].rearrange("p (t k e) -> p t k e", t=NT, k=K)
            pr = PROD[:, 0:NT * K * E].rearrange("p (t k e) -> p t k e", t=NT, k=K)
            for t in range(NT):
                st(nc.vector.max(tp[:, t, :], lg[:, t, :]))
            st.wait()
            for t in range(NT):
                st(nc.vector.max_index(ti[:, t, :], tp[:, t, :], lg[:, t, :]))
            st.wait()
            st.link(nc.vector.tensor_copy(TOPF[:, :], TOPI[:, :]))
            for t in range(NT):
                st(nc.vector.tensor_tensor(oh[:, t], bc(IOTA[:, 0:E].unsqueeze(1), [P, K, E]),
                                           bc(tf[:, t, 0:K].unsqueeze(2), [P, K, E]), ALU.is_equal))
            st.wait()
            st.link(nc.vector.tensor_reduce(v3(CUM[:, 0:NT * E], NT),
                                            ONEH[:, 0:NT * K * E].rearrange("p (t k e) -> p t e k", t=NT, k=K),
                                            AX, ALU.add))
            st(nc.vector.tensor_copy(MASKB[:, 0:NT * E], CUM[:, 0:NT * E]))
            st.link(nc.vector.memset(CUMB[:, 0:E], 0.0))
            for t in range(1, NT):
                st.link(nc.vector.tensor_tensor(CUM[:, t * E:(t + 1) * E], CUM[:, (t - 1) * E:t * E],
                                                CUM[:, t * E:(t + 1) * E], ALU.add))
            nc.vector.tensor_copy(CUMB[:, E:(NT + 1) * E], CUM[:, 0:NT * E]).then_inc(chosen, 1)
            nc.vector.tensor_tensor(g3, tp[:, :, 0:K], bc(tp[:, :, 0:1], [P, NT, K]), ALU.subtract).then_inc(gates_sub, 1)

        def route_dve_slots(dve, st, E, K, ntile, bank, layer):
            g3 = v3(GATE[:, 0:NT * K], NT)
            pr = PROD[:, 0:NT * K * E].rearrange("p (t k e) -> p t k e", t=NT, k=K)
            oh = ONEH[:, 0:NT * K * E].rearrange("p (t k e) -> p t k e", t=NT, k=K)
            dve.wait_ge(gates_exp, layer + 1)
            st.link(nc.vector.reduce_sum(GSUM[:, 0:NT], g3, AX))
            st.link(nc.vector.reciprocal(GSUM[:, NT:], GSUM[:, 0:NT]))
            st(nc.vector.tensor_tensor(g3, g3, bc(GSUM[:, NT:].unsqueeze(2), [P, NT, K]), ALU.mult))
            dve.wait_ge(rank_ok, layer + 1)
            n = START[:, 0:E]
            st.link(nc.vector.tensor_scalar(n, bank[:, NT * E:(NT + 1) * E], 1.0 / P,
                                            (P - 1.0) / P - 0.5 + 0.5 / P, ALU.mult, ALU.add))
            st.link(nc.vector.tensor_scalar(n, n, MAGIC, -MAGIC, ALU.add, ALU.add))
            st.link(nc.vector.memset(START[:, E0:E0 + E], 1.0))
            st.link(nc.vector.tensor_tensor_scan(START[:, 2 * E0:2 * E0 + E], START[:, E0:E0 + E], n, 0.0,
                                                 ALU.mult, ALU.add))
            st.link(nc.vector.tensor_tensor(n, START[:, 2 * E0:2 * E0 + E], n, ALU.subtract))
            st.link(nc.vector.tensor_scalar(START[:, E0:E0 + E], n, float(P), None, ALU.mult))
            st.link(nc.vector.tensor_tensor(v3(CUM[:, 0:NT * E], NT), v3(bank[:, 0:NT * E], NT),
                                            bc(START[:, E0:E0 + E].unsqueeze(1), [P, NT, E]), ALU.add))
            for t in range(NT):
                st(nc.vector.tensor_tensor(pr[:, t], oh[:, t],
                                           bc(CUM[:, t * E:(t + 1) * E].unsqueeze(1), [P, K, E]), ALU.mult))
            st.wait()
            st.link(nc.vector.tensor_reduce(v3(SLOTF[:, 0:NT * K], NT), pr, AX, ALU.add))
            nc.vector.tensor_copy(SLOT[:, 0:NT * K], SLOTF[:, 0:NT * K]).then_inc(slots_ok, 1)
            ge = WC[0:1, 0:ntile * E].rearrange("p (i e) -> p i e", i=ntile)
            dve.wait_ge(slots_ok, 2 * layer + 1)
            st.link(nc.vector.tensor_tensor(ge, bc(IOTA[0:1, 0:ntile].unsqueeze(2), [1, ntile, E]),
                                            bc(START[0:1, 0:E].unsqueeze(1), [1, ntile, E]), ALU.is_ge))
            st.link(nc.vector.reduce_sum(TEXP[0:1, 0:ntile], ge, AX))
            st.link(nc.vector.tensor_scalar(TEXP[0:1, 0:ntile], TEXP[0:1, 0:ntile], -1.0, None, ALU.add))
            nc.vector.tensor_copy(TEX[0:1, 0:ntile], TEXP[0:1, 0:ntile]).then_inc(slots_ok, 1)

        def rank_pe(pe, E, bank, layer):
            pe.wait_ge(chosen, layer + 1)
            for t in range(NT):
                nc.tensor.matmul(bank[:, t * E:(t + 1) * E], BEFOREB[:, :], MASKB[:, t * E:(t + 1) * E],
                                 start=True, stop=False)
                nc.tensor.matmul(bank[:, t * E:(t + 1) * E], ONESB[:, :], CUMB[:, t * E:(t + 1) * E],
                                 start=False, stop=True)
            nc.tensor.matmul(bank[:, NT * E:(NT + 1) * E], ONESB[:, :], CUMB[:, NT * E:(NT + 1) * E],
                             start=True, stop=True).then_inc(rank_ok, 1)

        def layernorm_dve(dve, st, layer):
            mv = v3(MV[:, :], NT)
            for t in range(NT):
                st(nc.vector.bn_stats(STAT[:, 6 * t:6 * t + 6], x3[:, t, :]))
            st.wait()
            for t in range(NT):
                ins = nc.vector.bn_aggr(mv[:, t, :], STAT[:, 6 * t:6 * t + 6])
                if t < NT - 1:
                    st(ins)
            ins.then_inc(ln_stats, 1)
            st.wait()
            dve.wait_ge(ln_rstd, layer + 1)
            for t in range(NT):
                nc.vector.tensor_scalar(xn3[:, t, :], x3[:, t, :], mv[:, t, 0:1], RSTD[:, t:t + 1],
                                        ALU.subtract, ALU.mult).then_inc(xn_ok, 1)

        def layernorm_pool(pool, layer):
            pool.wait_ge(ln_stats, layer + 1)
            nc.gpsimd.tensor_scalar(RSTD[:, :].unsqueeze(2), v3(MV[:, :], NT)[:, :, 1:2], LN_EPS, None,
                                    ALU.add).then_inc(ln_var, 1)
            pool.wait_ge(ln_var, layer + 1)
            nc.gpsimd.tensor_tensor(RSTD[:, :], RSTD[:, :], MHALF[:, 0:NT], ALU.pow).then_inc(ln_rstd, 1)

        ld_x, ld_c, ld_rt, ld_sh, ld_aw, ld_cp, ld_wg, ld_ex, ld_ex2, ld_ct = (
            sem(n) for n in ("ld_x", "ld_const", "ld_router", "ld_shared", "ld_attn_w", "ld_comp", "ld_wg",
                             "ld_experts", "ld_experts2", "ld_attn_tables"))
        n_c = n_rt = n_sh = n_aw = n_ex = n_ex2 = 0
        zero_set, zero_done = sem("zero_set"), sem("zero_done")
        const_set = sem("const_set")
        dve1, act1, pool1 = sem("dve1"), sem("act1"), sem("pool1")
        xt_ps, xt_sb = sem("xT_psum"), sem("xT_sbuf")
        lg_ps, lg_sb = sem("logit_psum"), sem("logit_sbuf")
        b1_ps, b1_sb = sem("b1_psum"), sem("b1_sbuf")
        scat0 = sem("scatter0")
        sh_ps, sh_sb, so_ps, so_sb = (sem(n) for n in ("shared_h_psum", "shared_h_sbuf", "shared_o_psum", "shared_o_sbuf"))
        wt_ps, wt_sb, wf_ps, wf_sb = (sem(n) for n in ("wgT_psum", "wgT_sbuf", "fold_psum", "fold_sbuf"))
        kv_ps, kv_sb, v2_ps, v2_sb, qc_ps, qc_sb, ck_ps = (
            sem(n) for n in ("kv_psum", "kv_sbuf", "v2_psum", "v2_sbuf", "qc_psum", "qc_sbuf", "ck_psum"))
        kss, krr, kn_r, kt_ps, kt_sb = (sem(n) for n in ("k_squares", "k_rms", "k_normed", "kT_psum", "kT_sbuf"))
        css, crr, ck_r, ckd, kvp = (sem(n) for n in ("ck_squares", "ck_rms", "ck_ready", "ck_moved", "pool_k"))

        wkv3, wqc3 = v3(WKV, KC), v3(WQC, KC)
        wcp3 = v3(WCP, M * KC)
        wgs3, wos3 = v3(WGS, H), v3(WOS, H // 2)
        sw1 = SW1[:, :].rearrange("p (s k n) -> p s k n", s=NSH, k=KC)
        sw2 = SW2[:, :].rearrange("p (s c n) -> p s c n", s=NSH, c=2)
        va3, v2a3, ck03 = v3(VA[:, :], NT), v3(V2A[:, :], B), v3(CK0[:, :], B)
        HF = T // 2
        shA = v3(TA[:, 0:NSH * HF], NSH)
        shB = v3(TA[:, NSH * HF:2 * NSH * HF], NSH)
        wgT = [TA[:, 2 * NSH * HF + i * HID:2 * NSH * HF + (i + 1) * HID] for i in range(2)]
        kraw3 = v3(KRAW, NT)

        with nc.Block() as block:
            @block.sync
            def _(sp):
                nonlocal n_c, n_rt, n_sh, n_aw, n_ex, n_ex2
                sp.dma_start(x3, a["L0_attn_h"].rearrange("b (j p) d -> p (b j) d", p=P)).then_inc(ld_x, 16)
                for t, n in ((IDN, "ident"), (BEFORE, "before"), (IOTA, "iota")):
                    sp.dma_start(t[:, :], a["table_" + n]).then_inc(ld_c, 16)
                    n_c += 16
                sp.dma_start(v3(RTW[:, :], KC), a["L0_ffn_router_w"].rearrange("(k p) e -> p k e", p=P)).then_inc(ld_rt, 16)
                sp.dma_start(RB[:, :], a["L0_ffn_router_b"].partition_broadcast(P)).then_inc(ld_rt, 16)
                for s in range(NSH):
                    sp.dma_start(sw1[:, s], a["L0_ffn_sw1"][s].rearrange("(k p) n -> p k n", p=P)).then_inc(ld_sh, 16)
                    sp.dma_start(sw2[:, s, 0], a["L0_ffn_sw2"][s, 0:P, :]).then_inc(ld_sh, 16)
                    sp.dma_start(sw2[0:DHB, s, 1], a["L0_ffn_sw2"][s, P:DH, :]).then_inc(ld_sh, 16)
                    sp.dma_start(sw2[DHB:DHB + 1, s, 1], a["L0_ffn_sb2"][s:s + 1, :]).then_inc(ld_sh, 16)
                    n_sh += 64
                sp.dma_start(B1[0:E0, :], a["L0_ffn_rb1"]).then_inc(ld_sh, 16)
                sp.dma_start(B1[E0:E0 + NSH, :], a["L0_ffn_sb1"]).then_inc(ld_sh, 16)
                n_sh += 32
                sp.wait_ge(zero_set, 1)
                for i in range(NT0 // 4):
                    sp.dma_start(xs0[i * 4 * P:(i + 1) * 4 * P, :].rearrange("(c p) d -> p c d", p=P),
                                 bc(ZERO[:, :].unsqueeze(1), [P, 4, HID])).then_inc(zero_done, 16)
                sp.dma_start(wcp3, a["L0_attn_W_comp"].rearrange("(c p) d -> p c d", p=P)).then_inc(ld_cp, 16)
                for k in range(KC):
                    sp.dma_start(wkv3[:, k, 0:D], a["L0_attn_Wk"][k * P:(k + 1) * P, :]).then_inc(ld_aw, 16)
                    sp.dma_start(wkv3[:, k, D:], a["L0_attn_Wv"][k * P:(k + 1) * P, :]).then_inc(ld_aw, 16)
                    sp.dma_start(wqc3[:, k, :], a["L0_attn_Wq_c"][k * P:(k + 1) * P, :]).then_inc(ld_aw, 16)
                col = lambda n: a[n].rearrange("(p o) -> p o", o=1)
                sp.dma_start(KW[:, 0:1], col("L0_attn_q_norm_w")).then_inc(ld_aw, 16)
                sp.dma_start(KW[:, 1:2], col("L0_attn_k_norm_w")).then_inc(ld_aw, 16)
                sp.dma_start(KWR[:, :], a["L0_attn_k_norm_w"].partition_broadcast(NB * B)).then_inc(ld_aw, 16)
                sp.dma_start(SINK[:, 0:H], a["L0_attn_sink"].partition_broadcast(P)).then_inc(ld_aw, 16)
                n_aw = 16 * (3 * KC + 4)
                sp.dma_start(wgs3, a["L0_attn_Wg"].rearrange("g (r p) i -> p (g r) i", p=P)).then_inc(ld_wg, 16)
                sp.dma_start(wos3, a["L0_attn_Wo"].rearrange("(c p) n -> p c n", p=P)).then_inc(ld_wg, 16)
                sp.dma_start(WQ[:, :], a["L0_attn_Wq_up"]).then_inc(ld_ex, 16)
                for t, n in ((WINDOW, "window"), (BLOCKS, "blocks"), (ROPE0, "rope0"), (ROPE1, "rope1")):
                    sp.dma_start(t[:, :], a["table_" + n]).then_inc(ld_ct, 16)

                def experts(e0, e1, done):
                    for k in range(KC):
                        sp.dma_start(rw3[:, e0:e1, k * DH:(k + 1) * DH],
                                     a["L0_ffn_rw1"][e0:e1, k * P:(k + 1) * P, :].rearrange("e p n -> p e n")).then_inc(done, 16)
                    sp.dma_start(rw3[:, e0:e1, W2A:W2B], a["L0_ffn_rw2"][e0:e1, 0:P, :].rearrange("e p n -> p e n")).then_inc(done, 16)
                    sp.dma_start(rw3[0:DHB, e0:e1, W2B:], a["L0_ffn_rw2"][e0:e1, P:DH, :].rearrange("e p n -> p e n")).then_inc(done, 16)
                    sp.dma_start(rw3[DHB:DHB + 1, e0:e1, W2B:], a["L0_ffn_rb2"][e0:e1, :].unsqueeze(0)).then_inc(done, 16)
                experts(0, ELATE, ld_ex)
                sp.wait_ge(ck_ps, 1)
                experts(ELATE, EMID, ld_ex2)
                sp.wait_ge(wf_ps, H)
                experts(EMID, EEND, ld_ex2)
                sp.wait_ge(qc_ps, 2)
                sp.wait_ge(v2_ps, 1)
                experts(EEND, E0, ld_ex2)
                sp.wait_ge(ck_r, 1)
                for b in range(B):
                    rows = CKR[b * NB:(b + 1) * NB, 0:D]
                    sp.dma_start(v2a3[WIN:WIN + NB, b, :], rows).then_inc(ckd, 16)
                    sp.dma_start(ck03[0:NB, b, :], rows).then_inc(ckd, 16)
                sp.wait_ge(ckd, 16 * 2 * B)

            @block.gpsimd
            def _(pool):
                st = Steps(pool, pool1)
                nc.gpsimd.memset(ZERO[:, :], 0.0).then_inc(zero_set, 1)
                pool.wait_ge(zero_set, 1)
                nc.gpsimd.memset(MHALF[:, :], -0.5).then_inc(const_set, 1)
                pool.wait_ge(const_set, 1)
                nc.gpsimd.memset(ONESB[:, :], 1.0).then_inc(const_set, 1)
                pool.wait_ge(const_set, 2)
                nc.gpsimd.memset(TA[32:64, NSH * HF:2 * NSH * HF], 1.0).then_inc(const_set, 1)
                pool.wait_ge(const_set, 3)
                nc.gpsimd.memset(QCT[:, NT * P:], 0.0).then_inc(const_set, 1)
                pool.wait_ge(const_set, 4)
                layernorm_pool(pool, 0)

                def scatter(t0, t1):
                    for t in range(t0, t1):
                        for k in range(K0):
                            nc.gpsimd.indirect_dma_start(
                                xs0, bass.IndirectOffsetOnAxis(ap=SLOT[:, t * K0 + k:t * K0 + k + 1], axis=0),
                                xn3[:, t, :], None).then_inc(scat0, 16)
                pool.wait_ge(slots_ok, 1)
                pool.wait_ge(zero_done, 16 * (NT0 // 4))
                scatter(0, NT)
                pool.wait_ge(css, 1)
                nc.gpsimd.tensor_scalar(CM[0:NB * B, 1:2], CM[0:NB * B, 0:1], 1.0 / D, RMS_EPS, ALU.mult, ALU.add).then_inc(kvp, 1)
                pool.wait_ge(kvp, 1)
                nc.gpsimd.tensor_tensor(CM[0:NB * B, 2:3], CM[0:NB * B, 1:2], MHALF[0:NB * B, 0:1], ALU.pow).then_inc(crr, 1)
                pool.wait_ge(kss, 1)
                nc.gpsimd.tensor_scalar(RR[:, 0:NT], SSQ[:, 0:NT], 1.0 / D, RMS_EPS, ALU.mult, ALU.add).then_inc(kvp, 1)
                pool.wait_ge(kvp, 2)
                nc.gpsimd.tensor_tensor(RR[:, NT:2 * NT], RR[:, 0:NT], MHALF[:, 0:NT], ALU.pow).then_inc(krr, 1)

            @block.scalar
            def _(act):
                for t in range(NT):
                    act.wait_ge(xt_ps, t + 1)
                    nc.scalar.activation(xnT3[:, :, t * P:(t + 1) * P], v3(ps[t % 2][:, 0:HID], KC), ACT.Copy).then_inc(xt_sb, 1)
                act.wait_ge(b1_ps, 1)
                nc.scalar.activation(B1A[:, :], ps[3][:, 0:E0 + NSH], ACT.Copy).then_inc(b1_sb, 1)
                nc.scalar.activation(B1B[:, :], ps[3][0:DHB, 64:64 + E0 + NSH], ACT.Copy).then_inc(b1_sb, 1)
                act.wait_ge(b1_sb, 2)
                act.wait_ge(const_set, 4)

                def shared_relu(i):
                    hf, s, c = i // 4, i // 2 % 2, i % 2
                    act.wait_ge(sh_ps, i + 1)
                    if hf and not s and not c:
                        act.wait_ge(so_ps, NT // 2)
                    if c == 0:
                        nc.scalar.activation(shA[:, s, :], ps[4 + i % 2][:, :], ACT.Relu,
                                             bias=B1A[:, E0 + s:E0 + s + 1]).then_inc(sh_sb, 1)
                    else:
                        nc.scalar.activation(shB[0:DHB, s, :], ps[4 + i % 2][0:DHB, :], ACT.Relu,
                                             bias=B1B[:, E0 + s:E0 + s + 1]).then_inc(sh_sb, 1)
                for i in range(4):
                    shared_relu(i)
                act.wait_ge(gates_sub, 1)
                nc.scalar.activation(GATE[:, :], GATE[:, :], ACT.Exp).then_inc(gates_exp, 1)
                for i in range(4, 8):
                    shared_relu(i)
                for n in range(2):
                    act.wait_ge(qc_ps, n + 1)
                    nc.scalar.activation(QCT[:, n * 512:(n + 1) * 512], ps[4 + n][0:QC, :], ACT.Copy).then_inc(qc_sb, 1)
                for h in range(H):
                    act.wait_ge(wt_ps, h + 1)
                    if h >= 2:
                        act.wait_ge(wf_ps, h - 1)
                    nc.scalar.activation(wgT[h % 2], ps[4 + h % 2][:, 0:HID], ACT.Copy).then_inc(wt_sb, 1)
                act.wait_ge(v2_ps, 1)
                nc.scalar.activation(V2A[0:WIN, :], ps[3][0:WIN, :], ACT.Copy).then_inc(v2_sb, 1)

            @block.vector
            def _(dve):
                st = Steps(dve, dve1)
                dve.wait_ge(ld_c, n_c)
                nc.vector.tensor_copy(BEFOREB[:, :], BEFORE[:, :]).then_inc(dve1, 1)
                st.n += 1
                dve.wait_ge(ld_x, 16)
                layernorm_dve(dve, st, 0)
                dve.wait_ge(lg_ps, 1)
                dve.wait_ge(ld_rt, 32)
                st.link(nc.vector.tensor_tensor(v3(LOGIT[:, :], NT), v3(ps[2][:, 0:NT * E0], NT),
                                                bc(RB[:, :].unsqueeze(1), [P, NT, E0]), ALU.add))
                route_dve(dve, st, E0, K0)
                route_dve_slots(dve, st, E0, K0, NT0, ps[3], 0)

                def shared_add(t):
                    dve.wait_ge(so_ps, t + 1)
                    nc.vector.scalar_tensor_tensor(out=x3[:, t, :], in0=ps[t % 2][:, 0:HID], scalar=1.0 / NSH,
                                                   in1=x3[:, t, :], op0=ALU.mult, op1=ALU.add).then_inc(so_sb, 1)
                for t in range(NT):
                    shared_add(t)
                dve.wait_ge(ck_ps, 1)
                dve.wait_ge(ld_aw, n_aw)
                ckn = CKR[:, 0:D]
                st.link(nc.vector.tensor_copy(CKR[:, D:], ps[2][0:NB * B, 0:D]))
                nc.vector.scalar_tensor_tensor(out=ckn, in0=CKR[:, D:], scalar=1.0, in1=CKR[:, D:], op0=ALU.mult,
                                               op1=ALU.mult, accum_out=CM[0:NB * B, 0:1]).then_inc(css, 1)
                dve.wait_ge(css, 1)
                for h in range(H):
                    dve.wait_ge(wf_ps, h + 1)
                    nc.vector.tensor_copy(wc3[:, h, :], ps[6 + h % 2][:, 0:HID]).then_inc(wf_sb, 1)
                for t in range(NT):
                    dve.wait_ge(kv_ps, t + 1)
                    st(nc.vector.tensor_copy(kraw3[:, t, :], ps[6 + t % 2][:, 0:D]))
                    nc.vector.tensor_copy(va3[:, t, :], ps[6 + t % 2][:, D:2 * D]).then_inc(kv_sb, 1)
                st.wait()
                sq = KTMP[:, 0:D]
                for t in range(NT):
                    ins = nc.vector.scalar_tensor_tensor(out=v3(KTMP, NT)[:, t, :], in0=kraw3[:, t, :], scalar=1.0, in1=kraw3[:, t, :],
                                                         op0=ALU.mult, op1=ALU.mult, accum_out=SSQ[:, t:t + 1])
                    if t < NT - 1:
                        st(ins)
                ins.then_inc(kss, 1)
                st.wait()
                dve.wait_ge(kss, 1)
                dve.wait_ge(ld_ct, 64)
                k4 = KRAW.rearrange("p (b j d) -> p b j d", b=B, j=TPB)
                k1, k2 = k4[:, :, :, 0:HR], k4[:, :, :, HR:ROPE]
                tmp = [KTMP[:, i * NT * HR:(i + 1) * NT * HR].rearrange("p (b j d) -> p b j d", b=B, j=TPB) for i in range(4)]
                cs = [bc(v3(ROPE0[:, i * TPB * HR:(i + 1) * TPB * HR], TPB).unsqueeze(1), [P, B, TPB, HR]) for i in range(2)]
                for dst, src, c in ((0, k1, 0), (1, k2, 1), (2, k1, 1), (3, k2, 0)):
                    for b in range(B):
                        st(nc.vector.tensor_tensor(tmp[dst][:, b], src[:, b], cs[c][:, b], ALU.mult))
                st.wait()
                st(nc.vector.tensor_tensor(k1, tmp[0], tmp[1], ALU.subtract))
                st(nc.vector.tensor_tensor(k2, tmp[2], tmp[3], ALU.add))
                st.link(nc.vector.tensor_tensor(KW[:, 2:3], KW[:, 0:1], KW[:, 1:2], ALU.mult))
                dve.wait_ge(crr, 1)
                nc.vector.scalar_tensor_tensor(out=ckn, in0=CKR[:, D:], scalar=CM[0:NB * B, 2:3], in1=KWR[:, :],
                                               op0=ALU.mult, op1=ALU.mult).then_inc(ck_r, 1)
                dve.wait_ge(krr, 1)
                nc.vector.tensor_tensor(kraw3, kraw3, bc(RR[:, NT:].unsqueeze(2), [P, NT, D]), ALU.mult).then_inc(kn_r, 1)
                for half in range(2):
                    dve.wait_ge(kt_ps, half + 1)
                    b4 = ps[half][:, :].rearrange("p (b j t) -> p b j t", b=2, j=TPB)
                    dst = kc3[:, 2 * half:2 * half + 2, :]
                    w = KW[:, 2:3]
                    nc.vector.tensor_scalar(dst[:, :, 0:P], b4[:, :, 0, :], w, None, ALU.mult).then_inc(kt_sb, 1)
                    nc.vector.tensor_scalar(dst[:, :, P + NB:2 * P + NB], b4[:, :, 1, :], w, None, ALU.mult).then_inc(kt_sb, 1)
                    nc.vector.tensor_scalar(dst[:, :, 2 * P + NB:2 * P + NB + WIN], b4[:, :, 0, P - WIN:], w, None, ALU.mult).then_inc(kt_sb, 1)
                dve.wait_ge(kt_ps, 3)
                c3 = v3(ps[2][:, 0:B * NB], B)
                nc.vector.tensor_scalar(kc3[:, :, P:P + NB], c3, KW[:, 0:1], None, ALU.mult).then_inc(kt_sb, 1)
                nc.vector.tensor_scalar(kc3[:, :, KROW - NB:], c3, KW[:, 0:1], None, ALU.mult).then_inc(kt_sb, 1)
                m0 = SINK[:, H:2 * H]
                st.link(nc.vector.tensor_scalar(m0, SINK[:, 0:H], 0.0, None, ALU.max))
                st(nc.vector.tensor_tensor(SINK[:, 2 * H:3 * H], SINK[:, 0:H], m0, ALU.subtract))
                st.link(nc.vector.tensor_scalar(m0, m0, -1.0, None, ALU.mult))

            @block.tensor
            def _(pe):
                pe.wait_ge(ld_c, n_c)
                for t in range(NT):
                    pe.wait_ge(xn_ok, t + 1)
                    if t >= 2:
                        pe.wait_ge(xt_sb, t - 1)
                    for k in range(KC):
                        ins = nc.tensor.transpose(ps[t % 2][:, k * P:(k + 1) * P], xn3[:, t, k * P:(k + 1) * P], IDN[:, :])
                    ins.then_inc(xt_ps, 1)
                pe.wait_ge(ld_rt, 32)
                pe.wait_ge(xt_sb, NT)
                for t in range(NT):
                    for k in range(KC):
                        ins = nc.tensor.matmul(ps[2][:, t * E0:(t + 1) * E0], xnT3[:, k, t * P:(t + 1) * P],
                                               v3(RTW[:, :], KC)[:, k, :], start=(k == 0), stop=(k == KC - 1))
                ins.then_inc(lg_ps, 1)
                pe.wait_ge(ld_sh, n_sh)
                nb = E0 + NSH
                nc.tensor.transpose(ps[3][:, 0:nb], B1[:, 0:P], IDN[0:nb, 0:nb])
                nc.tensor.transpose(ps[3][0:DHB, 64:64 + nb], B1[:, P:DH], IDN[0:nb, 0:nb]).then_inc(b1_ps, 1)

                def shared_up(hf):
                    for s in range(NSH):
                        for c in range(2):
                            i = 4 * hf + 2 * s + c
                            if i >= 2:
                                pe.wait_ge(sh_sb, i - 1)
                            n = P if c == 0 else DHB
                            for k in range(KC):
                                ins = nc.tensor.matmul(ps[4 + i % 2][0:n, :], sw1[:, s, k, c * P:c * P + n],
                                                       xnT3[:, k, hf * HF:(hf + 1) * HF], start=(k == 0), stop=(k == KC - 1))
                            ins.then_inc(sh_ps, 1)

                def shared_down(hf):
                    pe.wait_ge(sh_sb, 4 * hf + 4)
                    for i in range(NT // 2):
                        t = hf * NT // 2 + i
                        if t >= 2:
                            pe.wait_ge(so_sb, t - 1)
                        for s in range(NSH):
                            nc.tensor.matmul(ps[t % 2][:, 0:HID], shA[:, s, i * P:(i + 1) * P], sw2[:, s, 0],
                                             start=(s == 0), stop=False)
                            ins = nc.tensor.matmul(ps[t % 2][:, 0:HID], shB[0:DHB + 1, s, i * P:(i + 1) * P],
                                                   sw2[0:DHB + 1, s, 1], start=False, stop=(s == NSH - 1))
                        ins.then_inc(so_ps, 1)
                shared_up(0)
                pe.wait_ge(b1_sb, 2)
                rank_pe(pe, E0, ps[3], 0)
                shared_down(0)
                shared_up(1)
                shared_down(1)
                pe.wait_ge(ld_cp, 16)
                pe.wait_ge(chosen, 1)
                for c in range(M * KC):
                    m, k = c // KC, c % KC
                    ins = nc.tensor.matmul(ps[2][0:NB * B, 0:D], xnT3[:, k, m:T:M], wcp3[:, c, :],
                                           start=(c == 0), stop=(c == M * KC - 1))
                ins.then_inc(ck_ps, 1)
                pe.wait_ge(ld_aw, n_aw)
                pe.wait_ge(sh_sb, 8)
                for n in range(2):
                    for k in range(KC):
                        ins = nc.tensor.matmul(ps[4 + n][0:QC, :], wqc3[:, k, :], xnT3[:, k, n * 512:(n + 1) * 512],
                                               start=(k == 0), stop=(k == KC - 1))
                    ins.then_inc(qc_ps, 1)
                pe.wait_ge(ld_wg, 32)
                pe.wait_ge(qc_sb, 2)

                def fold(h):
                    pe.wait_ge(wt_sb, h + 1)
                    if h >= 2:
                        pe.wait_ge(wf_sb, h - 1)
                    for k in range(KC):
                        ins = nc.tensor.matmul(ps[6 + h % 2][:, 0:HID], wgT[h % 2][:, k * P:(k + 1) * P],
                                               wos3[:, h // 4 * KC + k, :], start=(k == 0), stop=(k == KC - 1))
                    ins.then_inc(wf_ps, 1)
                for h in range(H):
                    if h >= 2:
                        pe.wait_ge(wt_sb, h - 1)
                    for k in range(KC):
                        ins = nc.tensor.transpose(ps[4 + h % 2][:, k * P:(k + 1) * P], wgs3[:, h, k * P:(k + 1) * P], IDN[:, :])
                    ins.then_inc(wt_ps, 1)
                    if h >= 1:
                        fold(h - 1)
                fold(H - 1)
                pe.wait_ge(wf_sb, H)
                for t in range(NT):
                    if t >= 2:
                        pe.wait_ge(kv_sb, t - 1)
                    for k in range(KC):
                        ins = nc.tensor.matmul(ps[6 + t % 2][:, 0:2 * D], xnT3[:, k, t * P:(t + 1) * P], wkv3[:, k, :],
                                               start=(k == 0), stop=(k == KC - 1))
                    ins.then_inc(kv_ps, 1)
                pe.wait_ge(slots_ok, 1)
                for b in range(B):
                    for k in range(KC):
                        lo = b * S + P - WIN
                        ins = nc.tensor.matmul(ps[3][0:WIN, b * D:(b + 1) * D], xnT3[:, k, lo:lo + WIN], wkv3[:, k, D:],
                                               start=(k == 0), stop=(k == KC - 1))
                ins.then_inc(v2_ps, 1)
                pe.wait_ge(kn_r, 1)
                pe.wait_ge(so_sb, NT)
                for half in range(2):
                    for i in range(NT // 2):
                        ins = nc.tensor.transpose(ps[half][:, i * P:(i + 1) * P], kraw3[:, half * NT // 2 + i, :], IDN[:, :])
                    ins.then_inc(kt_ps, 1)
                pe.wait_ge(ck_r, 1)
                pe.wait_ge(v2_sb, 1)
                nc.tensor.transpose(ps[2][:, 0:B * NB], CKR[:, 0:D], IDN[0:B * NB, 0:B * NB]).then_inc(kt_ps, 1)

        tile_sems = ([sem(f"tile_loaded{i}") for i in range(4)], [sem(f"tile_stored{i}") for i in range(2)],
                     [sem("tile_" + n) for n in ("xT_psum", "xT_sbuf", "h_psum", "h_sbuf", "hT_psum", "hT_sbuf",
                                                 "y_psum", "y_sbuf", "silu")])

        def expert_parts(before, ntile, xs, ys, loads, scattered, n_scattered, stages):
            ld, stq, (xT_ps, xT_sb, h_ps, h_sb, hT_ps, hT_sb, y_ps, y_sb, mid) = tile_sems

            def await_tiles(eng, s, n):
                eng.wait_ge(s, n + before)

            def await_dma(eng, s, n, rings):
                eng.wait_ge(s, n + before * 16 // rings)
            SK = 3
            G0 = 5
            xt = [TA[:, i * HID:(i + 1) * HID] for i in range(4)]
            xT = [TA[:, (4 + i) * HID:(5 + i) * HID] for i in range(2)]
            hs = [TA[:, (6 + i) * HID:(7 + i) * HID] for i in range(2)]
            hT = [TA[:, (8 + i) * HID:(9 + i) * HID] for i in range(2)]
            yt = [TA[:, (10 + i) * HID:(11 + i) * HID] for i in range(2)]

            def experts(engine, g, n):
                return nc.values_load_multi_w_load_instructions(
                    TEX[0:1, bass.ds(g, n)], [engine], min_val=0, max_val=stages["E"] - 1,
                    skip_runtime_bounds_check_because="a count of the experts that start at a tile or before, less one")[1]

            def run(eng, step, engine=None, lags=()):
                def outside(g):
                    on = lambda lag: 0 <= g - lag < ntile
                    e = {lag: experts(engine, g - lag, 1)[0] for lag in lags if on(lag)}
                    step(g, g % 4, lambda n, lag: (g - lag) // n, on, e.get)
                for g in range(G0):
                    outside(g)
                n4 = (ntile - G0) // 4
                with eng.Fori(0, n4) as i:
                    e = {}
                    if lags:
                        first, n = G0 - max(lags), 4 + max(lags) - min(lags)
                        e = dict(zip(range(first, first + n), experts(engine, i * 4 + first, n)))
                    for c in range(G0, G0 + 4):
                        step(i * 4 + c, c % 4, lambda n, lag: i * (4 // n) + (c - lag) // n, lambda lag: True,
                             lambda lag: e.get(c - lag))
                for g in range(G0 + 4 * n4, ntile + SK):
                    outside(g)

            def early(g, n):
                return isinstance(g, int) and g < n

            def sync(sp):
                sp.wait_ge(scattered, n_scattered)
                for s, n in loads:
                    sp.wait_ge(s, n)

                def step(g, q, rounds, on, expert):
                    if on(0):
                        if not early(g, 4):
                            await_tiles(sp, xT_ps, g - 3)
                        sp.dma_start(xt[q], xs[bass.ds(g * P, P), :]).then_inc(ld[q], 16)
                run(sp, step)

            def tensor(pe):
                for s, n in loads:
                    pe.wait_ge(s, n)

                def step(g, q, rounds, on, expert):
                    if on(0):
                        await_dma(pe, ld[q], rounds(4, 0) * 16 + 16, 4)
                        for k in range(KC):
                            ins = nc.tensor.transpose(ps[q % 2][:, k * P:(k + 1) * P], xt[q][:, k * P:(k + 1) * P], IDN[:, :])
                        ins.then_inc(xT_ps, 1)
                    if on(1):
                        await_tiles(pe, xT_sb, g)
                        stages["up"](expert(1), ps[2 + (q + 1) % 2], xT[(q + 1) % 2]).then_inc(h_ps, 1)
                    if on(2):
                        await_tiles(pe, h_sb, g - 1)
                        stages["turn"](ps[4 + q % 2], hs[q % 2]).then_inc(hT_ps, 1)
                    if on(3):
                        await_tiles(pe, hT_sb, g - 2)
                        if not early(g, 5):
                            await_tiles(pe, y_sb, g - 4)
                        stages["down"](expert(3), ps[6 + (q + 1) % 2], hT[(q + 1) % 2]).then_inc(y_ps, 1)
                run(pe, step, mybir.EngineType.PE, (1, 3))

            def scalar(act):
                def step(g, q, rounds, on, expert):
                    if on(0):
                        await_tiles(act, xT_ps, g + 1)
                        if not early(g, 2):
                            await_tiles(act, h_ps, g - 1)
                        nc.scalar.activation(xT[q % 2], ps[q % 2][:, 0:HID], ACT.Copy).then_inc(xT_sb, 1)
                    if stages["act_mid"] and on(1):
                        await_tiles(act, h_ps, g)
                        if not early(g, 3):
                            await_tiles(act, hT_ps, g - 2)
                        stages["act_mid"](ps[2 + (q + 1) % 2], hs[(q + 1) % 2]).then_inc(mid, 1)
                    if on(2):
                        await_tiles(act, hT_ps, g - 1)
                        if not early(g, 4):
                            await_tiles(act, y_ps, g - 3)
                        stages["act_turn"](expert(2), ps[4 + q % 2], hT[q % 2], hT_sb)
                    if on(3):
                        if not stages["dve_mid"]:
                            await_tiles(act, y_ps, g - 2)
                            if not early(g, 5):
                                await_dma(act, stq[(q + 1) % 2], rounds(2, 3) * 16, 2)
                            nc.scalar.activation(yt[(q + 1) % 2], ps[6 + (q + 1) % 2][:, 0:HID], ACT.Copy).then_inc(y_sb, 1)
                        await_tiles(act, y_sb, g - 2)
                        act.dma_start(ys[bass.ds((g - 3) * P, P), :], yt[(q + 1) % 2]).then_inc(stq[(q + 1) % 2], 16)
                run(act, step, mybir.EngineType.Activation, (2,) if stages["bias"] else ())
                await_dma(act, stq[0], 16 * (ntile // 2), 2)
                await_dma(act, stq[1], 16 * (ntile // 2), 2)

            def vector(dve):
                def step(g, q, rounds, on, expert):
                    if on(1):
                        await_tiles(dve, h_ps, g)
                        if not early(g, 3):
                            await_tiles(dve, hT_ps, g - 2)
                        stages["dve_mid"](ps[2 + (q + 1) % 2], hs[(q + 1) % 2]).then_inc(h_sb, 1)
                    if on(3):
                        await_tiles(dve, y_ps, g - 2)
                        if not early(g, 5):
                            await_dma(dve, stq[(q + 1) % 2], rounds(2, 3) * 16, 2)
                        nc.vector.tensor_copy(yt[(q + 1) % 2], ps[6 + (q + 1) % 2][:, 0:HID]).then_inc(y_sb, 1)
                run(dve, step)
            return sync, tensor, scalar, vector

        def up0(e, bank, xt):
            w = rw3[:, bass.ds(e, 1), :]
            for k in range(KC):
                ins = nc.tensor.matmul(bank[:, 0:DH], xt[:, k * P:(k + 1) * P], w[:, 0, k * DH:(k + 1) * DH],
                                       start=(k == 0), stop=(k == KC - 1))
            return ins

        def turn0(bank, h):
            nc.tensor.transpose(bank[:, 0:P], h[:, 0:P], IDN[:, :])
            return nc.tensor.transpose(bank[0:DHB, P:2 * P], h[:, P:DH], IDN[:, :])

        def act_turn0(e, bank, hT, done):
            nc.scalar.activation(hT[:, 0:P], bank[:, 0:P], ACT.Relu, bias=B1A[:, bass.ds(e, 1)])
            nc.scalar.activation(hT[0:DHB, P:2 * P], bank[0:DHB, P:2 * P], ACT.Relu, bias=B1B[:, bass.ds(e, 1)]).then_inc(done, 1)

        def down0(e, bank, hT):
            w = rw3[:, bass.ds(e, 1), :]
            nc.tensor.matmul(bank[:, 0:HID], hT[:, 0:P], w[:, 0, W2A:W2B], start=True, stop=False)
            return nc.tensor.matmul(bank[:, 0:HID], hT[0:DHB + 1, P:2 * P], w[0:DHB + 1, 0, W2B:EW0], start=False, stop=True)

        ones_set = sem("ones_set")
        with nc.Block() as block:
            @block.gpsimd
            def _(pool):
                for i in range(2):
                    nc.gpsimd.memset(TA[32:64, (8 + i) * HID + P:(9 + i) * HID], 1.0).then_inc(ones_set, 1)
                    pool.wait_ge(ones_set, i + 1)

        parts0 = expert_parts(0, NT0, xs0, ys0, [(ld_ex, 16 * 6), (ld_ex2, 16 * 15)], scat0, 16 * NT * K0,
                     dict(E=E0, up=up0, turn=turn0, down=down0, act_mid=None, bias=True, act_turn=act_turn0,
                          dve_mid=lambda bank, h: nc.vector.tensor_copy(h[:, 0:DH], bank[:, 0:DH])))
        with nc.Block() as block:
            @block.sync
            def _(sp):
                parts0[0](sp)

            @block.tensor
            def _(pe):
                parts0[1](pe)

            @block.scalar
            def _(act):
                parts0[2](act)

            @block.vector
            def _(dve):
                parts0[3](dve)

        base = E1 * EW1
        o1 = base

        def cut1(n):
            nonlocal o1
            o1 += n
            return RW[:, o1 - n:o1]
        PB = cut1(TPB * H * NKEY).rearrange("p (j h n) -> p j h n", j=TPB, h=H)
        QB = [cut1(H * D) for _ in range(2)]
        QTB = [cut1(4 * P) for _ in range(2)]
        PTB = [cut1(4 * P) for _ in range(2)]
        AOB = [cut1(4 * P) for _ in range(2)]
        WR1 = cut1(6 * HID)
        BQKV, BO, RBD = SW2[:, 0:2 * HID], SW2[:, 2 * HID:3 * HID], SW2[:, 3 * HID:3 * HID + HKV * R1]
        RBT = SW2[0:HKV * R1, 3 * HID + P:3 * HID + 2 * P]
        YG = [XN[:, j * K0 * HID:(j + 1) * K0 * HID] for j in range(2)]
        NSW = [P, P + WIN]
        gates0 = v3(GATE[:, :], NT)
        rw13 = v3(RW[:, 0:base], E1)

        ld_e1, ld_w1, ld_s1, ld_r1, rb_zero = (sem(n) for n in ("ld_experts1", "ld_attn1", "ld_small1", "ld_rand1", "rand_zero"))
        zero1 = sem("zero1_done")
        dve2p, dve2l, dve2e = sem("dve2_head"), sem("dve2_loop"), sem("dve2_tail")
        es_ok = sem("sink_exp")
        (qcs_ok, v_ok, v_half, q_ps, q_ev, qss, qpow, q_mul, q_rot, qn, t_ps, t_sb, s_ps, th, s_ev, e_sb, pn, csub, cexp, cn,
         pt_ps, pt_sb, pv_ps, ao_sb, opg, op_sb, idx_ok, comb) = (
            sem("a_" + n) for n in (
                "qc_copied", "values_copied", "values_half", "q_psum", "q_sbuf", "q_squares", "q_mean", "q_products", "q_rotated", "q_normed",
                "qT_psum", "qT_sbuf", "scores_psum", "tanh", "scores_read", "exp", "probs", "blocks_sub", "blocks_exp",
                "blocks_probs", "pT_psum", "pT_sbuf", "out_psum", "out_sbuf", "proj_group", "proj_read", "slots_tile",
                "combined"))
        gat = [sem(f"a_gathered{j}") for j in range(TPB)]
        NSTEP = NT + 3

        def wait(eng, s, n):
            if not isinstance(n, int) or n > 0:
                eng.wait_ge(s, n)

        def run_attention(eng, step):
            def outside(g, section):
                step(g, g % 2, lambda lag: (g - lag) // 2, lambda lag: 0 <= g - lag < NT, section)
            for g in range(-1, 4):
                outside(g, (0, 0))
            with eng.Fori(0, (NT - 4) // 2) as i:
                for c in range(4, 6):
                    step(i * 2 + c, c % 2, lambda lag: i + (c - lag) // 2, lambda lag: True, (1, i))
            for g in range(NT, NSTEP):
                outside(g, (2, 0))

        with nc.Block() as block:
            @block.sync
            def _(sp):
                for e in range(E1):
                    w = rw13[:, e, :]
                    for k in range(KC):
                        for m, n in enumerate(("L1_ffn_wi_0", "L1_ffn_wi_1")):
                            sp.dma_start(w[:, (2 * k + m) * MI:(2 * k + m + 1) * MI], a[n][e, k * P:(k + 1) * P, :]).then_inc(ld_e1, 16)
                        sp.dma_start(w[:, 2 * KC * MI + k * HID:2 * KC * MI + (k + 1) * HID],
                                     a["L1_ffn_wo"][e, k * P:(k + 1) * P, :]).then_inc(ld_e1, 16)
                for i, (n, r) in enumerate((("Wq", 0), ("Wq", P), ("Wk", 0), ("Wv", 0), ("Wo", 0), ("Wo", P))):
                    sp.dma_start(WR1[:, i * HID:(i + 1) * HID], a["L1_attn_" + n][r:r + P, :]).then_inc(ld_w1, 16)
                sp.dma_start(v3(RTW[:, 0:KC * E1], KC), a["L1_ffn_gate_kernel"].rearrange("(k p) e -> p k e", p=P)).then_inc(ld_s1, 16)
                for n, lo, w in (("bq", 0, HID), ("bk", HID, P), ("bv", HID + P, P)):
                    sp.dma_start(BQKV[:, lo:lo + w], a["L1_attn_" + n].partition_broadcast(P)).then_inc(ld_s1, 16)
                sp.dma_start(BO, a["L1_attn_bo"].partition_broadcast(P)).then_inc(ld_s1, 16)
                sp.wait_ge(rb_zero, 1)
                for h in range(HKV):
                    sp.dma_start(RBT[h * R1:(h + 1) * R1, h * D1:(h + 1) * D1], a["L1_attn_rand_matrix"]).then_inc(ld_r1, 16)

            @block.gpsimd
            def _(pool):
                qcs = v3(QCS[:, :], TPB)
                vown = v3(VOWN[:, :], TPB)
                cos, sin = (v3(ROPE0[:, i * TPB * HR:(i + 1) * TPB * HR], TPB) for i in range(2))
                tmp = [v3(TA[:, i * H * HR:(i + 1) * H * HR], H) for i in range(4)]
                nc.gpsimd.memset(RBT, 0.0).then_inc(rb_zero, 1)

                def step(g, j, batch, on, section):
                    ja = 1 - j
                    if on(2):
                        wait(pool, gat[ja], (batch(3) + 1) * (16 * K0))
                        nc.gpsimd.tensor_copy(IDX[:, :], SLOT[:, bass.ds((g - 2) * K0, K0)]).then_inc(idx_ok, 1)
                        pool.wait_ge(idx_ok, g - 1)
                        wait(pool, comb, g - 3)
                    if on(1):
                        wait(pool, pv_ps, (g - 2) * NPAIR)
                        nc.gpsimd.tensor_copy(vown[:, ja, :], VA[:, bass.ds((g - 1) * D, D)]).then_inc(v_half, 1)
                        if ja:
                            nc.gpsimd.tensor_copy(V2[:, :], V2A[:, bass.ds(batch(1) * D, D)]).then_inc(v_ok, 1)
                        else:
                            nc.gpsimd.tensor_copy(CKS[:, :], CK0[:, bass.ds(batch(1) * D, D)]).then_inc(v_ok, 1)
                    if on(-1):
                        wait(pool, q_ps, g * NG)
                        nc.gpsimd.tensor_copy(qcs[:, ja, :], QCT[:, bass.ds((g + 1) * P, P)]).then_inc(qcs_ok, 1)
                    if on(0):
                        pool.wait_ge(qss, g + 1)
                        wait(pool, qn, g)
                        nc.gpsimd.tensor_tensor(RR[:, :], RR[:, :], MHALF[:, 0:H], ALU.pow).then_inc(qpow, 1)
                        q3 = v3(QB[j], H)
                        x1, x2 = q3[:, :, 0:HR], q3[:, :, HR:ROPE]
                        c, s = (bc(t[:, j, :].unsqueeze(1), [P, H, HR]) for t in (cos, sin))
                        for i, (x, w) in enumerate(((x1, c), (x2, s), (x1, s), (x2, c))):
                            nc.gpsimd.tensor_tensor(tmp[i], x, w, ALU.mult).then_inc(q_mul, 1)
                        pool.wait_ge(q_mul, g * 4 + 4)
                        nc.gpsimd.tensor_tensor(x1, tmp[0], tmp[1], ALU.subtract).then_inc(q_rot, 1)
                        nc.gpsimd.tensor_tensor(x2, tmp[2], tmp[3], ALU.add).then_inc(q_rot, 1)
                    if on(2):
                        for k in range(K0):
                            nc.gpsimd.indirect_dma_start(YG[j][:, k * HID:(k + 1) * HID], None, ys0,
                                                         bass.IndirectOffsetOnAxis(ap=IDX[:, k:k + 1], axis=0)).then_inc(gat[j], 16)
                run_attention(pool, step)

            @block.tensor
            def _(pe):
                wq3 = v3(WQ[:, :], NG)
                qcs = v3(QCS[:, :], TPB)
                vown = v3(VOWN[:, :], TPB)

                def step(g, j, batch, on, section):
                    ja = 1 - j

                    def queries(k):
                        if on(-1):
                            pe.wait_ge(qcs_ok, g + 2)
                            wait(pe, q_ev, (g + 1) * NG + k)
                            nc.tensor.matmul(ps[0][:, :], qcs[:, ja, :], wq3[:, k, :], start=True, stop=True).then_inc(q_ps, 1)

                    def turn_queries(k):
                        if on(1):
                            pe.wait_ge(qn, g)
                            wait(pe, t_sb, (g - 1) * NG + k)
                            q3 = v3(QB[ja], H)
                            for h in range(4):
                                ins = nc.tensor.transpose(ps[1][:, h * P:(h + 1) * P], q3[:, 4 * k + h, :], IDN[:, :])
                            ins.then_inc(t_ps, 1)

                    def scores(p):
                        if on(1):
                            pe.wait_ge(t_sb, (g - 1) * NG + (p // 2 + 1))
                            wait(pe, s_ev, (g - 1) * NPAIR + (p - 1))
                            n = NSW[ja] + NB
                            keys = KCAT[:, bass.ds(batch(1) * KROW + (P + NB if ja else 0), n)]
                            for i in range(2):
                                h = 2 * p + i
                                ins = nc.tensor.matmul(ps[2 + p % 2][:, i * NKEY:i * NKEY + n],
                                                       QTB[h // 4 % 2][:, h % 4 * P:(h % 4 + 1) * P], keys, start=True, stop=True)
                            ins.then_inc(s_ps, 1)

                    def turn_probs(p):
                        if on(2):
                            pe.wait_ge(pn, (g - 2) * NPAIR + (p + 1))
                            pe.wait_ge(cn, (g - 2) * 2 + (p // 4 + 1))
                            wait(pe, pt_sb, (g - 2) * NPAIR + (p - 1))
                            n = NSW[j] + NB
                            for i in range(2):
                                nc.tensor.transpose(ps[4 + p % 2][:, i * P:(i + 1) * P], PB[:, j, 2 * p + i, 0:P], IDN[:, :])
                                ins = nc.tensor.transpose(ps[4 + p % 2][0:n - P, (2 + i) * P:(3 + i) * P],
                                                          PB[:, j, 2 * p + i, P:n], IDN[:, :])
                            ins.then_inc(pt_ps, 1)

                    def values(p):
                        if on(2):
                            pe.wait_ge(v_ok, g - 1)
                            pe.wait_ge(v_half, g - 1)
                            pe.wait_ge(pt_sb, (g - 2) * NPAIR + (p + 1))
                            if p % 2 == 0:
                                wait(pe, ao_sb, (g - 2) * NG + p // 2)
                            n = NSW[j] + NB - P
                            for i in range(2):
                                o = ps[6][:, (2 * p + i) % 4 * P:((2 * p + i) % 4 + 1) * P]
                                nc.tensor.matmul(o, vown[:, j, :], PTB[p % 2][:, i * P:(i + 1) * P], start=True, stop=False)
                                ins = nc.tensor.matmul(o, V2[:, :] if j else CKS[:, :], PTB[p % 2][0:n, (2 + i) * P:(3 + i) * P],
                                                       start=False, stop=True)
                            ins.then_inc(pv_ps, 1)

                    def project(k):
                        if on(2):
                            pe.wait_ge(ao_sb, (g - 2) * NG + (k + 1))
                            if k == 0:
                                wait(pe, op_sb, g - 2)
                            for h in range(4):
                                ins = nc.tensor.matmul(ps[7][:, 0:HID], AOB[k % 2][:, h * P:(h + 1) * P], wc3[:, 4 * k + h, :],
                                                       start=(k + h == 0), stop=(k == NG - 1 and h == 3))
                            ins.then_inc(opg, 1)

                    turn_queries(0)
                    for p in range(NPAIR):
                        if p % 2 == 0 and p // 2 + 1 < NG:
                            turn_queries(p // 2 + 1)
                        scores(p)
                        turn_probs(p)
                        if p >= NPAIR - NG:
                            queries(p - (NPAIR - NG))
                        if p >= 1:
                            values(p - 1)
                        if p >= 3 and p % 2:
                            project((p - 3) // 2)
                    values(NPAIR - 1)
                    project(NG - 1)
                run_attention(pe, step)

            @block.scalar
            def _(act):
                for i in range(NT1 // 4):
                    act.dma_start(xs1[i * 4 * P:(i + 1) * 4 * P, :].rearrange("(c p) d -> p c d", p=P),
                                  bc(ZERO[:, :].unsqueeze(1), [P, 4, HID])).then_inc(zero1, 16)
                nc.scalar.activation(SINK[:, 3 * H:], SINK[:, 2 * H:3 * H], ACT.Exp).then_inc(es_ok, 1)

                def step(g, j, batch, on, section):
                    ja = 1 - j
                    nsw = NSW[ja]

                    def queries(k):
                        if on(-1):
                            act.wait_ge(q_ps, (g + 1) * NG + (k + 1))
                            wait(act, t_ps, g * NG)
                            nc.scalar.activation(QB[ja][:, k * 512:(k + 1) * 512], ps[0][:, :], ACT.Copy).then_inc(q_ev, 1)

                    def probs(p):
                        if on(1):
                            act.wait_ge(s_ps, (g - 1) * NPAIR + (p + 1))
                            wait(act, pt_ps, (g - 3) * NPAIR + (p + 1))
                            sc = v3(ps[2 + p % 2][:, 0:2 * NKEY], 2)
                            pb = PB[:, ja, 2 * p:2 * p + 2, :]
                            nc.scalar.activation(pb[:, :, 0:nsw], sc[:, :, 0:nsw], ACT.Tanh, scale=SCALE / CAP).then_inc(th, 1)
                            nc.scalar.activation(pb[:, :, nsw:nsw + NB], sc[:, :, nsw:nsw + NB], ACT.Copy, scale=SCALE).then_inc(s_ev, 1)
                            act.wait_ge(th, (g - 1) * NPAIR + (p + 1))
                            for i in range(2):
                                h = 2 * p + i
                                ins = nc.scalar.activation(pb[:, i, 0:nsw], pb[:, i, 0:nsw], ACT.Exp, scale=CAP, bias=SINK[:, H + h:H + h + 1])
                            ins.then_inc(e_sb, 1)

                    def probs_T(p):
                        if on(2):
                            act.wait_ge(pt_ps, (g - 2) * NPAIR + (p + 1))
                            wait(act, pv_ps, (g - 2) * NPAIR + (p - 1))
                            n = NSW[j] + NB - P
                            nc.scalar.activation(PTB[p % 2][:, 0:2 * P], ps[4 + p % 2][:, 0:2 * P], ACT.Copy)
                            nc.scalar.activation(PTB[p % 2][0:n, 2 * P:], ps[4 + p % 2][0:n, 2 * P:], ACT.Copy).then_inc(pt_sb, 1)

                    def outs(k):
                        if on(2):
                            act.wait_ge(pv_ps, (g - 2) * NPAIR + (2 * k + 2))
                            wait(act, opg, (g - 2) * NG + (k - 1))
                            nc.scalar.activation(AOB[k % 2], ps[6][:, :], ACT.Copy).then_inc(ao_sb, 1)

                    def blocks(half):
                        if on(1):
                            act.wait_ge(csub, (g - 1) * 2 + (half + 1))
                            cb = PB[:, ja, 8 * half:8 * half + 8, nsw:nsw + NB]
                            nc.scalar.activation(cb, cb, ACT.Exp)
                            nc.scalar.activation(CM[:, 24:32], CM[:, 16:24], ACT.Exp).then_inc(cexp, 1)

                    for p in range(NPAIR):
                        probs(p)
                        probs_T(p)
                        if p >= NPAIR - NG:
                            queries(p - (NPAIR - NG))
                        if p >= 2 and p % 2 == 0:
                            outs(p // 2 - 1)
                        if p == 6:
                            blocks(0)
                    outs(NG - 1)
                    blocks(1)
                run_attention(act, step)
                act.wait_ge(zero1, 16 * (NT1 // 4))

            @block.vector
            def _(dve):
                PER_STEP = NPAIR * 4 + 2 * 6 + H + (K0 - 1)
                sections = {}

                def step(g, j, batch, on, section):
                    kind, i = section
                    if kind not in sections:
                        sections[kind] = Steps(dve, (dve2p, dve2l, dve2e)[kind], i * (2 * PER_STEP) if kind == 1 else 0)
                    st = sections[kind]
                    ja = 1 - j
                    nsw = NSW[ja]

                    def queries_T(k):
                        if on(1):
                            dve.wait_ge(t_ps, (g - 1) * NG + (k + 1))
                            wait(dve, s_ps, (g - 1) * NPAIR + (2 * k - 2))
                            nc.vector.tensor_copy(QTB[k % 2], ps[1][:, :]).then_inc(t_sb, 1)

                    def norm(p):
                        if on(1):
                            dve.wait_ge(e_sb, (g - 1) * NPAIR + (p + 1))
                            hs = slice(2 * p, 2 * p + 2)
                            for h in range(2 * p, 2 * p + 2):
                                pb = PB[:, ja, h, 0:nsw]
                                st(nc.vector.scalar_tensor_tensor(out=pb, in0=pb, scalar=1.0, in1=WINDOW[:, 0:nsw], op0=ALU.mult,
                                                                  op1=ALU.mult, accum_out=LSUM[:, h:h + 1]))
                            st.wait()
                            st.link(nc.vector.tensor_tensor(LSUM[:, H + 2 * p:H + 2 * p + 2], LSUM[:, hs],
                                                            SINK[:, 3 * H + 2 * p:3 * H + 2 * p + 2], ALU.add))
                            st.link(nc.vector.reciprocal(LSUM[:, 2 * H + 2 * p:2 * H + 2 * p + 2], LSUM[:, H + 2 * p:H + 2 * p + 2]))
                            for h in range(2 * p, 2 * p + 2):
                                pb = PB[:, ja, h, 0:nsw]
                                ins = nc.vector.tensor_scalar(pb, pb, LSUM[:, 2 * H + h:2 * H + h + 1], None, ALU.mult)
                            ins.then_inc(pn, 1)

                    def blocks_sub(half):
                        if on(1):
                            dve.wait_ge(s_ev, (g - 1) * NPAIR + (4 * half + 4))
                            cb = PB[:, ja, 8 * half:8 * half + 8, nsw:nsw + NB]
                            sk = SINK[:, 8 * half:8 * half + 8]
                            st.link(nc.vector.tensor_tensor(cb, cb, bc(v3(BLOCKS[:, :], TPB)[:, ja, :].unsqueeze(1), [P, 8, NB]), ALU.add))
                            st.link(nc.vector.reduce_max(CM[:, 0:8], cb, AX))
                            st.link(nc.vector.tensor_tensor(CM[:, 8:16], CM[:, 0:8], sk, ALU.max))
                            nc.vector.tensor_tensor(CM[:, 16:24], sk, CM[:, 8:16], ALU.subtract)
                            nc.vector.tensor_tensor(cb, cb, bc(CM[:, 8:16].unsqueeze(2), [P, 8, NB]), ALU.subtract).then_inc(csub, 1)

                    def blocks_norm(half):
                        if on(1):
                            dve.wait_ge(cexp, (g - 1) * 2 + (half + 1))
                            cb = PB[:, ja, 8 * half:8 * half + 8, nsw:nsw + NB]
                            st.link(nc.vector.reduce_sum(CM[:, 32:40], cb, AX))
                            st.link(nc.vector.tensor_tensor(CM[:, 40:48], CM[:, 32:40], CM[:, 24:32], ALU.add))
                            st.link(nc.vector.reciprocal(CM[:, 48:56], CM[:, 40:48]))
                            nc.vector.tensor_tensor(cb, cb, bc(CM[:, 48:56].unsqueeze(2), [P, 8, NB]), ALU.mult).then_inc(cn, 1)

                    def squares():
                        if on(0):
                            dve.wait_ge(q_ev, g * NG + NG)
                            wait(dve, qn, g)
                            q3 = v3(QB[j], H)
                            for h in range(H):
                                ins = nc.vector.scalar_tensor_tensor(out=TA[:, h * D:(h + 1) * D], in0=q3[:, h, :], scalar=1.0,
                                                                     in1=q3[:, h, :], op0=ALU.mult, op1=ALU.mult, accum_out=SSQ[:, h:h + 1])
                                st(ins)
                            st.wait()
                            nc.vector.tensor_scalar(RR[:, :], SSQ[:, :], 1.0 / D, RMS_EPS, ALU.mult, ALU.add).then_inc(qss, 1)

                    def query_norm():
                        if on(0):
                            dve.wait_ge(qpow, g + 1)
                            dve.wait_ge(q_rot, g * 2 + 2)
                            q3 = v3(QB[j], H)
                            nc.vector.tensor_tensor(q3, q3, bc(RR[:, :].unsqueeze(2), [P, H, D]), ALU.mult).then_inc(qn, 1)

                    def take_out():
                        if on(3):
                            x = X[:, bass.ds((g - 3) * HID, HID)]
                            dve.wait_ge(opg, (g - 3) * NG + NG)
                            nc.vector.tensor_tensor(x, ps[7][:, 0:HID], x, ALU.add).then_inc(op_sb, 1)

                    def combine():
                        if on(3):
                            x = X[:, bass.ds((g - 3) * HID, HID)]
                            dve.wait_ge(op_sb, g - 2)
                            dve.wait_ge(gat[ja], (batch(3) + 1) * (16 * K0))
                            for k in range(K0):
                                ins = nc.vector.scalar_tensor_tensor(out=x, in0=YG[ja][:, k * HID:(k + 1) * HID],
                                                                     scalar=GATE[:, bass.ds((g - 3) * K0 + k, 1)], in1=x,
                                                                     op0=ALU.mult, op1=ALU.add)
                                if k < K0 - 1:
                                    st.link(ins)
                            ins.then_inc(comb, 1)

                    queries_T(0)
                    squares()
                    for p in range(NPAIR):
                        if p % 2 == 0 and p // 2 + 1 < NG:
                            queries_T(p // 2 + 1)
                        if p == 1:
                            take_out()
                        if p >= 1:
                            norm(p - 1)
                        if p == 4:
                            combine()
                        if p == 6:
                            query_norm()
                        if p == 5:
                            blocks_sub(0)
                        if p == 7:
                            blocks_norm(0)
                    norm(NPAIR - 1)
                    blocks_sub(1)
                    blocks_norm(1)
                    if kind == 1 and j == 1:
                        assert st.n == 2 * PER_STEP, (st.n, PER_STEP)
                dve.wait_ge(es_ok, 1)
                run_attention(dve, step)

        o1 = base
        NHK = H1 + HKV
        HF1 = NHK * D1
        QKV = cut1(NT * 2 * HID)
        WT1 = cut1(KC * 2 * HID)
        WOT = cut1(KC * HID)
        TURN = cut1(NT * HF1)
        VOUT = cut1(NT * HID)
        FEAT = cut1(NT * HF1)
        ANG = cut1(NT * NHK * R1)
        assert ANG.shape == WR1.shape and o1 <= E0 * EW0
        SSN, RNORM = SW1[:, 0:NT * NHK], SW1[:, NT * NHK:2 * NT * NHK]
        MEET = [SW1[:, 2 * NT * NHK + i * P:2 * NT * NHK + (i + 1) * P] for i in range(2)]
        DT = [KCAT[:, i * 3 * P:(i + 1) * 3 * P] for i in range(2)]
        OT = [VA[:, i * HID:(i + 1) * HID] for i in range(2)]
        RNT = VA[:, 2 * HID:2 * HID + NT * NHK]
        NPR = H1 * HKV * D1
        PRF = [xnT[:, 0:NPR], TURN[:, 0:NPR]]
        PRD = WC[:, NPR:2 * NPR]
        VIN = WC[:, 0:NT * HID]
        hst, hld = sem("b_heads_stored"), [sem(f"b_heads_loaded{b}") for b in range(B)]
        fgat = [sem(f"f_gathered{b}") for b in range(B)]
        f_ok, f_st = sem("f_combined"), sem("f_stored")
        qkv3 = v3(QKV, NT)

        (dve3, dve3l, dve3e, x1t_ps, x1t_sb, lg1_ps, wt1_ps, wt1_sb, qkv_ps, qkv_sb,
         scat1, d_ok, sq_ok, ssum, root, dT_ps, dT_sb, u_ps, u_sb, u_ok, sin_ok,
         prf_ok, prf_rd, o_ok, bo_ok, oT_ps, oT_sb, ao_ps, ao_rd) = (
            sem("b_" + n) for n in (
                "dve", "dve_loop", "dve_tail", "xT_psum", "xT_sbuf", "logits",
                "wT_psum", "wT_sbuf", "qkv_psum", "qkv_sbuf", "scatter",
                "rotated", "squares", "square_sums", "roots", "dT_psum", "dT_sbuf", "angles_psum", "angles_sbuf", "turns",
                "features", "products", "products_read", "outs", "bias_added", "oT_psum", "oT_sbuf", "proj", "proj_read"))

        def up1(e, bank, xt):
            w = rw13[:, bass.ds(e, 1), :]
            for k in range(KC):
                ins = nc.tensor.matmul(bank[:, :], xt[:, k * P:(k + 1) * P], w[:, 0, k * 2 * MI:(k + 1) * 2 * MI],
                                       start=(k == 0), stop=(k == KC - 1))
            return ins

        def turn1(bank, h):
            for k in range(KC):
                ins = nc.tensor.transpose(bank[:, k * P:(k + 1) * P], h[:, k * P:(k + 1) * P], IDN[:, :])
            return ins

        def act_turn1(e, bank, hT, done):
            nc.scalar.activation(hT, bank[:, 0:MI], ACT.Copy).then_inc(done, 1)

        def down1(e, bank, hT):
            w = rw13[:, bass.ds(e, 1), :]
            for k in range(KC):
                ins = nc.tensor.matmul(bank[:, 0:HID], hT[:, k * P:(k + 1) * P],
                                       w[:, 0, 2 * KC * MI + k * HID:2 * KC * MI + (k + 1) * HID], start=(k == 0), stop=(k == KC - 1))
            return ins

        parts1 = expert_parts(NT0, NT1, xs1, ys1, [(ld_e1, 16 * 3 * KC * E1)], scat1, 16 * NT * K1,
                              dict(E=E1, up=up1, turn=turn1, down=down1, bias=False, act_turn=act_turn1, dve_mid=None,
                                   act_mid=lambda bank, h: nc.scalar.activation(h, bank[:, 0:MI], ACT.Silu)))

        with nc.Block() as block:
            @block.sync
            def _(sp):
                parts1[0](sp)
                for b in range(B):
                    for j in range(TPB):
                        t = b * TPB + j
                        sp.wait_ge(o_ok, t + 1)
                        sp.dma_start(heads1[t * P:(t + 1) * P, :], VOUT[:, t * HID:(t + 1) * HID]).then_inc(hst, 16)
                    sp.wait_ge(hst, 16 * TPB * (b + 1))
                    for j in range(TPB):
                        t = b * TPB + j
                        hh = H1 // TPB
                        src = heads1[b * S:(b + 1) * S, j * hh * D1:(j + 1) * hh * D1].rearrange("(g l) (h d) -> h g l d", l=H1, d=D1)
                        sp.dma_start(VIN[:, t * HID:(t + 1) * HID].rearrange("p (l d) -> p l d", l=H1), src).then_inc(hld[b], 16)
                rows = out.rearrange("b (j p) d -> (b j) p d", p=P)
                for t in range(NT):
                    sp.wait_ge(f_ok, t + 1)
                    sp.dma_start(rows[t], x3[:, t, :]).then_inc(f_st, 16)
                sp.wait_ge(f_st, 16 * NT)

            @block.gpsimd
            def _(pool):
                layernorm_pool(pool, 1)
                pool.wait_ge(slots_ok, 3)
                for t in range(NT):
                    for k in range(K1):
                        nc.gpsimd.indirect_dma_start(
                            xs1, bass.IndirectOffsetOnAxis(ap=SLOT[:, t * K1 + k:t * K1 + k + 1], axis=0),
                            xn3[:, t, :], None).then_inc(scat1, 16)
                ft = FEAT.rearrange("p (t n f) -> p t n f", t=NT, n=NHK)
                for t in range(NT):
                    pool.wait_ge(sin_ok, 1 if t == 0 else NT // 2)
                    wait(pool, prf_rd, t - 1)
                    nc.gpsimd.tensor_tensor(PRF[t % 2].rearrange("p (h k f) -> p h k f", h=H1, k=HKV),
                                            bc(ft[:, t, 0:H1].unsqueeze(2), [P, H1, HKV, D1]),
                                            bc(ft[:, t, H1:].unsqueeze(1), [P, H1, HKV, D1]), ALU.mult).then_inc(prf_ok, 1)
                pool.wait_ge(ld_s1, 16 * 5)
                for t in range(NT):
                    nc.gpsimd.tensor_tensor(x3[:, t, :], x3[:, t, :], BO, ALU.add).then_inc(bo_ok, 1)
                for s in tile_sems[1]:
                    pool.wait_ge(s, 16 * (NT0 + NT1) // 2)
                pool.wait_ge(prf_rd, NT)
                for t in range(NT):
                    for k in range(K1):
                        i = t * K1 + k
                        nc.gpsimd.indirect_dma_start(XN[:, i * HID:(i + 1) * HID], None, ys1,
                                                     bass.IndirectOffsetOnAxis(ap=SLOT[:, i:i + 1], axis=0)).then_inc(fgat[t // TPB], 16)

            @block.scalar
            def _(act):
                act.wait_ge(wt1_ps, 1)
                for k in range(KC):
                    nc.scalar.activation(WT1[:, k * 2 * HID:(k + 1) * 2 * HID], ps[2 + k][:, :], ACT.Copy).then_inc(wt1_sb, 1)
                nc.scalar.activation(WOT, ps[4][:, :], ACT.Copy).then_inc(wt1_sb, 1)
                nc.scalar.activation(RBD, ps[5][:, 0:HKV * R1], ACT.Copy).then_inc(wt1_sb, 1)
                for t in range(NT):
                    act.wait_ge(x1t_ps, t + 1)
                    nc.scalar.activation(xnT3[:, :, t * P:(t + 1) * P], v3(ps[t % 2][:, 0:HID], KC), ACT.Copy).then_inc(x1t_sb, 1)
                act.wait_ge(gates_sub, 2)
                nc.scalar.activation(GATE[:, 0:NT * K1], GATE[:, 0:NT * K1], ACT.Exp).then_inc(gates_exp, 1)

                def angles_out(i):
                    act.wait_ge(u_ps, 2 * i + 2)
                    n = 2 * NHK * R1
                    nc.scalar.activation(ANG[:, i * n:(i + 1) * n], ps[2 + i][:, 0:n], ACT.Copy).then_inc(u_sb, 1)
                for t in range(NT):
                    act.wait_ge(d_ok, t + 1)
                    nc.scalar.activation(TURN[:, t * HF1:(t + 1) * HF1], qkv3[:, t, 0:HF1], ACT.Square).then_inc(sq_ok, 1)
                    act.wait_ge(dT_ps, t + 1)
                    wait(act, u_ps, t - 1)
                    nc.scalar.activation(DT[t % 2], ps[t % 2][:, 0:3 * P], ACT.Copy).then_inc(dT_sb, 1)
                    if t >= 2 and t % 2 == 0:
                        angles_out(t // 2 - 1)
                angles_out(NT // 2 - 1)
                act.wait_ge(ssum, 1)
                nc.scalar.activation(RNORM, SSN, ACT.Sqrt).then_inc(root, 1)
                for i in range(NT // 2):
                    act.wait_ge(u_ok, i + 1)
                    f = FEAT[:, i * 2 * HF1:(i + 1) * 2 * HF1]
                    nc.scalar.activation(f, f, ACT.Sin, scale=2 * 3.1415925).then_inc(sin_ok, 1)
                parts1[2](act)
                for t in range(NT):
                    act.wait_ge(oT_ps, t + 1)
                    wait(act, ao_ps, t - 1)
                    nc.scalar.activation(OT[t % 2], ps[4 + t % 2][:, 0:HID], ACT.Copy).then_inc(oT_sb, 1)

            @block.vector
            def _(dve):
                st = Steps(dve, dve3)
                layernorm_dve(dve, st, 1)
                dve.wait_ge(lg1_ps, 1)
                st.link(nc.vector.tensor_copy(LOGIT[:, 0:NT * E1], ps[2][:, 0:NT * E1]))
                route_dve(dve, st, E1, K1)
                route_dve_slots(dve, st, E1, K1, NT1, ps[3], 1)
                dve.wait_ge(ld_s1, 16 * 5)
                hd = D1 // 2
                cos, sin = (v3(ROPE1[:, i * TPB * hd:(i + 1) * TPB * hd], TPB) for i in range(2))
                nt4 = NHK * hd

                def take_qkv(t):
                    dve.wait_ge(qkv_ps, t + 1)
                    nc.vector.tensor_tensor(qkv3[:, t, :], ps[4 + t % 4][:, :], BQKV, ALU.add).then_inc(qkv_sb, 1)

                def rotate(t):
                    dve.wait_ge(qkv_sb, t + 1)
                    q = v3(qkv3[:, t, 0:HF1], NHK)
                    y1, y2 = q[:, :, 0:hd], q[:, :, hd:]
                    tmp = [v3(FEAT[:, i * nt4:(i + 1) * nt4], NHK) for i in range(4 * (t % 4), 4 * (t % 4) + 4)]
                    c, s = (bc(w[:, t % TPB, :].unsqueeze(1), [P, NHK, hd]) for w in (cos, sin))
                    for i, (y, w) in enumerate(((y1, c), (y2, s), (y1, s), (y2, c))):
                        st(nc.vector.tensor_tensor(tmp[i], y, w, ALU.mult))
                    st.wait()
                    st(nc.vector.tensor_tensor(y1, tmp[0], tmp[1], ALU.subtract))
                    nc.vector.tensor_tensor(y2, tmp[3], tmp[2], ALU.add).then_inc(d_ok, 1)
                take_qkv(0)
                for t in range(NT):
                    if t + 1 < NT:
                        take_qkv(t + 1)
                    rotate(t)
                st.wait()
                dve.wait_ge(sq_ok, NT)
                st.link(nc.vector.tensor_reduce(SSN, TURN.rearrange("p (n d) -> p n d", d=D1), AX, ALU.add))
                nc.vector.tensor_scalar(SSN, SSN, 1e-12, None, ALU.max).then_inc(ssum, 1)
                dve.wait_ge(root, 1)
                st.link(nc.vector.reciprocal(RNORM, RNORM))
                st.link(nc.vector.tensor_tensor(RNT, RNORM, RNORM, ALU.mult))
                st.link(nc.vector.tensor_tensor(RNT, RNT, SSN, ALU.mult))
                st.link(nc.vector.tensor_scalar(RNT, RNT, -0.5 / (2 * np.pi), 1.5 / (2 * np.pi), ALU.mult, ALU.add))
                st.link(nc.vector.tensor_tensor(RNORM, RNORM, RNT, ALU.mult))
                for i in range(NT // 2):
                    dve.wait_ge(u_sb, i + 1)
                    cols = slice(i * 2 * HF1, (i + 1) * 2 * HF1)
                    turn = v3(TURN[:, cols], 2 * NHK)
                    st.link(nc.vector.tensor_tensor(turn[:, :, 0:R1], v3(ANG, NT * NHK)[:, i * 2 * NHK:(i + 1) * 2 * NHK, :],
                                                    bc(RNORM[:, i * 2 * NHK:(i + 1) * 2 * NHK].unsqueeze(2), [P, 2 * NHK, R1]), ALU.mult))
                    st.link(nc.vector.tensor_scalar(turn[:, :, R1:], turn[:, :, 0:R1], 0.25, None, ALU.add))
                    st.link(nc.vector.tensor_scalar(FEAT[:, cols], TURN[:, cols], MAGIC, -MAGIC, ALU.add, ALU.add))
                    st.link(nc.vector.tensor_tensor(FEAT[:, cols], TURN[:, cols], FEAT[:, cols], ALU.subtract))
                    nc.vector.tensor_scalar(FEAT[:, cols], FEAT[:, cols], 0.5, -0.5, ALU.min, ALU.max).then_inc(u_ok, 1)

                xt_ps1, _, h_ps1, h_sb1, hT_ps1, _, _, _, mid = tile_sems[2]
                hs = [TA[:, (6 + i) * HID:(7 + i) * HID] for i in range(2)]
                PER_TILE = 2
                with dve.Fori(0, NT1 // 6) as i:
                    stl = Steps(dve, dve3l, i * (2 * PER_TILE))
                    for c in range(6):
                        u, t, even = i * 6 + c, i * 2 + c // 3, c // 3
                        dve.wait_ge(mid, u + 1)
                        dve.wait_ge(hT_ps1, u + (NT0 - 1))
                        nc.vector.tensor_tensor(hs[c % 2], ps[2 + c % 2][:, MI:2 * MI], hs[c % 2], ALU.mult).then_inc(h_sb1, 1)
                        w = MEET[even].rearrange("p (h k) -> p h k", h=H1)
                        prd = PRD.rearrange("p (h d k) -> p h d k", h=H1, d=D1)
                        if c % 3 == 0:
                            dve.wait_ge(prf_ok, t + 1)
                            nc.vector.tensor_reduce(w, PRF[even].rearrange("p (h k f) -> p h k f", h=H1, k=HKV), AX, ALU.add).then_inc(prf_rd, 1)
                            dve.wait_ge(prf_rd, t + 1)
                            stl.link(nc.vector.tensor_scalar(w, w, float(H1 // HKV) / D1, None, ALU.mult))
                        elif c % 3 == 1:
                            vals = QKV[:, bass.ds(t * (2 * HID) + HID + P, P)].rearrange("p (k d) -> p d k", k=HKV)
                            stl.link(nc.vector.tensor_tensor(prd, bc(w.unsqueeze(2), [P, H1, D1, HKV]),
                                                             bc(vals.unsqueeze(1), [P, H1, D1, HKV]), ALU.mult))
                        else:
                            nc.vector.tensor_reduce(VOUT[:, bass.ds(t * HID, HID)].rearrange("p (h d) -> p h d", h=H1), prd, AX, ALU.add).then_inc(o_ok, 1)
                    assert stl.n == 2 * PER_TILE

                ste = Steps(dve, dve3e)
                dve.wait_ge(bo_ok, NT)
                for t in range(NT):
                    dve.wait_ge(ao_ps, t + 1)
                    nc.vector.tensor_tensor(x3[:, t, :], ps[6 + t % 2][:, 0:HID], x3[:, t, :], ALU.add).then_inc(ao_rd, 1)
                    dve.wait_ge(ao_rd, t + 1)
                    dve.wait_ge(fgat[t // TPB], 16 * TPB * K1)
                    for k in range(K1):
                        i = t * K1 + k
                        ins = nc.vector.scalar_tensor_tensor(out=x3[:, t, :], in0=XN[:, i * HID:(i + 1) * HID], scalar=GATE[:, i:i + 1],
                                                             in1=x3[:, t, :], op0=ALU.mult, op1=ALU.add)
                        if k < K1 - 1:
                            ste.link(ins)
                    ins.then_inc(f_ok, 1)

            @block.tensor
            def _(pe):
                pe.wait_ge(ld_w1, 16 * 6)
                for k in range(KC):
                    for i in range(4):
                        nc.tensor.transpose(ps[2 + k][:, i * P:(i + 1) * P], WR1[:, i * HID + k * P:i * HID + (k + 1) * P], IDN[:, :])
                for k in range(KC):
                    for i in range(2):
                        nc.tensor.transpose(ps[4][:, (2 * k + i) * P:(2 * k + i + 1) * P],
                                            WR1[:, (4 + i) * HID + k * P:(4 + i) * HID + (k + 1) * P], IDN[:, :])
                pe.wait_ge(ld_r1, 16 * HKV)
                nc.tensor.transpose(ps[5][:, 0:HKV * R1], RBT, IDN[0:HKV * R1, 0:HKV * R1]).then_inc(wt1_ps, 1)
                for t in range(NT):
                    pe.wait_ge(xn_ok, NT + t + 1)
                    wait(pe, x1t_sb, t - 1)
                    for k in range(KC):
                        ins = nc.tensor.transpose(ps[t % 2][:, k * P:(k + 1) * P], xn3[:, t, k * P:(k + 1) * P], IDN[:, :])
                    ins.then_inc(x1t_ps, 1)
                pe.wait_ge(x1t_sb, NT)
                pe.wait_ge(ld_s1, 16 * 5)
                pe.wait_ge(wt1_sb, 4)
                for t in range(NT):
                    for k in range(KC):
                        ins = nc.tensor.matmul(ps[2][:, t * E1:(t + 1) * E1], xnT3[:, k, t * P:(t + 1) * P],
                                               RTW[:, k * E1:(k + 1) * E1], start=(k == 0), stop=(k == KC - 1))
                ins.then_inc(lg1_ps, 1)

                def qkv(t):
                    wait(pe, qkv_sb, t - 3)
                    for k in range(KC):
                        ins = nc.tensor.matmul(ps[4 + t % 4][:, :], xnT3[:, k, t * P:(t + 1) * P],
                                               WT1[:, k * 2 * HID:(k + 1) * 2 * HID], start=(k == 0), stop=(k == KC - 1))
                    ins.then_inc(qkv_ps, 1)
                qkv(0)
                qkv(1)
                rank_pe(pe, E1, ps[3], 1)
                for t in range(2, NT):
                    qkv(t)
                pe.wait_ge(slots_ok, 4)

                def angles(t):
                    pe.wait_ge(dT_sb, t + 1)
                    if t == 4:
                        pe.wait_ge(qkv_sb, NT)
                    for c in range(3):
                        lo = t % 2 * NHK * R1 + c * HKV * R1
                        ins = nc.tensor.matmul(ps[2 + t // 2][:, lo:lo + HKV * R1], DT[t % 2][:, c * P:(c + 1) * P], RBD,
                                               start=True, stop=True)
                    ins.then_inc(u_ps, 1)
                for t in range(NT):
                    pe.wait_ge(d_ok, t + 1)
                    wait(pe, dT_sb, t - 1)
                    for c in range(3):
                        ins = nc.tensor.transpose(ps[t % 2][:, c * P:(c + 1) * P], qkv3[:, t, c * P:(c + 1) * P], IDN[:, :])
                    ins.then_inc(dT_ps, 1)
                    if t:
                        angles(t - 1)
                angles(NT - 1)
                pe.wait_ge(u_sb, NT // 2)

                parts1[1](pe)
                pe.wait_ge(tile_sems[2][5], NT0 + NT1)
                pe.wait_ge(tile_sems[2][7], NT0 + NT1)

                def project1(t):
                    pe.wait_ge(oT_sb, t + 1)
                    wait(pe, ao_rd, t - 1)
                    for k in range(KC):
                        ins = nc.tensor.matmul(ps[6 + t % 2][:, 0:HID], OT[t % 2][:, k * P:(k + 1) * P], WOT[:, k * HID:(k + 1) * HID],
                                               start=(k == 0), stop=(k == KC - 1))
                    ins.then_inc(ao_ps, 1)
                for t in range(NT):
                    pe.wait_ge(hld[t // TPB], 16 * TPB)
                    wait(pe, oT_sb, t - 1)
                    for k in range(KC):
                        ins = nc.tensor.transpose(ps[4 + t % 2][:, k * P:(k + 1) * P], VIN[:, t * HID + k * P:t * HID + (k + 1) * P], IDN[:, :])
                    ins.then_inc(oT_ps, 1)
                    if t:
                        project1(t - 1)
                project1(NT - 1)


INPUTS = ["L0_attn_h", "L0_attn_Wq_c", "L0_attn_Wq_up", "L0_attn_Wk", "L0_attn_Wv", "L0_attn_W_comp", "L0_attn_q_norm_w",
          "L0_attn_k_norm_w", "L0_attn_sink", "L0_attn_Wg", "L0_attn_Wo", "L0_ffn_sw1", "L0_ffn_sb1", "L0_ffn_sw2", "L0_ffn_sb2",
          "L0_ffn_rw1", "L0_ffn_rb1", "L0_ffn_rw2", "L0_ffn_rb2", "L0_ffn_router_w", "L0_ffn_router_b", "L1_attn_Wq", "L1_attn_bq",
          "L1_attn_Wk", "L1_attn_bk", "L1_attn_Wv", "L1_attn_bv", "L1_attn_Wo", "L1_attn_bo", "L1_attn_rand_matrix",
          "L1_ffn_gate_kernel", "L1_ffn_wi_0", "L1_ffn_wi_1", "L1_ffn_wo"]


def kernel(**inputs):
    import concourse.bacc as bacc
    from concourse.bass_utils import run_bass_kernel_spmd

    nc = bacc.Bacc("TRN2", target_bir_lowering=False, num_devices=1)
    arrays = {n: np.ascontiguousarray(inputs[n]) for n in INPUTS}
    arrays.update(constants())
    args = {n: nc.dram_tensor(n, v.shape, mybir.dt.from_np(v.dtype), kind="ExternalInput").ap() for n, v in arrays.items()}
    out = nc.dram_tensor("out", (B, S, HID), F32, kind="ExternalOutput").ap()
    build(nc, args, out)
    r = run_bass_kernel_spmd(nc, [arrays], core_ids=[0])
    return r.results[0]["out"]
```

```python
from contextlib import ExitStack

import numpy as np

import concourse.bass as bass
from concourse import mybir

F32 = mybir.dt.float32
BF16 = mybir.dt.bfloat16
I32 = mybir.dt.int32
U32 = mybir.dt.uint32
ALU = mybir.AluOpType
ACT = mybir.ActivationFunctionType
AX = mybir.AxisListType.X

P = 128
B, S, HID = 4, 256, 256
T = B * S
NT = T // P
KC = HID // P
TPB = S // P
LN_EPS, RMS_EPS = 1e-5, 1e-6

H, D, QC, M, ROPE, WIN, CAP = 16, 128, 64, 16, 64, 64, 50.0
HR = ROPE // 2
NB = S // M
SCALE = 1.0 / float(np.sqrt(np.float32(D)))
NKEY = P + WIN + NB
KROW = P + NB + NKEY
NPAIR = H // 2
NG = H // 4

E0, K0, DH, NSH = 32, 6, 176, 2
DHB = DH - P
W1A, W1B, W2A, W2B, EW0 = 0, DH, 2 * DH, 2 * DH + HID, 2 * DH + 2 * HID
NT0 = T * K0 // P + E0 - 1
NT0Z = -(-NT0 // 4) * 4

H1, D1, HKV, E1, K1, MI = 16, 16, 8, 8, 2, 256
R1 = 8
EW1 = KC * 2 * MI + KC * HID
NT1 = T * K1 // P + E1 - 1
NT1Z = -(-NT1 // 4) * 4
MAGIC = 1.5 * 2.0 ** 23


def constants():
    f = np.float32
    t = np.arange(S, dtype=f)[:, None]
    c = {}
    a0 = t * (f(1) / f(10000.0) ** (np.arange(0, ROPE, 2, dtype=f) / f(ROPE)))[None]
    a1 = t * (f(1) / f(10000.0) ** (np.arange(0, D1, 2, dtype=f) / f(D1)))[None]
    tile = lambda a: a.reshape(TPB, P, -1).transpose(1, 0, 2).reshape(P, -1)
    c["rope0"] = np.concatenate([tile(np.cos(a0)), tile(np.sin(a0))], 1)
    c["rope1"] = np.concatenate([tile(np.cos(a1)), tile(np.sin(a1))], 1)
    p = np.arange(P)
    own = (p[None] <= p[:, None]) & (p[:, None] - p[None] < WIN)
    prev = np.arange(WIN)[None] > p[:, None]
    c["window"] = np.concatenate([own, prev], 1)
    end = np.arange(NB) * M + M - 1
    c["blocks"] = np.concatenate([np.where(end[None] < (p + j * P)[:, None], 0.0, -1e30) for j in range(TPB)], 1)
    c["ident"] = np.eye(P)
    c["before"] = p[:, None] < p[None]
    c["iota"] = np.tile(np.arange(NT0)[None], (P, 1))
    return {"table_" + k: np.ascontiguousarray(v, dtype=f) for k, v in c.items()}


class Steps:

    def __init__(self, eng, sem, base=0):
        self.eng, self.sem, self.base, self.n = eng, sem, base, 0

    def __call__(self, ins):
        ins.then_inc(self.sem, 1)
        self.n += 1

    def wait(self):
        self.eng.wait_ge(self.sem, self.base + self.n)

    def link(self, ins):
        self(ins)
        self.wait()


def bc(ap, shape):
    return ap.to_broadcast(shape)


def build(nc, a, out):
    ctx = ExitStack()
    sb = lambda name, cols, dt=F32, rows=P: ctx.enter_context(nc.sbuf_tensor(name, [rows, cols], dt))
    sem = lambda name: ctx.enter_context(nc.semaphore(name))
    v3 = lambda ap, n: ap.rearrange("p (a b) -> p a b", a=n)

    with ctx:
        xs0 = nc.dram_tensor("sorted_x0", [NT0Z * P, HID], F32).ap()
        ys0 = nc.dram_tensor("sorted_y0", [NT0 * P, HID], F32).ap()
        xs1 = nc.dram_tensor("sorted_x1", [NT1Z * P, HID], F32).ap()
        ys1 = nc.dram_tensor("sorted_y1", [NT1 * P, HID], F32).ap()
        heads1 = nc.dram_tensor("heads1", [T, HID], F32).ap()

        RW = sb("expert_weights", E0 * EW0)
        X = sb("residual", NT * HID)
        XN = sb("normed", 2 * NT * HID)
        WC = sb("out_weights", H * HID)
        WQ = sb("q_up_weights", H * D, rows=QC)
        SW1 = sb("shared_w1", NSH * KC * DH)
        SW2 = sb("shared_w2", NSH * 2 * HID)
        TA = sb("tiles", 3072)
        VA = sb("values", NT * D)
        V2A = sb("values_before", B * D, rows=WIN + NB)
        CK0 = sb("blocks_at_zero", B * D, rows=NB)
        QCT = sb("qc_T", (NT + 1) * P, rows=QC)
        KCAT = sb("keys", B * KROW)
        VOWN = sb("values_tile", TPB * D)
        V2 = sb("values_before_tile", D, rows=WIN + NB)
        CKS = sb("blocks_tile", D, rows=NB)
        QCS = sb("qc_tile", TPB * P, rows=QC)
        IDN = sb("ident", P)
        WINDOW = sb("window", P + WIN)
        BLOCKS = sb("blocks_valid", TPB * NB)
        BEFORE = sb("before", P)
        BEFOREB = sb("before_bf16", P, BF16)
        ONESB = sb("ones_bf16", P, BF16)
        IOTA = sb("iota", NT0)
        ROPE0 = sb("rope0", 2 * TPB * HR)
        ROPE1 = sb("rope1", 2 * TPB * D1 // 2)
        ZERO = sb("zeros", HID)
        MHALF = sb("minus_half", NT * (H1 + HKV))
        RB = sb("router_bias", E0)
        RTW = sb("router_w", KC * E0)
        TOP = sb("top8", NT * 8)
        TOPI = sb("top8_index", NT * 8, U32)
        TOPF = sb("top8_float", NT * 8)
        GATE = sb("gates", NT * K0)
        GSUM = sb("gate_sums", 2 * NT)
        SLOTF = sb("slots_float", NT * K0)
        SLOT = sb("slots", NT * K0, I32)
        IDX = sb("slots_tile", K0, I32)
        MASKB = sb("chosen_bf16", NT * E0, BF16)
        CUMB = sb("chosen_before_bf16", (NT + 1) * E0, BF16)
        START = sb("starts", 4 * E0)
        TEXP = sb("tile_expert_float", NT0)
        TEX = sb("tile_expert", NT0, I32)
        B1A = sb("expert_b1_T", E0 + NSH)
        B1B = sb("expert_b1_T2", E0 + NSH, rows=DHB)
        STAT = sb("ln_stats", NT * 6)
        MV = sb("ln_mean_var", NT * 2)
        RSTD = sb("rstd", NT)
        RR = sb("rms", 2 * H)
        SSQ = sb("sum_squares", 2 * H)
        KW = sb("norm_columns", 4)
        SINK = sb("sinks", 4 * H)
        LSUM = sb("prob_sums", 4 * H)
        CM = sb("block_max", 4 * H)
        ps = [ctx.enter_context(nc.psum_tensor(f"bank{i}", [P, 512], F32)) for i in range(8)]

        xn, xnT = XN[:, 0:NT * HID], XN[:, NT * HID:]
        x3, xn3 = v3(X[:, :], NT), v3(xn, NT)
        xnT3 = v3(xnT, KC)
        rw3 = v3(RW[:, :], E0)
        wc3 = v3(WC[:, :], H)
        kc3 = v3(KCAT[:, :], B)

        ELATE = 17
        tail = RW[:, ELATE * EW0:]
        o = 0

        def cut(n):
            nonlocal o
            o += n
            return tail[:, o - n:o]
        WCP = cut(M * KC * D)
        WGS = cut(H * HID)
        WOS = cut(H // 2 * HID)
        WKV = cut(KC * 2 * D)
        WQC = cut(KC * QC)
        EMID, EHALF = ELATE + M * KC * D // EW0, ELATE + (M * KC * D + H // 2 * HID) // EW0
        EEND = ELATE - -(M * KC * D + H * HID + H // 2 * HID) // EW0
        KRAW, KTMP = TA[:, 0:NT * D], TA[:, NT * D:2 * NT * D]
        o2 = 2 * NT * K0 * E0
        B1 = WC[0:E0 + NSH, o2:o2 + DH]
        KWR = TA[0:NB * B, 2816:2816 + D]
        LOGIT = WC[:, o2 + DH + D:o2 + DH + D + NT * E0]
        CUM = WC[:, o2 + DH + D + NT * E0:o2 + DH + D + 2 * NT * E0]
        CKR = TA[0:NB * B, 2560:2560 + 2 * D]
        ONEH, PROD = WC[:, 0:NT * K0 * E0], WC[:, NT * K0 * E0:2 * NT * K0 * E0]

        ln_stats, ln_var, ln_rstd, xn_ok = (sem("norm_" + n) for n in ("stats", "var", "rstd", "done"))
        chosen, rank_ok, gates_sub, gates_exp, slots_ok = (sem("route_" + n) for n in ("chosen", "rank", "gates_sub", "gates_exp", "slots"))

        def route_dve(dve, st, E, K):
            lg, tp, ti = v3(LOGIT[:, 0:NT * E], NT), v3(TOP[:, :], NT), v3(TOPI[:, :], NT)
            tf, g3 = v3(TOPF[:, :], NT), v3(GATE[:, 0:NT * K], NT)
            oh = ONEH[:, 0:NT * K * E].rearrange("p (t k e) -> p t k e", t=NT, k=K)
            pr = PROD[:, 0:NT * K * E].rearrange("p (t k e) -> p t k e", t=NT, k=K)
            for t in range(NT):
                st(nc.vector.max(tp[:, t, :], lg[:, t, :]))
            st.wait()
            for t in range(NT):
                st(nc.vector.max_index(ti[:, t, :], tp[:, t, :], lg[:, t, :]))
            st.wait()
            st.link(nc.vector.tensor_copy(TOPF[:, :], TOPI[:, :]))
            for t in range(NT):
                st(nc.vector.tensor_tensor(oh[:, t], bc(IOTA[:, 0:E].unsqueeze(1), [P, K, E]),
                                           bc(tf[:, t, 0:K].unsqueeze(2), [P, K, E]), ALU.is_equal))
            st.wait()
            st.link(nc.vector.tensor_reduce(v3(CUM[:, 0:NT * E], NT),
                                            ONEH[:, 0:NT * K * E].rearrange("p (t k e) -> p t e k", t=NT, k=K),
                                            AX, ALU.add))
            st(nc.vector.tensor_copy(MASKB[:, 0:NT * E], CUM[:, 0:NT * E]))
            st.link(nc.vector.memset(CUMB[:, 0:E], 0.0))
            for t in range(1, NT):
                st.link(nc.vector.tensor_tensor(CUM[:, t * E:(t + 1) * E], CUM[:, (t - 1) * E:t * E],
                                                CUM[:, t * E:(t + 1) * E], ALU.add))
            nc.vector.tensor_copy(CUMB[:, E:(NT + 1) * E], CUM[:, 0:NT * E]).then_inc(chosen, 1)
            nc.vector.tensor_tensor(g3, tp[:, :, 0:K], bc(tp[:, :, 0:1], [P, NT, K]), ALU.subtract).then_inc(gates_sub, 1)

        def route_dve_slots(dve, st, E, K, bank, layer):
            g3 = v3(GATE[:, 0:NT * K], NT)
            pr = PROD[:, 0:NT * K * E].rearrange("p (t k e) -> p t k e", t=NT, k=K)
            oh = ONEH[:, 0:NT * K * E].rearrange("p (t k e) -> p t k e", t=NT, k=K)
            dve.wait_ge(gates_exp, layer + 1)
            st.link(nc.vector.reduce_sum(GSUM[:, 0:NT], g3, AX))
            st.link(nc.vector.reciprocal(GSUM[:, NT:], GSUM[:, 0:NT]))
            st(nc.vector.tensor_tensor(g3, g3, bc(GSUM[:, NT:].unsqueeze(2), [P, NT, K]), ALU.mult))
            dve.wait_ge(rank_ok, layer + 1)
            n = START[:, 0:E]
            st.link(nc.vector.tensor_scalar(n, bank[:, NT * E:(NT + 1) * E], 1.0 / P,
                                            (P - 1.0) / P - 0.5 + 0.5 / P, ALU.mult, ALU.add))
            st.link(nc.vector.tensor_scalar(n, n, MAGIC, -MAGIC, ALU.add, ALU.add))
            if layer == 0:
                st.link(nc.vector.tensor_scalar(n, n, 1.0, None, ALU.max))
            st.link(nc.vector.memset(START[:, E0:E0 + E], 1.0))
            st.link(nc.vector.tensor_tensor_scan(START[:, 2 * E0:2 * E0 + E], START[:, E0:E0 + E], n, 0.0,
                                                 ALU.mult, ALU.add))
            st.link(nc.vector.tensor_tensor(n, START[:, 2 * E0:2 * E0 + E], n, ALU.subtract))
            st.link(nc.vector.tensor_scalar(START[:, E0:E0 + E], n, float(P), None, ALU.mult))
            st.link(nc.vector.tensor_tensor(v3(CUM[:, 0:NT * E], NT), v3(bank[:, 0:NT * E], NT),
                                            bc(START[:, E0:E0 + E].unsqueeze(1), [P, NT, E]), ALU.add))
            for t in range(NT):
                st(nc.vector.tensor_tensor(pr[:, t], oh[:, t],
                                           bc(CUM[:, t * E:(t + 1) * E].unsqueeze(1), [P, K, E]), ALU.mult))
            st.wait()
            st.link(nc.vector.tensor_reduce(v3(SLOTF[:, 0:NT * K], NT), pr, AX, ALU.add))
            nc.vector.tensor_copy(SLOT[:, 0:NT * K], SLOTF[:, 0:NT * K]).then_inc(slots_ok, 1)

        def route_dve_experts(dve, st, E, ntile, layer):
            ge = WC[0:1, 0:ntile * E].rearrange("p (i e) -> p i e", i=ntile)
            dve.wait_ge(slots_ok, 2 * layer + 1)
            st.link(nc.vector.tensor_tensor(ge, bc(IOTA[0:1, 0:ntile].unsqueeze(2), [1, ntile, E]),
                                            bc(START[0:1, 0:E].unsqueeze(1), [1, ntile, E]), ALU.is_ge))
            st.link(nc.vector.reduce_sum(TEXP[0:1, 0:ntile], ge, AX))
            st.link(nc.vector.tensor_scalar(TEXP[0:1, 0:ntile], TEXP[0:1, 0:ntile], -1.0, None, ALU.add))
            nc.vector.tensor_copy(TEX[0:1, 0:ntile], TEXP[0:1, 0:ntile]).then_inc(slots_ok, 1)

        def rank_pe(pe, E, bank, layer):
            pe.wait_ge(chosen, layer + 1)
            for t in range(NT):
                nc.tensor.matmul(bank[:, t * E:(t + 1) * E], BEFOREB[:, :], MASKB[:, t * E:(t + 1) * E],
                                 start=True, stop=False)
                nc.tensor.matmul(bank[:, t * E:(t + 1) * E], ONESB[:, :], CUMB[:, t * E:(t + 1) * E],
                                 start=False, stop=True)
            nc.tensor.matmul(bank[:, NT * E:(NT + 1) * E], ONESB[:, :], CUMB[:, NT * E:(NT + 1) * E],
                             start=True, stop=True).then_inc(rank_ok, 1)

        def layernorm_dve(dve, st, n, tiles):
            mv = v3(MV[:, :], NT)
            for t in tiles:
                st(nc.vector.bn_stats(STAT[:, 6 * t:6 * t + 6], x3[:, t, :]))
            st.wait()
            for t in tiles:
                ins = nc.vector.bn_aggr(mv[:, t, :], STAT[:, 6 * t:6 * t + 6])
                if t < tiles[-1]:
                    st(ins)
            ins.then_inc(ln_stats, 1)
            st.wait()
            dve.wait_ge(ln_rstd, n)
            for t in tiles:
                nc.vector.tensor_scalar(xn3[:, t, :], x3[:, t, :], mv[:, t, 0:1], RSTD[:, t:t + 1],
                                        ALU.subtract, ALU.mult).then_inc(xn_ok, 1)

        def layernorm_pool(pool, n, tiles):
            r = RSTD[:, tiles[0]:tiles[-1] + 1]
            pool.wait_ge(ln_stats, n)
            nc.gpsimd.tensor_scalar(r.unsqueeze(2), v3(MV[:, :], NT)[:, tiles[0]:tiles[-1] + 1, 1:2], LN_EPS, None,
                                    ALU.add).then_inc(ln_var, 1)
            pool.wait_ge(ln_var, n)
            nc.gpsimd.tensor_tensor(r, r, MHALF[:, 0:len(tiles)], ALU.pow).then_inc(ln_rstd, 1)

        base = E1 * EW1
        o1 = base

        def cut1(n):
            nonlocal o1
            o1 += n
            return RW[:, o1 - n:o1]
        PB = cut1(TPB * H * NKEY).rearrange("p (j h n) -> p j h n", j=TPB, h=H)
        YG = [cut1(K0 * HID) for _ in range(TPB)]
        QTB = [cut1(4 * P) for _ in range(2)]
        PTB = [cut1(4 * P) for _ in range(2)]
        AOB = [cut1(4 * P) for _ in range(2)]
        WR1 = cut1(6 * HID)
        BQKV, BO, RBD = SW2[:, 0:2 * HID], SW2[:, 2 * HID:3 * HID], SW2[:, 3 * HID:3 * HID + HKV * R1]
        RBT = SW2[0:HKV * R1, 3 * HID + P:3 * HID + 2 * P]
        QB = [XN[:, (1 - j) * H * D:(2 - j) * H * D] for j in range(TPB)]
        NSW = [P, P + WIN]
        gates0 = v3(GATE[:, :], NT)
        rw13 = v3(RW[:, 0:base], E1)

        ld_e1, ld_w1, ld_s1, ld_r1, rb_zero = (sem(n) for n in ("ld_experts1", "ld_attn1", "ld_small1", "ld_rand1", "rand_zero"))
        zero1 = sem("zero1_done")
        x1t_ps, x1t_sb = sem("b_xT_psum"), sem("b_xT_sbuf")
        dve2p, dve2l, dve2e = sem("dve2_head"), sem("dve2_loop"), sem("dve2_tail")
        es_ok = sem("sink_exp")
        (qcs_ok, v_ok, v_half, q_ps, q_ev, qss, qpow, q_mul, q_rot, qn, t_ps, t_sb, s_ps, th, s_ev, e_sb, pn, csub, cexp, cn,
         pt_ps, pt_sb, pv_ps, ao_sb, opg, op_sb, idx_ok, comb) = (
            sem("a_" + n) for n in (
                "qc_copied", "values_copied", "values_half", "q_psum", "q_sbuf", "q_squares", "q_mean", "q_products", "q_rotated", "q_normed",
                "qT_psum", "qT_sbuf", "scores_psum", "tanh", "scores_read", "exp", "probs", "blocks_sub", "blocks_exp",
                "blocks_probs", "pT_psum", "pT_sbuf", "out_psum", "out_sbuf", "proj_group", "proj_read", "slots_tile",
                "combined"))
        gat = [sem(f"a_gathered{j}") for j in range(TPB)]
        NSTEP = NT + 3
        MOST, LAST = range(NT - 1), range(NT - 1, NT)

        def wait(eng, s, n):
            if not isinstance(n, int) or n > 0:
                eng.wait_ge(s, n)

        def attention_step(eng, step, g, section, only=None):
            step(eng, g, g % 2, lambda lag: (g - lag) // 2, lambda lag: 0 <= g - lag < NT and only in (None, lag), section)

        def run_attention(eng, step, before_last=lambda: None):
            for g in range(1, 4):
                attention_step(eng, step, g, (0, 0))
            with eng.Fori(0, (NT - 4) // 2) as i:
                for c in range(4, 6):
                    step(eng, i * 2 + c, c % 2, lambda lag: i + (c - lag) // 2, lambda lag: True, (1, i))
            for g in range(NT, NSTEP):
                if g == NSTEP - 1:
                    before_last()
                attention_step(eng, step, g, (2, 0))

        qcs, vown, wq3 = v3(QCS[:, :], TPB), v3(VOWN[:, :], TPB), v3(WQ[:, :], NG)
        cos0, sin0 = (v3(ROPE0[:, i * TPB * HR:(i + 1) * TPB * HR], TPB) for i in range(2))
        HH = H // 2

        def first(g):
            return isinstance(g, int) and g == 1

        def ahead(g):
            return isinstance(g, int) and g <= 1

        def hoisted(g):
            return isinstance(g, int) and g <= 0

        def query_rotate(pool, g, j):
            pool.wait_ge(qss, g + 1)
            if not ahead(g):
                wait(pool, qn, g)
            r = RR[:, j * H:(j + 1) * H]
            nc.gpsimd.tensor_tensor(r, r, MHALF[:, 0:H], ALU.pow).then_inc(qpow, 1)
            c, s = (bc(t[:, j, :].unsqueeze(1), [P, HH, HR]) for t in (cos0, sin0))
            for half in range(2):
                q3 = v3(QB[j], H)[:, half * HH:(half + 1) * HH, :]
                x1, x2 = q3[:, :, 0:HR], q3[:, :, HR:ROPE]
                room = SW2[:, :] if ahead(g) else TA[:, half * 4 * HH * HR:(half + 1) * 4 * HH * HR]
                tmp = [v3(room[:, i * HH * HR:(i + 1) * HH * HR], HH) for i in range(4)]
                if ahead(g):
                    wait(pool, q_rot, g * 4 + 2 * half)
                for i, (x, w) in enumerate(((x1, c), (x2, s), (x1, s), (x2, c))):
                    nc.gpsimd.tensor_tensor(tmp[i], x, w, ALU.mult).then_inc(q_mul, 1)
                pool.wait_ge(q_mul, g * 8 + 4 * half + 4)
                nc.gpsimd.tensor_tensor(x1, tmp[0], tmp[1], ALU.subtract).then_inc(q_rot, 1)
                nc.gpsimd.tensor_tensor(x2, tmp[2], tmp[3], ALU.add).then_inc(q_rot, 1)

        def attention_pool(pool, g, j, batch, on, section):
            ja = 1 - j
            if on(2):
                wait(pool, gat[ja], (batch(3) + 1) * (16 * K0))
                nc.gpsimd.tensor_copy(IDX[:, :], SLOT[:, bass.ds((g - 2) * K0, K0)]).then_inc(idx_ok, 1)
                pool.wait_ge(idx_ok, g - 1)
                wait(pool, comb, g - 3)
            if on(1):
                wait(pool, pv_ps, (g - 2) * NPAIR)
                nc.gpsimd.tensor_copy(vown[:, ja, :], VA[:, bass.ds((g - 1) * D, D)]).then_inc(v_half, 1)
                if ja:
                    nc.gpsimd.tensor_copy(V2[:, :], V2A[:, bass.ds(batch(1) * D, D)]).then_inc(v_ok, 1)
                else:
                    nc.gpsimd.tensor_copy(CKS[:, :], CK0[:, bass.ds(batch(1) * D, D)]).then_inc(v_ok, 1)
            if on(-1):
                wait(pool, q_ps, g * NG)
                nc.gpsimd.tensor_copy(qcs[:, ja, :], QCT[:, bass.ds((g + 1) * P, P)]).then_inc(qcs_ok, 1)
            if on(0) and not ahead(g):
                query_rotate(pool, g, j)
            if on(2):
                for k in range(K0):
                    nc.gpsimd.indirect_dma_start(YG[j][:, k * HID:(k + 1) * HID], None, ys0,
                                                 bass.IndirectOffsetOnAxis(ap=IDX[:, k:k + 1], axis=0)).then_inc(gat[j], 16)

        def attention_pe(pe, g, j, batch, on, section):
            ja = 1 - j

            def queries(k):
                if on(-1):
                    pe.wait_ge(qcs_ok, g + 2)
                    if not hoisted(g):
                        wait(pe, q_ev, (g + 1) * NG + k)
                    bank = ps[(2 + g) % 2 * NG + k if hoisted(g) else 0]
                    nc.tensor.matmul(bank[:, :], qcs[:, ja, :], wq3[:, k, :], start=True, stop=True).then_inc(q_ps, 1)

            def turn_queries(k, lag=1):
                if on(lag):
                    t = g - lag
                    pe.wait_ge(qn, t + 1)
                    wait(pe, t_sb, t * NG + k)
                    q3 = v3(QB[ja if lag else j], H)
                    for h in range(4):
                        ins = nc.tensor.transpose(ps[1][:, h * P:(h + 1) * P], q3[:, 4 * k + h, :], IDN[:, :])
                    ins.then_inc(t_ps, 1)

            def scores(p):
                if on(1):
                    pe.wait_ge(t_sb, (g - 1) * NG + (p // 2 + 1))
                    wait(pe, s_ev, (g - 1) * NPAIR + (p - 1))
                    n = NSW[ja] + NB
                    keys = KCAT[:, bass.ds(batch(1) * KROW + (P + NB if ja else 0), n)]
                    for i in range(2):
                        h = 2 * p + i
                        ins = nc.tensor.matmul(ps[2 + p % 2][:, i * NKEY:i * NKEY + n],
                                               QTB[h // 4 % 2][:, h % 4 * P:(h % 4 + 1) * P], keys, start=True, stop=True)
                    ins.then_inc(s_ps, 1)

            def turn_probs(p):
                if on(2):
                    pe.wait_ge(pn, (g - 2) * NPAIR + (p + 1))
                    pe.wait_ge(cn, (g - 2) * 2 + (p // 4 + 1))
                    wait(pe, pt_sb, (g - 2) * NPAIR + (p - 1))
                    n = NSW[j] + NB
                    for i in range(2):
                        nc.tensor.transpose(ps[4 + p % 2][:, i * P:(i + 1) * P], PB[:, j, 2 * p + i, 0:P], IDN[:, :])
                        ins = nc.tensor.transpose(ps[4 + p % 2][0:n - P, (2 + i) * P:(3 + i) * P],
                                                  PB[:, j, 2 * p + i, P:n], IDN[:, :])
                    ins.then_inc(pt_ps, 1)

            def values(p):
                if on(2):
                    pe.wait_ge(v_ok, g - 1)
                    pe.wait_ge(v_half, g - 1)
                    pe.wait_ge(pt_sb, (g - 2) * NPAIR + (p + 1))
                    if p % 2 == 0:
                        wait(pe, ao_sb, (g - 2) * NG + p // 2)
                    n = NSW[j] + NB - P
                    for i in range(2):
                        o = ps[6][:, (2 * p + i) % 4 * P:((2 * p + i) % 4 + 1) * P]
                        nc.tensor.matmul(o, vown[:, j, :], PTB[p % 2][:, i * P:(i + 1) * P], start=True, stop=False)
                        ins = nc.tensor.matmul(o, V2[:, :] if j else CKS[:, :], PTB[p % 2][0:n, (2 + i) * P:(3 + i) * P],
                                               start=False, stop=True)
                    ins.then_inc(pv_ps, 1)

            def project(k, lag=2):
                if on(lag):
                    pe.wait_ge(ao_sb, (g - lag) * NG + (k + 1))
                    if k == 0:
                        wait(pe, op_sb, g - lag)
                    for h in range(4):
                        ins = nc.tensor.matmul(ps[7][:, 0:HID], AOB[k % 2][:, h * P:(h + 1) * P], wc3[:, 4 * k + h, :],
                                               start=(k + h == 0), stop=(k == NG - 1 and h == 3))
                    ins.then_inc(opg, 1)

            if first(g):
                turn_queries(0)
            for p in range(NPAIR):
                if p % 2 == 0 and p // 2 + 1 < NG:
                    turn_queries(p // 2 + 1)
                scores(p)
                turn_probs(p)
                if p == 0:
                    project(NG - 1, lag=3)
                if p >= NPAIR - NG:
                    queries(p - (NPAIR - NG))
                if p >= 1:
                    values(p - 1)
                if p >= 3 and p % 2:
                    project((p - 3) // 2)
            if not hoisted(g):
                turn_queries(0, lag=0)
            values(NPAIR - 1)

        def attention_act(act, g, j, batch, on, section):
            ja = 1 - j
            nsw = NSW[ja]

            def queries(k):
                if on(-1):
                    act.wait_ge(q_ps, (g + 1) * NG + (k + 1))
                    wait(act, t_ps, g * NG)
                    bank = ps[(2 + g) % 2 * NG + k if hoisted(g) else 0]
                    nc.scalar.activation(QB[ja][:, k * 512:(k + 1) * 512], bank[:, :], ACT.Copy).then_inc(q_ev, 1)

            def probs(p):
                if on(1):
                    act.wait_ge(s_ps, (g - 1) * NPAIR + (p + 1))
                    wait(act, pt_ps, (g - 3) * NPAIR + (p + 1))
                    sc = v3(ps[2 + p % 2][:, 0:2 * NKEY], 2)
                    pb = PB[:, ja, 2 * p:2 * p + 2, :]
                    nc.scalar.activation(pb[:, :, 0:nsw], sc[:, :, 0:nsw], ACT.Tanh, scale=SCALE / CAP).then_inc(th, 1)
                    nc.scalar.activation(pb[:, :, nsw:nsw + NB], sc[:, :, nsw:nsw + NB], ACT.Copy, scale=SCALE).then_inc(s_ev, 1)
                    act.wait_ge(th, (g - 1) * NPAIR + (p + 1))
                    for i in range(2):
                        h = 2 * p + i
                        ins = nc.scalar.activation(pb[:, i, 0:nsw], pb[:, i, 0:nsw], ACT.Exp, scale=CAP, bias=SINK[:, H + h:H + h + 1])
                    ins.then_inc(e_sb, 1)

            def probs_T(p):
                if on(2):
                    act.wait_ge(pt_ps, (g - 2) * NPAIR + (p + 1))
                    wait(act, pv_ps, (g - 2) * NPAIR + (p - 1))
                    n = NSW[j] + NB - P
                    nc.scalar.activation(PTB[p % 2][:, 0:2 * P], ps[4 + p % 2][:, 0:2 * P], ACT.Copy)
                    nc.scalar.activation(PTB[p % 2][0:n, 2 * P:], ps[4 + p % 2][0:n, 2 * P:], ACT.Copy).then_inc(pt_sb, 1)

            def outs(k):
                if on(2):
                    act.wait_ge(pv_ps, (g - 2) * NPAIR + (2 * k + 2))
                    wait(act, opg, (g - 2) * NG + (k - 1))
                    nc.scalar.activation(AOB[k % 2], ps[6][:, :], ACT.Copy).then_inc(ao_sb, 1)

            def blocks(half):
                if on(1):
                    act.wait_ge(csub, (g - 1) * 2 + (half + 1))
                    cb = PB[:, ja, 8 * half:8 * half + 8, nsw:nsw + NB]
                    nc.scalar.activation(cb, cb, ACT.Exp)
                    nc.scalar.activation(CM[:, 24:32], CM[:, 16:24], ACT.Exp).then_inc(cexp, 1)

            for p in range(NPAIR):
                probs(p)
                probs_T(p)
                if p >= NPAIR - NG:
                    queries(p - (NPAIR - NG))
                if p >= 2 and p % 2 == 0:
                    outs(p // 2 - 1)
                if p == 6:
                    blocks(0)
            outs(NG - 1)
            blocks(1)

        PER_STEP = NPAIR * 4 + 2 * 6 + H + (K0 - 1)
        sections = {}

        def dve_steps(dve, kind, i=0):
            if kind not in sections:
                sections[kind] = Steps(dve, (dve2p, dve2l, dve2e)[kind], i * (2 * PER_STEP) if kind == 1 else 0)
            sections[kind].eng = dve
            return sections[kind]

        def query_squares(dve, st, g, j):
            dve.wait_ge(q_ev, g * NG + NG)
            if not ahead(g):
                wait(dve, qn, g)
            q3 = v3(QB[j], H)
            n = SW1.shape[1] // D if ahead(g) else H
            room = SW1 if ahead(g) else TA
            for h in range(H):
                if h and h % n == 0:
                    st.wait()
                st(nc.vector.scalar_tensor_tensor(out=room[:, h % n * D:(h % n + 1) * D], in0=q3[:, h, :], scalar=1.0,
                                                  in1=q3[:, h, :], op0=ALU.mult, op1=ALU.mult, accum_out=SSQ[:, j * H + h:j * H + h + 1]))
            st.wait()
            nc.vector.tensor_scalar(RR[:, j * H:(j + 1) * H], SSQ[:, j * H:(j + 1) * H], 1.0 / D, RMS_EPS, ALU.mult, ALU.add).then_inc(qss, 1)

        def query_norm(dve, g, j):
            dve.wait_ge(qpow, g + 1)
            dve.wait_ge(q_rot, g * 4 + 4)
            q3 = v3(QB[j], H)
            nc.vector.tensor_tensor(q3, q3, bc(RR[:, j * H:(j + 1) * H].unsqueeze(2), [P, H, D]), ALU.mult).then_inc(qn, 1)

        def attention_dve(dve, g, j, batch, on, section):
            kind, i = section
            st = dve_steps(dve, kind, i)
            ja = 1 - j
            nsw = NSW[ja]

            def queries_T(k, lag=1):
                if on(lag):
                    t = g - lag
                    dve.wait_ge(t_ps, t * NG + (k + 1))
                    wait(dve, s_ps, t * NPAIR + (2 * k - 2))
                    nc.vector.tensor_copy(QTB[k % 2], ps[1][:, :]).then_inc(t_sb, 1)

            def norm(p):
                if on(1):
                    dve.wait_ge(e_sb, (g - 1) * NPAIR + (p + 1))
                    hs = slice(2 * p, 2 * p + 2)
                    for h in range(2 * p, 2 * p + 2):
                        pb = PB[:, ja, h, 0:nsw]
                        st(nc.vector.scalar_tensor_tensor(out=pb, in0=pb, scalar=1.0, in1=WINDOW[:, 0:nsw], op0=ALU.mult,
                                                          op1=ALU.mult, accum_out=LSUM[:, h:h + 1]))
                    st.wait()
                    st.link(nc.vector.tensor_tensor(LSUM[:, H + 2 * p:H + 2 * p + 2], LSUM[:, hs],
                                                    SINK[:, 3 * H + 2 * p:3 * H + 2 * p + 2], ALU.add))
                    st.link(nc.vector.reciprocal(LSUM[:, 2 * H + 2 * p:2 * H + 2 * p + 2], LSUM[:, H + 2 * p:H + 2 * p + 2]))
                    for h in range(2 * p, 2 * p + 2):
                        pb = PB[:, ja, h, 0:nsw]
                        ins = nc.vector.tensor_scalar(pb, pb, LSUM[:, 2 * H + h:2 * H + h + 1], None, ALU.mult)
                    ins.then_inc(pn, 1)

            def blocks_sub(half):
                if on(1):
                    dve.wait_ge(s_ev, (g - 1) * NPAIR + (4 * half + 4))
                    cb = PB[:, ja, 8 * half:8 * half + 8, nsw:nsw + NB]
                    sk = SINK[:, 8 * half:8 * half + 8]
                    st.link(nc.vector.tensor_tensor(cb, cb, bc(v3(BLOCKS[:, :], TPB)[:, ja, :].unsqueeze(1), [P, 8, NB]), ALU.add))
                    st.link(nc.vector.reduce_max(CM[:, 0:8], cb, AX))
                    st.link(nc.vector.tensor_tensor(CM[:, 8:16], CM[:, 0:8], sk, ALU.max))
                    nc.vector.tensor_tensor(CM[:, 16:24], sk, CM[:, 8:16], ALU.subtract)
                    nc.vector.tensor_tensor(cb, cb, bc(CM[:, 8:16].unsqueeze(2), [P, 8, NB]), ALU.subtract).then_inc(csub, 1)

            def blocks_norm(half):
                if on(1):
                    dve.wait_ge(cexp, (g - 1) * 2 + (half + 1))
                    cb = PB[:, ja, 8 * half:8 * half + 8, nsw:nsw + NB]
                    st.link(nc.vector.reduce_sum(CM[:, 32:40], cb, AX))
                    st.link(nc.vector.tensor_tensor(CM[:, 40:48], CM[:, 32:40], CM[:, 24:32], ALU.add))
                    st.link(nc.vector.reciprocal(CM[:, 48:56], CM[:, 40:48]))
                    nc.vector.tensor_tensor(cb, cb, bc(CM[:, 48:56].unsqueeze(2), [P, 8, NB]), ALU.mult).then_inc(cn, 1)

            def take_out():
                if on(3):
                    x = X[:, bass.ds((g - 3) * HID, HID)]
                    dve.wait_ge(opg, (g - 3) * NG + NG)
                    nc.vector.tensor_tensor(x, ps[7][:, 0:HID], x, ALU.add).then_inc(op_sb, 1)

            def combine():
                if on(3):
                    x = X[:, bass.ds((g - 3) * HID, HID)]
                    dve.wait_ge(op_sb, g - 2)
                    dve.wait_ge(gat[ja], (batch(3) + 1) * (16 * K0))
                    for k in range(K0):
                        ins = nc.vector.scalar_tensor_tensor(out=x, in0=YG[ja][:, k * HID:(k + 1) * HID],
                                                             scalar=GATE[:, bass.ds((g - 3) * K0 + k, 1)], in1=x,
                                                             op0=ALU.mult, op1=ALU.add)
                        if k < K0 - 1:
                            st.link(ins)
                    ins.then_inc(comb, 1)

            if first(g):
                queries_T(0)
            for p in range(NPAIR):
                if p % 2 == 0 and p // 2 + 1 < NG:
                    queries_T(p // 2 + 1)
                if p == 0 and on(0) and not ahead(g):
                    query_squares(dve, st, g, j)
                if p == 1:
                    take_out()
                if p >= 1:
                    norm(p - 1)
                if p == 4:
                    combine()
                if p == 6:
                    if on(0) and not ahead(g):
                        query_norm(dve, g, j)
                if p == 5:
                    blocks_sub(0)
                if p == 7:
                    blocks_norm(0)
            queries_T(0, lag=0)
            norm(NPAIR - 1)
            blocks_sub(1)
            blocks_norm(1)
            if kind == 1 and j == 1:
                assert st.n == 2 * PER_STEP, (st.n, PER_STEP)

        ld_x, ld_c, ld_rt, ld_sh, ld_aw, ld_cp, ld_wg, ld_ex, ld_ex2, ld_ct = (
            sem(n) for n in ("ld_x", "ld_const", "ld_router", "ld_shared", "ld_attn_w", "ld_comp", "ld_wg",
                             "ld_experts", "ld_experts2", "ld_attn_tables"))
        n_c = n_rt = n_sh = n_aw = n_ex = n_ex2 = 0
        zero_set, zero_done = sem("zero_set"), sem("zero_done")
        const_set = sem("const_set")
        dve1, act1, pool1 = sem("dve1"), sem("act1"), sem("pool1")
        xt_ps, xt_sb = sem("xT_psum"), sem("xT_sbuf")
        lg_ps, lg_sb = sem("logit_psum"), sem("logit_sbuf")
        b1_ps, b1_sb = sem("b1_psum"), sem("b1_sbuf")
        scat0 = sem("scatter0")
        sh_ps, sh_sb, so_ps, so_sb = (sem(n) for n in ("shared_h_psum", "shared_h_sbuf", "shared_o_psum", "shared_o_sbuf"))
        wt_ps, wt_sb, wf_ps, wf_sb = (sem(n) for n in ("wgT_psum", "wgT_sbuf", "fold_psum", "fold_sbuf"))
        kv_ps, kv_sb, v2_ps, v2_sb, qc_ps, qc_sb, ck_ps = (
            sem(n) for n in ("kv_psum", "kv_sbuf", "v2_psum", "v2_sbuf", "qc_psum", "qc_sbuf", "ck_psum"))
        kss, krr, kn_r, kt_ps, kt_sb = (sem(n) for n in ("k_squares", "k_rms", "k_normed", "kT_psum", "kT_sbuf"))
        css, crr, ck_r, ckd, kvp = (sem(n) for n in ("ck_squares", "ck_rms", "ck_ready", "ck_moved", "pool_k"))

        wkv3, wqc3 = v3(WKV, KC), v3(WQC, KC)
        wcp3 = v3(WCP, M * KC)
        wgs3, wos3 = v3(WGS, H), v3(WOS, H // 2)
        sw1 = SW1[:, :].rearrange("p (s k n) -> p s k n", s=NSH, k=KC)
        sw2 = SW2[:, :].rearrange("p (s c n) -> p s c n", s=NSH, c=2)
        va3, v2a3, ck03 = v3(VA[:, :], NT), v3(V2A[:, :], B), v3(CK0[:, :], B)
        HF = T // 2
        shA = v3(TA[:, 0:NSH * HF], NSH)
        shB = v3(TA[:, NSH * HF:2 * NSH * HF], NSH)
        wgT = [TA[:, 2 * NSH * HF + i * HID:2 * NSH * HF + (i + 1) * HID] for i in range(2)]
        kraw3 = v3(KRAW, NT)

        def load_experts(sp, e0, e1, done):
            for k in range(KC):
                sp.dma_start(rw3[:, e0:e1, k * DH:(k + 1) * DH],
                             a["L0_ffn_rw1"][e0:e1, k * P:(k + 1) * P, :].rearrange("e p n -> p e n")).then_inc(done, 16)
            sp.dma_start(rw3[:, e0:e1, W2A:W2B], a["L0_ffn_rw2"][e0:e1, 0:P, :].rearrange("e p n -> p e n")).then_inc(done, 16)
            sp.dma_start(rw3[0:DHB, e0:e1, W2B:], a["L0_ffn_rw2"][e0:e1, P:DH, :].rearrange("e p n -> p e n")).then_inc(done, 16)
            sp.dma_start(rw3[DHB:DHB + 1, e0:e1, W2B:], a["L0_ffn_rb2"][e0:e1, :].unsqueeze(0)).then_inc(done, 16)

        SHARED_BANKS = (0, 1, 6, 7)

        with nc.Block() as block:
            @block.sync
            def _(sp):
                nonlocal n_c, n_rt, n_sh, n_aw, n_ex, n_ex2
                sp.dma_start(x3, a["L0_attn_h"].rearrange("b (j p) d -> p (b j) d", p=P)).then_inc(ld_x, 16)
                for t, n in ((IDN, "ident"), (BEFORE, "before"), (IOTA, "iota")):
                    sp.dma_start(t[:, :], a["table_" + n]).then_inc(ld_c, 16)
                    n_c += 16
                sp.dma_start(v3(RTW[:, :], KC), a["L0_ffn_router_w"].rearrange("(k p) e -> p k e", p=P)).then_inc(ld_rt, 16)
                sp.dma_start(RB[:, :], a["L0_ffn_router_b"].partition_broadcast(P)).then_inc(ld_rt, 16)
                for s in range(NSH):
                    sp.dma_start(sw1[:, s], a["L0_ffn_sw1"][s].rearrange("(k p) n -> p k n", p=P)).then_inc(ld_sh, 16)
                    sp.dma_start(sw2[:, s, 0], a["L0_ffn_sw2"][s, 0:P, :]).then_inc(ld_sh, 16)
                    sp.dma_start(sw2[0:DHB, s, 1], a["L0_ffn_sw2"][s, P:DH, :]).then_inc(ld_sh, 16)
                    sp.dma_start(sw2[DHB:DHB + 1, s, 1], a["L0_ffn_sb2"][s:s + 1, :]).then_inc(ld_sh, 16)
                    n_sh += 64
                sp.dma_start(B1[0:E0, :], a["L0_ffn_rb1"]).then_inc(ld_sh, 16)
                sp.dma_start(B1[E0:E0 + NSH, :], a["L0_ffn_sb1"]).then_inc(ld_sh, 16)
                n_sh += 32
                sp.wait_ge(zero_set, 1)
                for i in range(NT0Z // 4):
                    sp.dma_start(xs0[i * 4 * P:(i + 1) * 4 * P, :].rearrange("(c p) d -> p c d", p=P),
                                 bc(ZERO[:, :].unsqueeze(1), [P, 4, HID])).then_inc(zero_done, 16)
                sp.dma_start(wcp3, a["L0_attn_W_comp"].rearrange("(c p) d -> p c d", p=P)).then_inc(ld_cp, 16)
                for k in range(KC):
                    sp.dma_start(wkv3[:, k, 0:D], a["L0_attn_Wk"][k * P:(k + 1) * P, :]).then_inc(ld_aw, 16)
                    sp.dma_start(wkv3[:, k, D:], a["L0_attn_Wv"][k * P:(k + 1) * P, :]).then_inc(ld_aw, 16)
                    sp.dma_start(wqc3[:, k, :], a["L0_attn_Wq_c"][k * P:(k + 1) * P, :]).then_inc(ld_aw, 16)
                col = lambda n: a[n].rearrange("(p o) -> p o", o=1)
                sp.dma_start(KW[:, 0:1], col("L0_attn_q_norm_w")).then_inc(ld_aw, 16)
                sp.dma_start(KW[:, 1:2], col("L0_attn_k_norm_w")).then_inc(ld_aw, 16)
                sp.dma_start(KWR[:, :], a["L0_attn_k_norm_w"].partition_broadcast(NB * B)).then_inc(ld_aw, 16)
                sp.dma_start(SINK[:, 0:H], a["L0_attn_sink"].partition_broadcast(P)).then_inc(ld_aw, 16)
                n_aw = 16 * (3 * KC + 4)
                sp.dma_start(wgs3, a["L0_attn_Wg"].rearrange("g (r p) i -> p (g r) i", p=P)).then_inc(ld_wg, 16)
                sp.dma_start(wos3, a["L0_attn_Wo"].rearrange("(c p) n -> p c n", p=P)).then_inc(ld_wg, 16)
                sp.dma_start(WQ[:, :], a["L0_attn_Wq_up"]).then_inc(ld_ct, 16)
                for t, n in ((WINDOW, "window"), (BLOCKS, "blocks"), (ROPE0, "rope0"), (ROPE1, "rope1")):
                    sp.dma_start(t[:, :], a["table_" + n]).then_inc(ld_ct, 16)

                load_experts(sp, 0, ELATE, ld_ex)
                sp.wait_ge(ck_ps, 1)
                load_experts(sp, ELATE, EMID, ld_ex2)
                sp.wait_ge(qc_ps, 2)
                sp.wait_ge(v2_ps, 1)
                load_experts(sp, EEND, E0, ld_ex2)
                sp.wait_ge(ck_r, 1)
                for b in range(B):
                    rows = CKR[b * NB:(b + 1) * NB, 0:D]
                    sp.dma_start(v2a3[WIN:WIN + NB, b, :], rows).then_inc(ckd, 16)
                    sp.dma_start(ck03[0:NB, b, :], rows).then_inc(ckd, 16)
                sp.wait_ge(ckd, 16 * 2 * B)

            @block.gpsimd
            def _(pool):
                st = Steps(pool, pool1)
                nc.gpsimd.memset(ZERO[:, :], 0.0).then_inc(zero_set, 1)
                pool.wait_ge(zero_set, 1)
                nc.gpsimd.memset(MHALF[:, :], -0.5).then_inc(const_set, 1)
                pool.wait_ge(const_set, 1)
                nc.gpsimd.memset(ONESB[:, :], 1.0).then_inc(const_set, 1)
                pool.wait_ge(const_set, 2)
                nc.gpsimd.memset(TA[32:64, NSH * HF:2 * NSH * HF], 1.0).then_inc(const_set, 1)
                pool.wait_ge(const_set, 3)
                nc.gpsimd.memset(QCT[:, NT * P:], 0.0).then_inc(const_set, 1)
                pool.wait_ge(const_set, 4)
                layernorm_pool(pool, 1, range(NT))

                def scatter(t0, t1):
                    for t in range(t0, t1):
                        for k in range(K0):
                            nc.gpsimd.indirect_dma_start(
                                xs0, bass.IndirectOffsetOnAxis(ap=SLOT[:, t * K0 + k:t * K0 + k + 1], axis=0),
                                xn3[:, t, :], None).then_inc(scat0, 16)
                pool.wait_ge(slots_ok, 1)
                pool.wait_ge(zero_done, 16 * (NT0Z // 4))
                scatter(0, NT - 2)
                pool.wait_ge(css, 1)
                nc.gpsimd.tensor_scalar(CM[0:NB * B, 1:2], CM[0:NB * B, 0:1], 1.0 / D, RMS_EPS, ALU.mult, ALU.add).then_inc(kvp, 1)
                pool.wait_ge(kvp, 1)
                nc.gpsimd.tensor_tensor(CM[0:NB * B, 2:3], CM[0:NB * B, 1:2], MHALF[0:NB * B, 0:1], ALU.pow).then_inc(crr, 1)
                pool.wait_ge(kss, 1)
                nc.gpsimd.tensor_scalar(RR[:, 0:NT], SSQ[:, 0:NT], 1.0 / D, RMS_EPS, ALU.mult, ALU.add).then_inc(kvp, 1)
                pool.wait_ge(kvp, 2)
                nc.gpsimd.tensor_tensor(RR[:, NT:2 * NT], RR[:, 0:NT], MHALF[:, 0:NT], ALU.pow).then_inc(krr, 1)
                scatter(NT - 2, NT)
                pool.wait_ge(qc_sb, 2)
                for g in (-1, 0):
                    attention_step(pool, attention_pool, g, (0, 0), only=-1)

            @block.scalar
            def _(act):
                for t in range(NT):
                    act.wait_ge(xt_ps, t + 1)
                    nc.scalar.activation(xnT3[:, :, t * P:(t + 1) * P], v3(ps[t % 2][:, 0:HID], KC), ACT.Copy).then_inc(xt_sb, 1)
                act.wait_ge(b1_ps, 1)
                nc.scalar.activation(B1A[:, :], ps[3][:, 0:E0 + NSH], ACT.Copy).then_inc(b1_sb, 1)
                nc.scalar.activation(B1B[:, :], ps[3][0:DHB, 64:64 + E0 + NSH], ACT.Copy).then_inc(b1_sb, 1)
                act.wait_ge(b1_sb, 2)
                act.wait_ge(const_set, 4)

                def shared_relu(i):
                    hf, s, c = i // 4, i // 2 % 2, i % 2
                    act.wait_ge(sh_ps, i + 1)
                    if hf and not s and not c:
                        act.wait_ge(so_ps, NT // 2)
                    if c == 0:
                        nc.scalar.activation(shA[:, s, :], ps[4 + i % 2][:, :], ACT.Relu,
                                             bias=B1A[:, E0 + s:E0 + s + 1]).then_inc(sh_sb, 1)
                    else:
                        nc.scalar.activation(shB[0:DHB, s, :], ps[4 + i % 2][0:DHB, :], ACT.Relu,
                                             bias=B1B[:, E0 + s:E0 + s + 1]).then_inc(sh_sb, 1)
                for i in range(4):
                    shared_relu(i)
                act.wait_ge(gates_sub, 1)
                nc.scalar.activation(GATE[:, :], GATE[:, :], ACT.Exp).then_inc(gates_exp, 1)
                for i in range(4, 8):
                    shared_relu(i)
                for n in range(2):
                    act.wait_ge(qc_ps, n + 1)
                    nc.scalar.activation(QCT[:, n * 512:(n + 1) * 512], ps[4 + n][0:QC, :], ACT.Copy).then_inc(qc_sb, 1)
                act.wait_ge(v2_ps, 1)
                nc.scalar.activation(V2A[0:WIN, :], ps[3][0:WIN, :], ACT.Copy).then_inc(v2_sb, 1)
                act.wait_ge(slots_ok, 2)

                def take_folded(h):
                    act.wait_ge(wf_ps, h + 1)
                    nc.scalar.activation(wc3[:, h, :], ps[6 + h % 2][:, 0:HID], ACT.Copy).then_inc(wf_sb, 1)
                for h in range(H):
                    act.wait_ge(wt_ps, h + 1)
                    nc.scalar.activation(wgT[h % 2], ps[4 + h % 2][:, 0:HID], ACT.Copy).then_inc(wt_sb, 1)
                    if h >= 1:
                        take_folded(h - 1)
                take_folded(H - 1)
                attention_step(act, attention_act, -1, (0, 0), only=-1)
                act.wait_ge(scat0, 16 * NT * K0)
                attention_step(act, attention_act, 0, (0, 0), only=-1)

            @block.vector
            def _(dve):
                st = Steps(dve, dve1)
                dve.wait_ge(ld_c, n_c)
                nc.vector.tensor_copy(BEFOREB[:, :], BEFORE[:, :]).then_inc(dve1, 1)
                st.n += 1
                dve.wait_ge(ld_x, 16)
                layernorm_dve(dve, st, 1, range(NT))
                dve.wait_ge(lg_ps, 1)
                dve.wait_ge(ld_rt, 32)
                st.link(nc.vector.tensor_tensor(v3(LOGIT[:, :], NT), v3(ps[2][:, 0:NT * E0], NT),
                                                bc(RB[:, :].unsqueeze(1), [P, NT, E0]), ALU.add))
                route_dve(dve, st, E0, K0)
                route_dve_slots(dve, st, E0, K0, ps[3], 0)

                def shared_add(t):
                    dve.wait_ge(so_ps, t + 1)
                    nc.vector.scalar_tensor_tensor(out=x3[:, t, :], in0=ps[SHARED_BANKS[t % 4]][:, 0:HID], scalar=1.0 / NSH,
                                                   in1=x3[:, t, :], op0=ALU.mult, op1=ALU.add).then_inc(so_sb, 1)
                for t in range(NT // 2):
                    shared_add(t)
                route_dve_experts(dve, st, E0, NT0, 0)
                for t in range(NT // 2, NT):
                    shared_add(t)
                dve.wait_ge(ck_ps, 1)
                dve.wait_ge(ld_aw, n_aw)
                ckn = CKR[:, 0:D]
                st.link(nc.vector.tensor_copy(CKR[:, D:], ps[2][0:NB * B, 0:D]))
                nc.vector.scalar_tensor_tensor(out=ckn, in0=CKR[:, D:], scalar=1.0, in1=CKR[:, D:], op0=ALU.mult,
                                               op1=ALU.mult, accum_out=CM[0:NB * B, 0:1]).then_inc(css, 1)
                dve.wait_ge(css, 1)
                for t in range(NT):
                    dve.wait_ge(kv_ps, t + 1)
                    st(nc.vector.tensor_copy(kraw3[:, t, :], ps[6 + t % 2][:, 0:D]))
                    nc.vector.tensor_copy(va3[:, t, :], ps[6 + t % 2][:, D:2 * D]).then_inc(kv_sb, 1)
                st.wait()
                sq = KTMP[:, 0:D]
                for t in range(NT):
                    ins = nc.vector.scalar_tensor_tensor(out=v3(KTMP, NT)[:, t, :], in0=kraw3[:, t, :], scalar=1.0, in1=kraw3[:, t, :],
                                                         op0=ALU.mult, op1=ALU.mult, accum_out=SSQ[:, t:t + 1])
                    if t < NT - 1:
                        st(ins)
                ins.then_inc(kss, 1)
                st.wait()
                dve.wait_ge(kss, 1)
                dve.wait_ge(ld_ct, 16 * 5)
                k4 = KRAW.rearrange("p (b j d) -> p b j d", b=B, j=TPB)
                k1, k2 = k4[:, :, :, 0:HR], k4[:, :, :, HR:ROPE]
                tmp = [KTMP[:, i * NT * HR:(i + 1) * NT * HR].rearrange("p (b j d) -> p b j d", b=B, j=TPB) for i in range(4)]
                cs = [bc(v3(ROPE0[:, i * TPB * HR:(i + 1) * TPB * HR], TPB).unsqueeze(1), [P, B, TPB, HR]) for i in range(2)]
                for dst, src, c in ((0, k1, 0), (1, k2, 1), (2, k1, 1), (3, k2, 0)):
                    for b in range(B):
                        st(nc.vector.tensor_tensor(tmp[dst][:, b], src[:, b], cs[c][:, b], ALU.mult))
                st.wait()
                st(nc.vector.tensor_tensor(k1, tmp[0], tmp[1], ALU.subtract))
                st(nc.vector.tensor_tensor(k2, tmp[2], tmp[3], ALU.add))
                st.link(nc.vector.tensor_tensor(KW[:, 2:3], KW[:, 0:1], KW[:, 1:2], ALU.mult))
                dve.wait_ge(crr, 1)
                nc.vector.scalar_tensor_tensor(out=ckn, in0=CKR[:, D:], scalar=CM[0:NB * B, 2:3], in1=KWR[:, :],
                                               op0=ALU.mult, op1=ALU.mult).then_inc(ck_r, 1)
                dve.wait_ge(krr, 1)
                nc.vector.tensor_tensor(kraw3, kraw3, bc(RR[:, NT:2 * NT].unsqueeze(2), [P, NT, D]), ALU.mult).then_inc(kn_r, 1)
                for half in range(2):
                    dve.wait_ge(kt_ps, half + 1)
                    b4 = ps[half][:, :].rearrange("p (b j t) -> p b j t", b=2, j=TPB)
                    dst = kc3[:, 2 * half:2 * half + 2, :]
                    w = KW[:, 2:3]
                    nc.vector.tensor_scalar(dst[:, :, 0:P], b4[:, :, 0, :], w, None, ALU.mult).then_inc(kt_sb, 1)
                    nc.vector.tensor_scalar(dst[:, :, P + NB:2 * P + NB], b4[:, :, 1, :], w, None, ALU.mult).then_inc(kt_sb, 1)
                    nc.vector.tensor_scalar(dst[:, :, 2 * P + NB:2 * P + NB + WIN], b4[:, :, 0, P - WIN:], w, None, ALU.mult).then_inc(kt_sb, 1)
                dve.wait_ge(kt_ps, 3)
                c3 = v3(ps[2][:, 0:B * NB], B)
                nc.vector.tensor_scalar(kc3[:, :, P:P + NB], c3, KW[:, 0:1], None, ALU.mult).then_inc(kt_sb, 1)
                nc.vector.tensor_scalar(kc3[:, :, KROW - NB:], c3, KW[:, 0:1], None, ALU.mult).then_inc(kt_sb, 1)
                m0 = SINK[:, H:2 * H]
                st.link(nc.vector.tensor_scalar(m0, SINK[:, 0:H], 0.0, None, ALU.max))
                st(nc.vector.tensor_tensor(SINK[:, 2 * H:3 * H], SINK[:, 0:H], m0, ALU.subtract))
                st.link(nc.vector.tensor_scalar(m0, m0, -1.0, None, ALU.mult))

            @block.tensor
            def _(pe):
                pe.wait_ge(ld_c, n_c)
                for t in range(NT):
                    pe.wait_ge(xn_ok, t + 1)
                    if t >= 2:
                        pe.wait_ge(xt_sb, t - 1)
                    for k in range(KC):
                        ins = nc.tensor.transpose(ps[t % 2][:, k * P:(k + 1) * P], xn3[:, t, k * P:(k + 1) * P], IDN[:, :])
                    ins.then_inc(xt_ps, 1)
                pe.wait_ge(ld_rt, 32)
                pe.wait_ge(xt_sb, NT)
                for t in range(NT):
                    for k in range(KC):
                        ins = nc.tensor.matmul(ps[2][:, t * E0:(t + 1) * E0], xnT3[:, k, t * P:(t + 1) * P],
                                               v3(RTW[:, :], KC)[:, k, :], start=(k == 0), stop=(k == KC - 1))
                ins.then_inc(lg_ps, 1)
                pe.wait_ge(ld_sh, n_sh)
                nb = E0 + NSH
                nc.tensor.transpose(ps[3][:, 0:nb], B1[:, 0:P], IDN[0:nb, 0:nb])
                nc.tensor.transpose(ps[3][0:DHB, 64:64 + nb], B1[:, P:DH], IDN[0:nb, 0:nb]).then_inc(b1_ps, 1)

                def shared_up(hf):
                    for s in range(NSH):
                        for c in range(2):
                            i = 4 * hf + 2 * s + c
                            if i >= 2:
                                pe.wait_ge(sh_sb, i - 1)
                            n = P if c == 0 else DHB
                            for k in range(KC):
                                ins = nc.tensor.matmul(ps[4 + i % 2][0:n, :], sw1[:, s, k, c * P:c * P + n],
                                                       xnT3[:, k, hf * HF:(hf + 1) * HF], start=(k == 0), stop=(k == KC - 1))
                            ins.then_inc(sh_ps, 1)

                def shared_down(hf):
                    pe.wait_ge(sh_sb, 4 * hf + 4)
                    for i in range(NT // 2):
                        t = hf * NT // 2 + i
                        if t >= 4:
                            pe.wait_ge(so_sb, t - 3)
                        bank = ps[SHARED_BANKS[t % 4]]
                        for s in range(NSH):
                            nc.tensor.matmul(bank[:, 0:HID], shA[:, s, i * P:(i + 1) * P], sw2[:, s, 0],
                                             start=(s == 0), stop=False)
                            ins = nc.tensor.matmul(bank[:, 0:HID], shB[0:DHB + 1, s, i * P:(i + 1) * P],
                                                   sw2[0:DHB + 1, s, 1], start=False, stop=(s == NSH - 1))
                        ins.then_inc(so_ps, 1)
                shared_up(0)
                pe.wait_ge(b1_sb, 2)
                rank_pe(pe, E0, ps[3], 0)
                shared_down(0)
                shared_up(1)
                shared_down(1)
                pe.wait_ge(ld_cp, 16)
                pe.wait_ge(chosen, 1)
                for c in range(M * KC):
                    m, k = c // KC, c % KC
                    ins = nc.tensor.matmul(ps[2][0:NB * B, 0:D], xnT3[:, k, m:T:M], wcp3[:, c, :],
                                           start=(c == 0), stop=(c == M * KC - 1))
                ins.then_inc(ck_ps, 1)
                pe.wait_ge(ld_aw, n_aw)
                pe.wait_ge(sh_sb, 8)
                for n in range(2):
                    for k in range(KC):
                        ins = nc.tensor.matmul(ps[4 + n][0:QC, :], wqc3[:, k, :], xnT3[:, k, n * 512:(n + 1) * 512],
                                               start=(k == 0), stop=(k == KC - 1))
                    ins.then_inc(qc_ps, 1)
                pe.wait_ge(so_sb, NT)
                for t in range(NT):
                    if t >= 2:
                        pe.wait_ge(kv_sb, t - 1)
                    for k in range(KC):
                        ins = nc.tensor.matmul(ps[6 + t % 2][:, 0:2 * D], xnT3[:, k, t * P:(t + 1) * P], wkv3[:, k, :],
                                               start=(k == 0), stop=(k == KC - 1))
                    ins.then_inc(kv_ps, 1)
                pe.wait_ge(slots_ok, 1)
                for b in range(B):
                    for k in range(KC):
                        lo = b * S + P - WIN
                        ins = nc.tensor.matmul(ps[3][0:WIN, b * D:(b + 1) * D], xnT3[:, k, lo:lo + WIN], wkv3[:, k, D:],
                                               start=(k == 0), stop=(k == KC - 1))
                ins.then_inc(v2_ps, 1)
                pe.wait_ge(ld_wg, 32)
                pe.wait_ge(qc_sb, 2)
                pe.wait_ge(kv_sb, NT)

                def fold(h):
                    pe.wait_ge(wt_sb, h + 1)
                    if h >= 2:
                        pe.wait_ge(wf_sb, h - 1)
                    for k in range(KC):
                        ins = nc.tensor.matmul(ps[6 + h % 2][:, 0:HID], wgT[h % 2][:, k * P:(k + 1) * P],
                                               wos3[:, h // 4 * KC + k, :], start=(k == 0), stop=(k == KC - 1))
                    ins.then_inc(wf_ps, 1)
                for h in range(H):
                    if h >= 2:
                        pe.wait_ge(wt_sb, h - 1)
                    for k in range(KC):
                        ins = nc.tensor.transpose(ps[4 + h % 2][:, k * P:(k + 1) * P], wgs3[:, h, k * P:(k + 1) * P], IDN[:, :])
                    ins.then_inc(wt_ps, 1)
                    if h >= 1:
                        fold(h - 1)
                fold(H - 1)
                pe.wait_ge(kn_r, 1)
                pe.wait_ge(so_sb, NT)
                pe.wait_ge(v2_sb, 1)
                for half in range(2):
                    for i in range(NT // 2):
                        ins = nc.tensor.transpose(ps[half][:, i * P:(i + 1) * P], kraw3[:, half * NT // 2 + i, :], IDN[:, :])
                    ins.then_inc(kt_ps, 1)
                pe.wait_ge(ck_r, 1)
                nc.tensor.transpose(ps[2][:, 0:B * NB], CKR[:, 0:D], IDN[0:B * NB, 0:B * NB]).then_inc(kt_ps, 1)
                pe.wait_ge(ld_ct, 16 * 5)
                pe.wait_ge(wf_sb, H)
                attention_step(pe, attention_pe, -1, (0, 0), only=-1)
                pe.wait_ge(kt_sb, 8)
                attention_step(pe, attention_pe, 0, (0, 0), only=-1)

        tile_sems = ([sem(f"tile_loaded{i}") for i in range(4)], [sem(f"tile_stored{i}") for i in range(2)],
                     [sem("tile_" + n) for n in ("xT_psum", "xT_sbuf", "h_psum", "h_sbuf", "hT_psum", "hT_sbuf",
                                                 "y_psum", "y_sbuf", "silu")])

        def in_ring(tiles, length, r):
            return (tiles + length - 1 - r) // length * 16

        def expert_parts(before, ntile, xs, ys, loads, scattered, n_scattered, stages):
            ld, stq, (xT_ps, xT_sb, h_ps, h_sb, hT_ps, hT_sb, y_ps, y_sb, mid) = tile_sems

            def await_tiles(eng, s, n):
                eng.wait_ge(s, n + before)

            def await_dma(eng, ring, r, n):
                eng.wait_ge(ring[r], n + in_ring(before, len(ring), r))
            SK = 3
            BODY = stages["body"]
            late = stages.get("late")
            G0 = 5
            xt = [TA[:, i * HID:(i + 1) * HID] for i in range(4)]
            xT = [TA[:, (4 + i) * HID:(5 + i) * HID] for i in range(2)]
            hs = [TA[:, (6 + i) * HID:(7 + i) * HID] for i in range(2)]
            hT = [TA[:, (8 + i) * HID:(9 + i) * HID] for i in range(2)]
            yt = [TA[:, (10 + i) * HID:(11 + i) * HID] for i in range(2)]

            def experts(engine, g, n):
                return nc.values_load_multi_w_load_instructions(
                    TEX[0:1, bass.ds(g, n)], [engine], min_val=0, max_val=stages["E"] - 1,
                    skip_runtime_bounds_check_because="a count of the experts that start at a tile or before, less one")[1]

            def run(eng, step, engine=None, lags=(), ahead_of=None, mark_last=False):
                def outside(g):
                    on = lambda lag: 0 <= g - lag < ntile
                    here = [g - lag for lag in lags if on(lag)]
                    e = {}
                    if here:
                        first, last = min(here), max(here)
                        e = dict(zip(range(first, last + 1), experts(engine, first, last + 1 - first)))
                    step(g, g % 4, lambda n, lag: (g - lag) // n, on, lambda lag: e.get(g - lag))
                for g in range(G0):
                    if ahead_of:
                        ahead_of(g)
                    outside(g)
                if ahead_of:
                    ahead_of(G0)
                n = (ntile - G0) // BODY
                with eng.Fori(0, n) as i:
                    for c0 in range(G0, G0 + BODY, 4):
                        e = {}
                        if lags:
                            first, many = c0 - max(lags), 4 + max(lags) - min(lags)
                            e = dict(zip(range(first, first + many), experts(engine, i * BODY + first, many)))
                        for c in range(c0, c0 + 4):
                            marks = {"last": True} if mark_last and c == G0 + BODY - 1 else {}
                            step(i * BODY + c, c % 4, lambda n, lag: i * (BODY // n) + (c - lag) // n, lambda lag: True,
                                 lambda lag: e.get(c - lag), **marks)
                for g in range(G0 + BODY * n, ntile + SK):
                    if ahead_of:
                        ahead_of(g)
                    outside(g)

            def early(g, n):
                return isinstance(g, int) and g < n

            def sync(sp, ahead_of_loop=None):
                sp.wait_ge(scattered, n_scattered)

                def step(g, q, rounds, on, expert):
                    if on(0):
                        if not early(g, 4):
                            await_tiles(sp, xT_ps, g - 3)
                        sp.dma_start(xt[q], xs[bass.ds(g * P, P), :]).then_inc(ld[q], 16)
                        if early(g, G0) and g == G0 - 1 and ahead_of_loop:
                            ahead_of_loop()
                run(sp, step)

            def tensor(pe):
                for s, n in loads:
                    pe.wait_ge(s, n)

                def step(g, q, rounds, on, expert, last=False):
                    if last and late:
                        pe.wait_ge(*late)
                    if on(0):
                        await_dma(pe, ld, q, rounds(4, 0) * 16 + 16)
                        for k in range(KC):
                            ins = nc.tensor.transpose(ps[q % 2][:, k * P:(k + 1) * P], xt[q][:, k * P:(k + 1) * P], IDN[:, :])
                        ins.then_inc(xT_ps, 1)
                    if on(1):
                        await_tiles(pe, xT_sb, g)
                        stages["up"](expert(1), ps[2 + (q + 1) % 2], xT[(q + 1) % 2]).then_inc(h_ps, 1)
                    if on(2):
                        await_tiles(pe, h_sb, g - 1)
                        stages["turn"](ps[4 + q % 2], hs[q % 2]).then_inc(hT_ps, 1)
                    if on(3):
                        await_tiles(pe, hT_sb, g - 2)
                        if not early(g, 5):
                            await_tiles(pe, y_sb, g - 4)
                        stages["down"](expert(3), ps[6 + (q + 1) % 2], hT[(q + 1) % 2]).then_inc(y_ps, 1)
                run(pe, step, mybir.EngineType.PE, (1, 3), mark_last=True)

            def scalar(act, ahead_of=None):
                def step(g, q, rounds, on, expert):
                    if on(0):
                        await_tiles(act, xT_ps, g + 1)
                        if not early(g, 2):
                            await_tiles(act, h_ps, g - 1)
                        nc.scalar.activation(xT[q % 2], ps[q % 2][:, 0:HID], ACT.Copy).then_inc(xT_sb, 1)
                    if stages["act_mid"] and on(1):
                        await_tiles(act, h_ps, g)
                        if not early(g, 3):
                            await_tiles(act, hT_ps, g - 2)
                        stages["act_mid"](ps[2 + (q + 1) % 2], hs[(q + 1) % 2]).then_inc(mid, 1)
                    if on(2):
                        await_tiles(act, hT_ps, g - 1)
                        if not early(g, 4):
                            await_tiles(act, y_ps, g - 3)
                        stages["act_turn"](expert(2), ps[4 + q % 2], hT[q % 2], hT_sb)
                    if on(3):
                        if not stages["dve_mid"]:
                            await_tiles(act, y_ps, g - 2)
                            if not early(g, 5):
                                await_dma(act, stq, (q + 1) % 2, rounds(2, 3) * 16)
                            nc.scalar.activation(yt[(q + 1) % 2], ps[6 + (q + 1) % 2][:, 0:HID], ACT.Copy).then_inc(y_sb, 1)
                        await_tiles(act, y_sb, g - 2)
                        act.dma_start(ys[bass.ds((g - 3) * P, P), :], yt[(q + 1) % 2]).then_inc(stq[(q + 1) % 2], 16)
                run(act, step, mybir.EngineType.Activation, (2,) if stages["bias"] else (), ahead_of)

            def vector(dve, ahead_of=None):
                def step(g, q, rounds, on, expert):
                    if on(1):
                        await_tiles(dve, h_ps, g)
                        if not early(g, 3):
                            await_tiles(dve, hT_ps, g - 2)
                        stages["dve_mid"](ps[2 + (q + 1) % 2], hs[(q + 1) % 2]).then_inc(h_sb, 1)
                    if on(3):
                        await_tiles(dve, y_ps, g - 2)
                        if not early(g, 5):
                            await_dma(dve, stq, (q + 1) % 2, rounds(2, 3) * 16)
                        nc.vector.tensor_copy(yt[(q + 1) % 2], ps[6 + (q + 1) % 2][:, 0:HID]).then_inc(y_sb, 1)
                run(dve, step, ahead_of=ahead_of)
            return sync, tensor, scalar, vector

        def up0(e, bank, xt):
            w = rw3[:, bass.ds(e, 1), :]
            for k in range(KC):
                ins = nc.tensor.matmul(bank[:, 0:DH], xt[:, k * P:(k + 1) * P], w[:, 0, k * DH:(k + 1) * DH],
                                       start=(k == 0), stop=(k == KC - 1))
            return ins

        def turn0(bank, h):
            nc.tensor.transpose(bank[:, 0:P], h[:, 0:P], IDN[:, :])
            return nc.tensor.transpose(bank[0:DHB, P:2 * P], h[:, P:DH], IDN[:, :])

        def act_turn0(e, bank, hT, done):
            nc.scalar.activation(hT[:, 0:P], bank[:, 0:P], ACT.Relu, bias=B1A[:, bass.ds(e, 1)])
            nc.scalar.activation(hT[0:DHB, P:2 * P], bank[0:DHB, P:2 * P], ACT.Relu, bias=B1B[:, bass.ds(e, 1)]).then_inc(done, 1)

        def down0(e, bank, hT):
            w = rw3[:, bass.ds(e, 1), :]
            nc.tensor.matmul(bank[:, 0:HID], hT[:, 0:P], w[:, 0, W2A:W2B], start=True, stop=False)
            return nc.tensor.matmul(bank[:, 0:HID], hT[0:DHB + 1, P:2 * P], w[0:DHB + 1, 0, W2B:EW0], start=False, stop=True)

        ones_set = sem("ones_set")
        assert 5 + 12 - 2 < ELATE
        parts0 = expert_parts(0, NT0, xs0, ys0, [(ld_ex, 16 * 5)], scat0, 16 * NT * K0,
                     dict(E=E0, late=(ld_ex2, 16 * 15), up=up0, turn=turn0, down=down0, act_mid=None, bias=True, body=12, act_turn=act_turn0,
                          dve_mid=lambda bank, h: nc.vector.tensor_copy(h[:, 0:DH], bank[:, 0:DH])))
        with nc.Block() as block:
            @block.sync
            def _(sp):
                def last_experts():
                    sp.wait_ge(wf_ps, H)
                    load_experts(sp, EMID, EEND, ld_ex2)
                parts0[0](sp, last_experts)

            @block.gpsimd
            def _(pool):
                for i in range(2):
                    nc.gpsimd.memset(TA[32:64, (8 + i) * HID + P:(9 + i) * HID], 1.0).then_inc(ones_set, 1)
                    pool.wait_ge(ones_set, i + 1)
                for g in (0, 1):
                    query_rotate(pool, g, g)

            @block.tensor
            def _(pe):
                parts0[1](pe)

            @block.scalar
            def _(act):
                act.wait_ge(ones_set, 2)
                parts0[2](act)

            @block.vector
            def _(dve):
                for g in (0, 1):
                    query_squares(dve, dve_steps(dve, 0), g, g)

                def norms(g):
                    if g in (NT0 - 2, NT0 - 1):
                        query_norm(dve, (NT0 - 2, NT0 - 1).index(g), (NT0 - 2, NT0 - 1).index(g))
                parts0[3](dve, norms)

        def turn_tokens(pe, t):
            pe.wait_ge(xn_ok, NT + t + 1)
            wait(pe, x1t_sb, t - 1)
            for k in range(KC):
                ins = nc.tensor.transpose(ps[t % 2][:, k * P:(k + 1) * P], xn3[:, t, k * P:(k + 1) * P], IDN[:, :])
            ins.then_inc(x1t_ps, 1)

        def logits(pe, t):
            pe.wait_ge(x1t_sb, t + 1)
            for k in range(KC):
                ins = nc.tensor.matmul(ps[2][:, t * E1:(t + 1) * E1], xnT3[:, k, t * P:(t + 1) * P],
                                       RTW[:, k * E1:(k + 1) * E1], start=(k == 0), stop=(k == KC - 1))
            return ins

        def take_tokens(act, t):
            act.wait_ge(x1t_ps, t + 1)
            nc.scalar.activation(xnT3[:, :, t * P:(t + 1) * P], v3(ps[t % 2][:, 0:HID], KC), ACT.Copy).then_inc(x1t_sb, 1)

        with nc.Block() as block:
            @block.sync
            def _(sp):
                for e in range(E1):
                    w = rw13[:, e, :]
                    for k in range(KC):
                        for m, n in enumerate(("L1_ffn_wi_0", "L1_ffn_wi_1")):
                            sp.dma_start(w[:, (2 * k + m) * MI:(2 * k + m + 1) * MI], a[n][e, k * P:(k + 1) * P, :]).then_inc(ld_e1, 16)
                        sp.dma_start(w[:, 2 * KC * MI + k * HID:2 * KC * MI + (k + 1) * HID],
                                     a["L1_ffn_wo"][e, k * P:(k + 1) * P, :]).then_inc(ld_e1, 16)
                for i, (n, r) in enumerate((("Wq", 0), ("Wq", P), ("Wk", 0), ("Wv", 0), ("Wo", 0), ("Wo", P))):
                    sp.dma_start(WR1[:, i * HID:(i + 1) * HID], a["L1_attn_" + n][r:r + P, :]).then_inc(ld_w1, 16)
                for i in range(NT1Z // 4):
                    sp.dma_start(xs1[i * 4 * P:(i + 1) * 4 * P, :].rearrange("(c p) d -> p c d", p=P),
                                  bc(ZERO[:, :].unsqueeze(1), [P, 4, HID])).then_inc(zero1, 16)
                sp.dma_start(v3(RTW[:, 0:KC * E1], KC), a["L1_ffn_gate_kernel"].rearrange("(k p) e -> p k e", p=P)).then_inc(ld_s1, 16)
                for n, lo, w in (("bq", 0, HID), ("bk", HID, P), ("bv", HID + P, P)):
                    sp.dma_start(BQKV[:, lo:lo + w], a["L1_attn_" + n].partition_broadcast(P)).then_inc(ld_s1, 16)
                sp.dma_start(BO, a["L1_attn_bo"].partition_broadcast(P)).then_inc(ld_s1, 16)
                sp.wait_ge(rb_zero, 1)
                for h in range(HKV):
                    sp.dma_start(RBT[h * R1:(h + 1) * R1, h * D1:(h + 1) * D1], a["L1_attn_rand_matrix"]).then_inc(ld_r1, 16)
                sp.wait_ge(zero1, 16 * (NT1Z // 4))

            @block.gpsimd
            def _(pool):
                nc.gpsimd.memset(RBT, 0.0).then_inc(rb_zero, 1)
                for r in range(2):
                    pool.wait_ge(tile_sems[1][r], in_ring(NT0, 2, r))
                run_attention(pool, attention_pool)
                layernorm_pool(pool, 2, MOST)

            @block.tensor
            def _(pe):
                run_attention(pe, attention_pe)
                pe.wait_ge(ld_s1, 16 * 5)
                for t in MOST:
                    turn_tokens(pe, t)
                    if t:
                        logits(pe, t - 1)
                logits(pe, MOST[-1])

            @block.scalar
            def _(act):
                nc.scalar.activation(SINK[:, 3 * H:], SINK[:, 2 * H:3 * H], ACT.Exp).then_inc(es_ok, 1)

                run_attention(act, attention_act)
                for t in MOST:
                    take_tokens(act, t)

            @block.vector
            def _(dve):
                dve.wait_ge(es_ok, 1)
                for r in range(2):
                    dve.wait_ge(tile_sems[1][r], in_ring(NT0, 2, r))

                def norm_most():
                    dve.wait_ge(q_ev, (NT + 1) * NG)
                    dve.wait_ge(comb, NT - 1)
                    layernorm_dve(dve, dve_steps(dve, 2), 2, MOST)
                run_attention(dve, attention_dve, norm_most)

        o1 = base
        NHK = H1 + HKV
        HF1 = NHK * D1
        QKV = cut1(NT * 2 * HID)
        WT1 = cut1(KC * 2 * HID)
        WOT = cut1(KC * HID)
        TURN = cut1(NT * HF1)
        VOUT = cut1(NT * HID)
        FEAT = cut1(NT * HF1)
        ANG = cut1(NT * NHK * R1)
        assert ANG.shape == WR1.shape and o1 <= E0 * EW0
        SSN, RNORM = SW1[:, 0:NT * NHK], SW1[:, NT * NHK:2 * NT * NHK]
        MEET = [SW1[:, 2 * NT * NHK + i * P:2 * NT * NHK + (i + 1) * P] for i in range(2)]
        DT = [KCAT[:, i * 3 * P:(i + 1) * 3 * P] for i in range(2)]
        OT = [VA[:, i * HID:(i + 1) * HID] for i in range(2)]
        RNT = VA[:, 2 * HID:2 * HID + NT * NHK]
        NPR = H1 * HKV * D1
        PRF = [xnT[:, 0:NPR], TURN[:, 0:NPR]]
        PRD = WC[:, NPR:2 * NPR]
        VIN = WC[:, 0:NT * HID]
        hst, hld = sem("b_heads_stored"), [sem(f"b_heads_loaded{b}") for b in range(B)]
        fgat = [sem(f"f_gathered{b}") for b in range(B)]
        f_ok, f_st = sem("f_combined"), sem("f_stored")
        qkv3 = v3(QKV, NT)

        (dve3, dve3l, dve3e, lg1_ps, wt1_ps, wt1_sb, qkv_ps, qkv_sb,
         scat1, d_ok, sq_ok, ssum, root, dT_ps, dT_sb, u_ps, u_sb, u_ok, sin_ok,
         prf_ok, prf_rd, o_ok, bo_ok, oT_ps, oT_sb, ao_ps, ao_rd) = (
            sem("b_" + n) for n in (
                "dve", "dve_loop", "dve_tail", "logits",
                "wT_psum", "wT_sbuf", "qkv_psum", "qkv_sbuf", "scatter",
                "rotated", "squares", "square_sums", "roots", "dT_psum", "dT_sbuf", "angles_psum", "angles_sbuf", "turns",
                "features", "products", "products_read", "outs", "bias_added", "oT_psum", "oT_sbuf", "proj", "proj_read"))

        def up1(e, bank, xt):
            w = rw13[:, bass.ds(e, 1), :]
            for k in range(KC):
                ins = nc.tensor.matmul(bank[:, :], xt[:, k * P:(k + 1) * P], w[:, 0, k * 2 * MI:(k + 1) * 2 * MI],
                                       start=(k == 0), stop=(k == KC - 1))
            return ins

        def turn1(bank, h):
            for k in range(KC):
                ins = nc.tensor.transpose(bank[:, k * P:(k + 1) * P], h[:, k * P:(k + 1) * P], IDN[:, :])
            return ins

        def act_turn1(e, bank, hT, done):
            nc.scalar.activation(hT, bank[:, 0:MI], ACT.Copy).then_inc(done, 1)

        def down1(e, bank, hT):
            w = rw13[:, bass.ds(e, 1), :]
            for k in range(KC):
                ins = nc.tensor.matmul(bank[:, 0:HID], hT[:, k * P:(k + 1) * P],
                                       w[:, 0, 2 * KC * MI + k * HID:2 * KC * MI + (k + 1) * HID], start=(k == 0), stop=(k == KC - 1))
            return ins

        parts1 = expert_parts(NT0, NT1, xs1, ys1, [(ld_e1, 16 * 3 * KC * E1)], scat1, 16 * NT * K1,
                              dict(E=E1, up=up1, turn=turn1, down=down1, bias=False, body=8, act_turn=act_turn1, dve_mid=None,
                                   act_mid=lambda bank, h: nc.scalar.activation(h, bank[:, 0:MI], ACT.Silu)))

        with nc.Block() as block:
            @block.sync
            def _(sp):
                parts1[0](sp)
                for b in range(B):
                    for j in range(TPB):
                        t = b * TPB + j
                        sp.wait_ge(o_ok, t + 1)
                        sp.dma_start(heads1[t * P:(t + 1) * P, :], VOUT[:, t * HID:(t + 1) * HID]).then_inc(hst, 16)
                    sp.wait_ge(hst, 16 * TPB * (b + 1))
                    for j in range(TPB):
                        t = b * TPB + j
                        hh = H1 // TPB
                        src = heads1[b * S:(b + 1) * S, j * hh * D1:(j + 1) * hh * D1].rearrange("(g l) (h d) -> h g l d", l=H1, d=D1)
                        sp.dma_start(VIN[:, t * HID:(t + 1) * HID].rearrange("p (l d) -> p l d", l=H1), src).then_inc(hld[b], 16)
                rows = out.rearrange("b (j p) d -> (b j) p d", p=P)
                for t in range(NT):
                    sp.wait_ge(f_ok, t + 1)
                    sp.dma_start(rows[t], x3[:, t, :]).then_inc(f_st, 16)
                sp.wait_ge(f_st, 16 * NT)

            @block.gpsimd
            def _(pool):
                layernorm_pool(pool, 3, LAST)
                pool.wait_ge(slots_ok, 3)
                for t in range(NT):
                    for k in range(K1):
                        nc.gpsimd.indirect_dma_start(
                            xs1, bass.IndirectOffsetOnAxis(ap=SLOT[:, t * K1 + k:t * K1 + k + 1], axis=0),
                            xn3[:, t, :], None).then_inc(scat1, 16)
                ft = FEAT.rearrange("p (t n f) -> p t n f", t=NT, n=NHK)
                for t in range(NT):
                    pool.wait_ge(sin_ok, 1 if t == 0 else NT // 2)
                    wait(pool, prf_rd, t - 1)
                    nc.gpsimd.tensor_tensor(PRF[t % 2].rearrange("p (h k f) -> p h k f", h=H1, k=HKV),
                                            bc(ft[:, t, 0:H1].unsqueeze(2), [P, H1, HKV, D1]),
                                            bc(ft[:, t, H1:].unsqueeze(1), [P, H1, HKV, D1]), ALU.mult).then_inc(prf_ok, 1)
                pool.wait_ge(ld_s1, 16 * 5)
                for t in range(NT):
                    nc.gpsimd.tensor_tensor(x3[:, t, :], x3[:, t, :], BO, ALU.add).then_inc(bo_ok, 1)
                for r in range(2):
                    pool.wait_ge(tile_sems[1][r], in_ring(NT0, 2, r) + in_ring(NT1, 2, r))
                pool.wait_ge(prf_rd, NT)
                for t in range(NT):
                    for k in range(K1):
                        i = t * K1 + k
                        nc.gpsimd.indirect_dma_start(XN[:, i * HID:(i + 1) * HID], None, ys1,
                                                     bass.IndirectOffsetOnAxis(ap=SLOT[:, i:i + 1], axis=0)).then_inc(fgat[t // TPB], 16)

            @block.scalar
            def _(act):
                for t in LAST:
                    take_tokens(act, t)
                act.wait_ge(wt1_ps, 1)
                for k in range(KC):
                    nc.scalar.activation(WT1[:, k * 2 * HID:(k + 1) * 2 * HID], ps[6 + k][:, :], ACT.Copy).then_inc(wt1_sb, 1)
                nc.scalar.activation(WOT, ps[4][:, :], ACT.Copy).then_inc(wt1_sb, 1)
                nc.scalar.activation(RBD, ps[5][:, 0:HKV * R1], ACT.Copy).then_inc(wt1_sb, 1)
                act.wait_ge(gates_sub, 2)
                nc.scalar.activation(GATE[:, 0:NT * K1], GATE[:, 0:NT * K1], ACT.Exp).then_inc(gates_exp, 1)

                def angles_out(i):
                    act.wait_ge(u_ps, 2 * i + 2)
                    n = 2 * NHK * R1
                    nc.scalar.activation(ANG[:, i * n:(i + 1) * n], ps[2 + i][:, 0:n], ACT.Copy).then_inc(u_sb, 1)
                for t in range(NT):
                    act.wait_ge(d_ok, t + 1)
                    nc.scalar.activation(TURN[:, t * HF1:(t + 1) * HF1], qkv3[:, t, 0:HF1], ACT.Square).then_inc(sq_ok, 1)
                    act.wait_ge(dT_ps, t + 1)
                    wait(act, u_ps, t - 1)
                    nc.scalar.activation(DT[t % 2], ps[t % 2][:, 0:3 * P], ACT.Copy).then_inc(dT_sb, 1)
                    if t >= 2 and t % 2 == 0:
                        angles_out(t // 2 - 1)
                angles_out(NT // 2 - 1)

                def features(g):
                    if g == 1:
                        act.wait_ge(ssum, 1)
                        nc.scalar.activation(RNORM, SSN, ACT.Sqrt).then_inc(root, 1)
                    for i in {3: (0, 1), 4: (2,), 5: (3,)}.get(g, ()):
                        act.wait_ge(u_ok, i + 1)
                        f = FEAT[:, i * 2 * HF1:(i + 1) * 2 * HF1]
                        nc.scalar.activation(f, f, ACT.Sin, scale=2 * 3.1415925).then_inc(sin_ok, 1)
                parts1[2](act, features)
                for t in range(NT):
                    act.wait_ge(oT_ps, t + 1)
                    wait(act, ao_ps, t - 1)
                    nc.scalar.activation(OT[t % 2], ps[4 + t % 2][:, 0:HID], ACT.Copy).then_inc(oT_sb, 1)

            @block.vector
            def _(dve):
                st = Steps(dve, dve3)
                dve.wait_ge(comb, NT)
                layernorm_dve(dve, st, 3, LAST)
                dve.wait_ge(lg1_ps, 1)
                st.link(nc.vector.tensor_copy(LOGIT[:, 0:NT * E1], ps[2][:, 0:NT * E1]))
                route_dve(dve, st, E1, K1)
                route_dve_slots(dve, st, E1, K1, ps[3], 1)
                route_dve_experts(dve, st, E1, NT1, 1)
                dve.wait_ge(ld_s1, 16 * 5)
                hd = D1 // 2
                cos, sin = (v3(ROPE1[:, i * TPB * hd:(i + 1) * TPB * hd], TPB) for i in range(2))
                nt4 = NHK * hd

                def take_qkv(t):
                    dve.wait_ge(qkv_ps, t + 1)
                    nc.vector.tensor_tensor(qkv3[:, t, :], ps[4 + t % 4][:, :], BQKV, ALU.add).then_inc(qkv_sb, 1)

                def rotate(t):
                    dve.wait_ge(qkv_sb, t + 1)
                    q = v3(qkv3[:, t, 0:HF1], NHK)
                    y1, y2 = q[:, :, 0:hd], q[:, :, hd:]
                    tmp = [v3(FEAT[:, i * nt4:(i + 1) * nt4], NHK) for i in range(4 * (t % 4), 4 * (t % 4) + 4)]
                    c, s = (bc(w[:, t % TPB, :].unsqueeze(1), [P, NHK, hd]) for w in (cos, sin))
                    for i, (y, w) in enumerate(((y1, c), (y2, s), (y1, s), (y2, c))):
                        st(nc.vector.tensor_tensor(tmp[i], y, w, ALU.mult))
                    st.wait()
                    st(nc.vector.tensor_tensor(y1, tmp[0], tmp[1], ALU.subtract))
                    nc.vector.tensor_tensor(y2, tmp[3], tmp[2], ALU.add).then_inc(d_ok, 1)
                take_qkv(0)
                for t in range(NT):
                    if t + 1 < NT:
                        take_qkv(t + 1)
                    rotate(t)
                st.wait()
                for t0, t1 in ((0, NT - 2), (NT - 2, NT)):
                    dve.wait_ge(sq_ok, t1)
                    st(nc.vector.tensor_reduce(SSN[:, t0 * NHK:t1 * NHK],
                                               TURN[:, t0 * HF1:t1 * HF1].rearrange("p (n d) -> p n d", d=D1), AX, ALU.add))
                st.wait()
                nc.vector.tensor_scalar(SSN, SSN, 1e-12, None, ALU.max).then_inc(ssum, 1)
                dve.wait_ge(root, 1)
                st.link(nc.vector.reciprocal(RNORM, RNORM))
                st.link(nc.vector.tensor_tensor(RNT, RNORM, RNORM, ALU.mult))
                st.link(nc.vector.tensor_tensor(RNT, RNT, SSN, ALU.mult))
                st.link(nc.vector.tensor_scalar(RNT, RNT, -0.5 / (2 * np.pi), 1.5 / (2 * np.pi), ALU.mult, ALU.add))
                st.link(nc.vector.tensor_tensor(RNORM, RNORM, RNT, ALU.mult))
                def turns(i):
                    dve.wait_ge(u_sb, i + 1)
                    cols = slice(i * 2 * HF1, (i + 1) * 2 * HF1)
                    turn = v3(TURN[:, cols], 2 * NHK)
                    st.link(nc.vector.tensor_tensor(turn[:, :, 0:R1], v3(ANG, NT * NHK)[:, i * 2 * NHK:(i + 1) * 2 * NHK, :],
                                                    bc(RNORM[:, i * 2 * NHK:(i + 1) * 2 * NHK].unsqueeze(2), [P, 2 * NHK, R1]), ALU.mult))
                    st.link(nc.vector.tensor_scalar(turn[:, :, R1:], turn[:, :, 0:R1], 0.25, None, ALU.add))
                    st.link(nc.vector.tensor_scalar(FEAT[:, cols], TURN[:, cols], MAGIC, -MAGIC, ALU.add, ALU.add))
                    st.link(nc.vector.tensor_tensor(FEAT[:, cols], TURN[:, cols], FEAT[:, cols], ALU.subtract))
                    nc.vector.tensor_scalar(FEAT[:, cols], FEAT[:, cols], 0.5, -0.5, ALU.min, ALU.max).then_inc(u_ok, 1)

                _, _, _, h_sb1, hT_ps1, _, _, _, silu1 = tile_sems[2]
                hs = [TA[:, (6 + i) * HID:(7 + i) * HID] for i in range(2)]

                def middle(u, odd):
                    dve.wait_ge(silu1, u + 1)
                    dve.wait_ge(hT_ps1, u + (NT0 - 1))
                    nc.vector.tensor_tensor(hs[odd], ps[2 + odd][:, MI:2 * MI], hs[odd], ALU.mult).then_inc(h_sb1, 1)

                def meet(part, t, odd, chain):
                    w = MEET[odd].rearrange("p (h k) -> p h k", h=H1)
                    prd = PRD.rearrange("p (h d k) -> p h d k", h=H1, d=D1)
                    if part == 0:
                        dve.wait_ge(prf_ok, t + 1)
                        nc.vector.tensor_reduce(w, PRF[odd].rearrange("p (h k f) -> p h k f", h=H1, k=HKV), AX, ALU.add).then_inc(prf_rd, 1)
                        dve.wait_ge(prf_rd, t + 1)
                        chain.link(nc.vector.tensor_scalar(w, w, float(H1 // HKV) / D1, None, ALU.mult))
                    elif part == 1:
                        vals = QKV[:, bass.ds(t * (2 * HID) + HID + P, P)].rearrange("p (k d) -> p d k", k=HKV)
                        chain.link(nc.vector.tensor_tensor(prd, bc(w.unsqueeze(2), [P, H1, D1, HKV]),
                                                           bc(vals.unsqueeze(1), [P, H1, D1, HKV]), ALU.mult))
                    else:
                        nc.vector.tensor_reduce(VOUT[:, bass.ds(t * HID, HID)].rearrange("p (h d) -> p h d", h=H1), prd, AX, ALU.add).then_inc(o_ok, 1)

                turns(0)
                middle(0, 0)
                turns(1)
                middle(1, 1)
                turns(2)
                middle(2, 0)
                middle(3, 1)
                turns(3)
                UA = 4
                PER_TILE = 2
                n = (NT1 - UA) // 6
                with dve.Fori(0, n) as i:
                    chain = Steps(dve, dve3l, i * (2 * PER_TILE))
                    for c in range(6):
                        middle(i * 6 + (c + UA), c % 2)
                        meet(c % 3, i * 2 + c // 3, c // 3, chain)
                    assert chain.n == 2 * PER_TILE
                ste = Steps(dve, dve3e)
                u = UA + 6 * n
                for c in range(3 * (NT - 2 * n)):
                    if u + c < NT1:
                        middle(u + c, c % 2)
                    meet(c % 3, 2 * n + c // 3, c // 3 % 2, ste)
                assert u + 3 * (NT - 2 * n) >= NT1

                dve.wait_ge(bo_ok, NT)
                for t in range(NT):
                    dve.wait_ge(ao_ps, t + 1)
                    nc.vector.tensor_tensor(x3[:, t, :], ps[6 + t % 2][:, 0:HID], x3[:, t, :], ALU.add).then_inc(ao_rd, 1)
                    dve.wait_ge(ao_rd, t + 1)
                    dve.wait_ge(fgat[t // TPB], 16 * TPB * K1)
                    for k in range(K1):
                        i = t * K1 + k
                        ins = nc.vector.scalar_tensor_tensor(out=x3[:, t, :], in0=XN[:, i * HID:(i + 1) * HID], scalar=GATE[:, i:i + 1],
                                                             in1=x3[:, t, :], op0=ALU.mult, op1=ALU.add)
                        if k < K1 - 1:
                            ste.link(ins)
                    ins.then_inc(f_ok, 1)

            @block.tensor
            def _(pe):
                for t in LAST:
                    turn_tokens(pe, t)
                    logits(pe, t).then_inc(lg1_ps, 1)
                pe.wait_ge(ld_w1, 16 * 6)
                for k in range(KC):
                    for i in range(4):
                        nc.tensor.transpose(ps[6 + k][:, i * P:(i + 1) * P], WR1[:, i * HID + k * P:i * HID + (k + 1) * P], IDN[:, :])
                for k in range(KC):
                    for i in range(2):
                        nc.tensor.transpose(ps[4][:, (2 * k + i) * P:(2 * k + i + 1) * P],
                                            WR1[:, (4 + i) * HID + k * P:(4 + i) * HID + (k + 1) * P], IDN[:, :])
                pe.wait_ge(ld_r1, 16 * HKV)
                nc.tensor.transpose(ps[5][:, 0:HKV * R1], RBT, IDN[0:HKV * R1, 0:HKV * R1]).then_inc(wt1_ps, 1)

                def qkv(t):
                    wait(pe, qkv_sb, t - 3)
                    for k in range(KC):
                        ins = nc.tensor.matmul(ps[4 + t % 4][:, :], xnT3[:, k, t * P:(t + 1) * P],
                                               WT1[:, k * 2 * HID:(k + 1) * 2 * HID], start=(k == 0), stop=(k == KC - 1))
                    ins.then_inc(qkv_ps, 1)
                rank_pe(pe, E1, ps[3], 1)
                pe.wait_ge(wt1_sb, 4)
                for t in range(NT):
                    qkv(t)
                pe.wait_ge(slots_ok, 4)

                def angles(t):
                    pe.wait_ge(dT_sb, t + 1)
                    if t == 4:
                        pe.wait_ge(qkv_sb, NT)
                    for c in range(3):
                        lo = t % 2 * NHK * R1 + c * HKV * R1
                        ins = nc.tensor.matmul(ps[2 + t // 2][:, lo:lo + HKV * R1], DT[t % 2][:, c * P:(c + 1) * P], RBD,
                                               start=True, stop=True)
                    ins.then_inc(u_ps, 1)
                for t in range(NT):
                    pe.wait_ge(d_ok, t + 1)
                    wait(pe, dT_sb, t - 1)
                    for c in range(3):
                        ins = nc.tensor.transpose(ps[t % 2][:, c * P:(c + 1) * P], qkv3[:, t, c * P:(c + 1) * P], IDN[:, :])
                    ins.then_inc(dT_ps, 1)
                    if t:
                        angles(t - 1)
                angles(NT - 1)
                pe.wait_ge(u_sb, NT // 2)

                parts1[1](pe)
                pe.wait_ge(tile_sems[2][5], NT0 + NT1)
                pe.wait_ge(tile_sems[2][7], NT0 + NT1)

                def project1(t):
                    pe.wait_ge(oT_sb, t + 1)
                    wait(pe, ao_rd, t - 1)
                    for k in range(KC):
                        ins = nc.tensor.matmul(ps[6 + t % 2][:, 0:HID], OT[t % 2][:, k * P:(k + 1) * P], WOT[:, k * HID:(k + 1) * HID],
                                               start=(k == 0), stop=(k == KC - 1))
                    ins.then_inc(ao_ps, 1)
                for t in range(NT):
                    pe.wait_ge(hld[t // TPB], 16 * TPB)
                    wait(pe, oT_sb, t - 1)
                    for k in range(KC):
                        ins = nc.tensor.transpose(ps[4 + t % 2][:, k * P:(k + 1) * P], VIN[:, t * HID + k * P:t * HID + (k + 1) * P], IDN[:, :])
                    ins.then_inc(oT_ps, 1)
                    if t:
                        project1(t - 1)
                project1(NT - 1)


INPUTS = ["L0_attn_h", "L0_attn_Wq_c", "L0_attn_Wq_up", "L0_attn_Wk", "L0_attn_Wv", "L0_attn_W_comp", "L0_attn_q_norm_w",
          "L0_attn_k_norm_w", "L0_attn_sink", "L0_attn_Wg", "L0_attn_Wo", "L0_ffn_sw1", "L0_ffn_sb1", "L0_ffn_sw2", "L0_ffn_sb2",
          "L0_ffn_rw1", "L0_ffn_rb1", "L0_ffn_rw2", "L0_ffn_rb2", "L0_ffn_router_w", "L0_ffn_router_b", "L1_attn_Wq", "L1_attn_bq",
          "L1_attn_Wk", "L1_attn_bk", "L1_attn_Wv", "L1_attn_bv", "L1_attn_Wo", "L1_attn_bo", "L1_attn_rand_matrix",
          "L1_ffn_gate_kernel", "L1_ffn_wi_0", "L1_ffn_wi_1", "L1_ffn_wo"]


def kernel(**inputs):
    import concourse.bacc as bacc
    from concourse.bass_utils import run_bass_kernel_spmd

    nc = bacc.Bacc("TRN2", target_bir_lowering=False, num_devices=1)
    arrays = {n: np.ascontiguousarray(inputs[n]) for n in INPUTS}
    arrays.update(constants())
    args = {n: nc.dram_tensor(n, v.shape, mybir.dt.from_np(v.dtype), kind="ExternalInput").ap() for n, v in arrays.items()}
    out = nc.dram_tensor("out", (B, S, HID), F32, kind="ExternalOutput").ap()
    build(nc, args, out)
    r = run_bass_kernel_spmd(nc, [arrays], core_ids=[0])
    return r.results[0]["out"]
```
